# Optimizing a Trainium2 kernel written in Bass

```python
import numpy as np
import jax
import jax.numpy as jnp

def _softmax(x, axis=-1):
    return jax.nn.softmax(x, axis=axis)

def _gelu(x):
    return jax.nn.gelu(x, approximate=True)

def _silu(x):
    return jax.nn.silu(x)

def _sigmoid(x):
    return jax.nn.sigmoid(x)

def _layernorm(x, axis=-1, eps=1e-05):
    m = jnp.mean(x, axis=axis, keepdims=True)
    v = jnp.var(x, axis=axis, keepdims=True)
    return (x - m) / jnp.sqrt(v + eps)

def _scatter_add(tgt, idx, src, axis=0):
    return tgt.at[idx].add(src)

def _segment_sum(src, seg, n):
    return jax.ops.segment_sum(src, seg, n)
kernel_name = 'mk_flamingo_gated_d1_seqx_r4_ec1fc5'

def setup_inputs(seed: int=0):
    np.random.seed(seed)
    _w = jnp.asarray

    def _rec_inputs():
        import jax
        import jax.numpy as jnp
        _rk = jax.random.key(seed)
        x = 7.22e-05 + 1 * jax.random.normal(jax.random.fold_in(_rk, 1), (32, 256, 256), jnp.float32)
        _lenS = 256 - jax.random.randint(jax.random.fold_in(_rk, 7), (32,), 0, max(1, 256 // 4) + 1, jnp.int32)
        _lenS2 = 77 - jax.random.randint(jax.random.fold_in(_rk, 8), (32,), 0, max(1, 77 // 4) + 1, jnp.int32)
        _ctx_1024P = jax.random.normal(jax.random.fold_in(_rk, 11), (32, 16, 256), jnp.float32)
        _ctx_1024c = jax.random.dirichlet(jax.random.fold_in(_rk, 511), 0.3 * jnp.ones((16,), jnp.float32), (32, 77))
        _ctx_1024t = jnp.einsum('bsk,bkd->bsd', _ctx_1024c, _ctx_1024P)
        _ctx_1024t = _ctx_1024t * jax.lax.rsqrt(jnp.mean(jnp.square(_ctx_1024t)) + 1e-12) * 0.953939
        ctx_1024 = 4.13588e-05 + 0.999923 * (_ctx_1024t + 0.3 * jax.random.normal(jax.random.fold_in(_rk, 611), (32, 77, 256), jnp.float32))
        _g = jax.random.normal(jax.random.fold_in(_rk, 9001), (2, 1), jnp.float32)
        _g = jnp.sign(_g) * jnp.maximum(jnp.abs(_g), 1.0) + (_g == 0) * 1.0
        g_xattn = _g[0]
        g_ffn = _g[1]
        return (x, ctx_1024, g_xattn, g_ffn)
    x, ctx_1024, g_xattn, g_ffn = _rec_inputs()

    def _L0_xattn_setup():
        import jax, jax.numpy as jnp
        import numpy as np
        H, D, DIM = (8, 128, 256)
        QB, N = (16, 128)

        def layer_norm(x, g, b, eps=1e-05):
            mu = x.mean(-1, keepdims=True)
            var = ((x - mu) ** 2).mean(-1, keepdims=True)
            return (x - mu) / jnp.sqrt(var + eps) * g + b
        key = jax.random.key(seed)
        ks = jax.random.split(key, 8)
        rn = lambda k, shape, s=1.0: jax.random.normal(k, shape, jnp.float32) * s
        return {'q': rn(ks[0], (QB, N, DIM)), 'k': rn(ks[1], (QB, N, DIM)), 'v': rn(ks[2], (QB, N, DIM)), 'ln_g': jnp.ones(DIM, jnp.float32), 'ln_b': jnp.zeros(DIM, jnp.float32), 'w_in': rn(ks[3], (H * D, DIM), 0.02), 'wp_w1': rn(ks[4], (D, 2 * D), 0.05), 'wp_b1': jnp.zeros(D, jnp.float32), 'wp_ln_g': jnp.ones(D, jnp.float32), 'wp_ln_b': jnp.zeros(D, jnp.float32), 'wp_w2': rn(ks[5], (3, D), 0.05), 'wp_b2': jnp.zeros(3, jnp.float32), 'w_out': rn(ks[6], (DIM, H * D), 0.02), 'b_out': jnp.zeros(DIM, jnp.float32)}
    _L0_xattn_all = _L0_xattn_setup()
    _L0_xattn_in = {k: v for k, v in _L0_xattn_all.items() if k in ('ln_g', 'ln_b', 'w_in', 'wp_w1', 'wp_b1', 'wp_ln_g', 'wp_ln_b', 'wp_w2', 'wp_b2', 'w_out', 'b_out')}
    del _L0_xattn_all

    def _L0_ffn_setup():
        import jax, jax.numpy as jnp
        import numpy as np
        from functools import partial
        HEADS = 16
        EPS = 1e-12

        def _l2_normalize(z):
            n = jnp.linalg.norm(z, axis=-1, keepdims=True)
            return z / jnp.maximum(n, EPS)
        key = jax.random.key(seed)
        kx, kq, kk, kv, ko, kf = jax.random.split(key, 6)
        B, S, D, L = (2, 512, 256, 256)
        scale = 0.02
        return {'x': jax.random.normal(kx, (B, S, D), dtype=jnp.float32), 'Wq': jax.random.normal(kq, (D, L), dtype=jnp.float32) * scale, 'Wk': jax.random.normal(kk, (D, L), dtype=jnp.float32) * scale, 'Wv': jax.random.normal(kv, (D, L), dtype=jnp.float32) * scale, 'Wo': jax.random.normal(ko, (L, D), dtype=jnp.float32) * scale, 'Wff': jax.random.normal(kf, (D, D), dtype=jnp.float32) * scale}
    _L0_ffn_all = _L0_ffn_setup()
    _L0_ffn_in = {k: v for k, v in _L0_ffn_all.items() if k in ('Wq', 'Wk', 'Wv', 'Wo', 'Wff')}
    del _L0_ffn_all
    return {'x': x, 'ctx_1024': ctx_1024, 'g_xattn': g_xattn, 'g_ffn': g_ffn, 'L0_xattn_ln_g': _L0_xattn_in['ln_g'], 'L0_xattn_ln_b': _L0_xattn_in['ln_b'], 'L0_xattn_w_in': _L0_xattn_in['w_in'], 'L0_xattn_wp_w1': _L0_xattn_in['wp_w1'], 'L0_xattn_wp_b1': _L0_xattn_in['wp_b1'], 'L0_xattn_wp_ln_g': _L0_xattn_in['wp_ln_g'], 'L0_xattn_wp_ln_b': _L0_xattn_in['wp_ln_b'], 'L0_xattn_wp_w2': _L0_xattn_in['wp_w2'], 'L0_xattn_wp_b2': _L0_xattn_in['wp_b2'], 'L0_xattn_w_out': _L0_xattn_in['w_out'], 'L0_xattn_b_out': _L0_xattn_in['b_out'], 'L0_ffn_Wq': _L0_ffn_in['Wq'], 'L0_ffn_Wk': _L0_ffn_in['Wk'], 'L0_ffn_Wv': _L0_ffn_in['Wv'], 'L0_ffn_Wo': _L0_ffn_in['Wo'], 'L0_ffn_Wff': _L0_ffn_in['Wff']}

def reference(x, ctx_1024, g_xattn, g_ffn, L0_xattn_ln_g, L0_xattn_ln_b, L0_xattn_w_in, L0_xattn_wp_w1, L0_xattn_wp_b1, L0_xattn_wp_ln_g, L0_xattn_wp_ln_b, L0_xattn_wp_w2, L0_xattn_wp_b2, L0_xattn_w_out, L0_xattn_b_out, L0_ffn_Wq, L0_ffn_Wk, L0_ffn_Wv, L0_ffn_Wo, L0_ffn_Wff):
    import jax
    import jax.numpy as jnp

    def _L0_xattn_ref(q, k, v, ln_g, ln_b, w_in, wp_w1, wp_b1, wp_ln_g, wp_ln_b, wp_w2, wp_b2, w_out, b_out):
        import jax, jax.numpy as jnp
        import numpy as np
        H, D, DIM = (8, 128, 256)
        QB, N = (16, 128)

        def layer_norm(x, g, b, eps=1e-05):
            mu = x.mean(-1, keepdims=True)
            var = ((x - mu) ** 2).mean(-1, keepdims=True)
            return (x - mu) / jnp.sqrt(var + eps) * g + b

        def proj(t):
            x = layer_norm(t, ln_g, ln_b) @ w_in.T
            Qd, Nd = (t.shape[0], t.shape[1])
            return x.reshape(Qd, Nd, H, D).transpose(2, 0, 1, 3)
        f_q, f_k, f_v = (proj(q), proj(k), proj(v))
        dots = jnp.einsum('hqnd,hqmd->hqnm', f_q, f_k)
        qn = jnp.linalg.norm(f_q, axis=-1)
        kn = jnp.linalg.norm(f_k, axis=-1)
        cosine_sim = dots / (qn[..., :, None] * kn[..., None, :])
        q_centered = f_q - f_q.mean(-1, keepdims=True)
        q_var = jnp.var(f_q, axis=-1, ddof=1)
        k_var = jnp.var(f_k, axis=-1, ddof=1)
        q_ratio = 2.0 * jnp.minimum(q_var, 1.0) / (q_var + 1.0)
        k_ratio = 2.0 * jnp.minimum(k_var, 1.0) / (k_var + 1.0)
        var_component = jnp.einsum('hqn,hqm->hqnm', q_ratio, k_ratio)
        q_flat = q_centered.reshape(H, -1, D)
        feat_corr = jnp.einsum('hnd,hne->hde', q_flat, q_flat) / q_flat.shape[1]
        feat_corr = feat_corr * (1.0 - jnp.eye(D, dtype=feat_corr.dtype))
        decorr_score = jnp.linalg.norm(feat_corr, axis=(-2, -1)) / (D * D)
        decorr_scale = jnp.exp(-5.0 * decorr_score)[:, None, None, None]
        cov_component = cosine_sim * decorr_scale
        q_global = f_q.mean(axis=(1, 2))
        k_global = f_k.mean(axis=(1, 2))
        feats = jnp.concatenate([q_global, k_global], axis=-1)
        h1 = jnp.maximum(layer_norm(feats @ wp_w1.T + wp_b1, wp_ln_g, wp_ln_b), 0.0)
        weights = jax.nn.softmax(h1 @ wp_w2.T + wp_b2, axis=-1)
        cw = weights[:, 0][:, None, None, None]
        vw = weights[:, 1][:, None, None, None]
        ww = weights[:, 2][:, None, None, None]
        mixed = cw * cosine_sim + vw * cov_component + ww * var_component
        out = jnp.einsum('hqnm,hqmd->hqnd', mixed, f_v)
        out = out.transpose(1, 2, 0, 3).reshape(q.shape[0], q.shape[1], H * D)
        return out @ w_out.T + b_out

    def _L0_ffn_ref(x, Wq, Wk, Wv, Wo, Wff):
        import jax, jax.numpy as jnp
        import numpy as np
        from functools import partial
        HEADS = 16
        EPS = 1e-12

        def _l2_normalize(z):
            n = jnp.linalg.norm(z, axis=-1, keepdims=True)
            return z / jnp.maximum(n, EPS)
        B, S, D = x.shape
        H = HEADS
        L = Wq.shape[1]
        dh = L // H

        def split_heads(t):
            return t.reshape(B, S, H, dh).transpose(0, 2, 1, 3).reshape(B * H, S, dh)
        q = split_heads(x @ Wq)
        k = split_heads(x @ Wk)
        v = split_heads(x @ Wv)
        scores = jnp.einsum('bqd,bkd->bkq', q, k) / jnp.sqrt(jnp.asarray(D, x.dtype))
        attn = jax.nn.softmax(scores, axis=-1)
        out = jnp.einsum('bkq,bkv->bqv', attn, v)
        z = out.reshape(B, H, S, dh).transpose(0, 2, 1, 3).reshape(B, S, L)
        z = z @ Wo
        z = _l2_normalize(z)
        z = z @ Wff
        z = _l2_normalize(z)
        z = jax.nn.gelu(z, approximate=False)
        return z
    x = x + jnp.tanh(g_xattn[0]) * _L0_xattn_ref(_layernorm(x, axis=-1), ctx_1024, ctx_1024, L0_xattn_ln_g, L0_xattn_ln_b, L0_xattn_w_in, L0_xattn_wp_w1, L0_xattn_wp_b1, L0_xattn_wp_ln_g, L0_xattn_wp_ln_b, L0_xattn_wp_w2, L0_xattn_wp_b2, L0_xattn_w_out, L0_xattn_b_out)
    x = x + jnp.tanh(g_ffn[0]) * _L0_ffn_ref(_layernorm(x, axis=-1), L0_ffn_Wq, L0_ffn_Wk, L0_ffn_Wv, L0_ffn_Wo, L0_ffn_Wff)
    return x

_drawn_inputs = setup_inputs


def setup_inputs(seed=0):
    import zlib

    import numpy as np

    out = dict(_drawn_inputs(seed))
    spreads = {'L0_xattn_ln_g': (1.0, 0.2),
     'L0_xattn_ln_b': (0.0, 0.1),
     'L0_xattn_wp_b1': (0.0, 0.1),
     'L0_xattn_wp_ln_g': (1.0, 0.6),
     'L0_xattn_wp_ln_b': (0.0, 0.483),
     'L0_xattn_wp_b2': (0.0, 2.0),
     'L0_xattn_b_out': (0.0, 0.1)}
    factors = {'L0_xattn_wp_w1': 2.948, 'L0_ffn_Wq': 8.0, 'L0_ffn_Wk': 21.474}
    for name, (base, spread) in spreads.items():
        noise = np.random.default_rng([zlib.crc32(name.encode()), seed]).standard_normal(out[name].shape)
        drawn = base * np.exp(spread * noise) if base else spread * noise
        out[name] = jnp.asarray(drawn.astype(out[name].dtype))
    for name, factor in factors.items():
        out[name] = (out[name] * factor).astype(out[name].dtype)
    return out
```

```python
import concourse.bass as bass
from concourse import mybir
from contextlib import ExitStack

F32 = mybir.dt.float32
F16 = mybir.dt.float16
ALU = mybir.AluOpType
ACT = mybir.ActivationFunctionType
AX = mybir.AxisListType

P = 128
NB, NQ, DIM = 32, 256, 256
MK = 77
H, DH = 8, 128
FH, FD = 16, 16
KT = DIM // P
HD = H * DH
ROWS = NB * NQ
NT = ROWS // P
NPAIR = NB // 2
PR = 2 * NQ
PT = PR // P
PM = 2 * MK
HM = H * MK
HT = -(-HM // P)
CROWS = NB * MK
CR = 112
CT = CROWS // CR
EPS = 1e-5
L2_EPS = 1e-12
PADW = 2 * 127 + MK

HEAD_PARTS = [(0, 3), (3, 6), (6, 8)]
HM_TILES = [(0, 1), (2, 3), (4,)]
HM_ROWS = [min(P, HM - P * t) for t in range(HT)]


def bc(ap, shape):
    return ap.to_broadcast(shape)


def build(nc, x, ctx_in, g_x, g_f, ln_g, ln_b, w_in, w_inT, w1T, b1, wln_g, wln_b, w2T, b2, w_outT, b_out,
          wq, wk, wv, wo, woT, wff, out):
    kstat = nc.dram_tensor("kstat", (2 * H, CROWS), F32, kind="Internal").ap()
    parts = nc.dram_tensor("parts", (4, DIM, PR), F16, kind="Internal").ap()
    x_rows = x.rearrange("b n d -> (b n) d")
    out_rows = out.rearrange("b n d -> (b n) d")
    c_rows = ctx_in.rearrange("b m d -> (b m) d")

    with ExitStack() as keep:
        def sb(name, shape, dt=F32, where=keep):
            return where.enter_context(nc.sbuf_tensor(name, shape, dt))

        w = {
            "wT": sb("wT", [P, KT, HD]), "wN": sb("wN", [P, H, DIM]), "woutT": sb("woutT", [P, H, DIM]),
            "wq": sb("wq", [P, KT, DIM]), "wk": sb("wk", [P, KT, DIM]), "wv": sb("wv", [P, KT, DIM]),
            "wof": sb("wof", [P, KT, 2 * DIM]), "ident": sb("ident", [P, P]),
            "gcol": sb("gcol", [P, KT]), "bcol": sb("bcol", [P, KT]), "tb": sb("tb", [P, DIM]),
            "tg": sb("tg", [P, 2]), "cvec": sb("cvec", [P, H]), "wwv": sb("wwv", [P, H]),
            "stats": sb("stats", [P, NT, 2]), "zcT": sb("zcT", [P, KT, CROWS]),
            "mhalf": sb("mhalf", [P, PT * H]), "phalf": sb("phalf", [P, H]),
        }
        with ExitStack() as first:
            setup_phase(nc, first, w, locals())
        with ExitStack() as second:
            main_phase(nc, second, w, x_rows, out_rows, kstat, parts)


def setup_phase(nc, ctx, w, a):
    x_rows, c_rows, kstat = a["x_rows"], a["c_rows"], a["kstat"]

    def sb(name, shape, dt=F32):
        return ctx.enter_context(nc.sbuf_tensor(name, shape, dt))

    def ps(name, shape):
        return ctx.enter_context(nc.psum_tensor(name, shape, F32))

    def sem(name):
        return ctx.enter_context(nc.semaphore(name))

    XT = 8
    NX = NT // (2 * XT)
    xin = sb("s_xin", [P, 2, XT, DIM])
    xa = sb("s_xa", [P, 2, XT, DIM + 4])
    xst = sb("s_xst", [P, 2, XT, 6])
    xmv = sb("s_xmv", [P, 2, XT, 2])
    xtmp, ctmp = sb("s_xtmp", [P, 2, XT, 2]), sb("s_ctmp", [CR, 2, 2])
    xrs = sb("s_xrs", [P, 2, XT])
    xvar = sb("s_xvar", [P, 2, XT])
    g_bc, b_bc = sb("s_gbc", [P, DIM]), sb("s_bbc", [P, DIM])
    cin = sb("s_cin", [CR, 2, DIM])
    cz = sb("s_cz", [CR, 2, DIM])
    cT = sb("s_cT", [P, KT, 2 * CR])
    cst, cmv = sb("s_cst", [CR, 2, 6]), sb("s_cmv", [CR, 2, 2])
    cvar, crs = sb("s_cvar", [CR, 2]), sb("s_crs", [CR, 2])
    fst = sb("s_fst", [CR, 2, H, 6])
    ft = sb("s_ft", [CR, 6, 2, H])
    kst = sb("s_kst", [CR, 2, 2, H])
    kstT = sb("s_kstT", [2 * H, 2, CR])
    zeros = sb("s_zeros", [1, DIM + 1])
    ones = sb("s_ones", [P, P])
    offdiag = sb("s_off", [P, P])
    gates = sb("s_gates", [P, 2])
    woT_sb, wff_sb = sb("s_woT", [P, KT, DIM]), sb("s_wff", [P, KT, DIM])
    w1T_sb, w2T_sb = sb("s_w1T", [P, 2, DH]), sb("s_w2T", [DH, 3])
    rows8 = sb("s_rows8", [H, 3, DH])
    b2row = sb("s_b2", [H, 3])
    gram = sb("s_gram", [P, KT, DIM + 1])
    csum = sb("s_csum", [P, KT])
    wmean = sb("s_wmean", [P, KT * H])
    wcT = sb("s_wcT", [P, KT, HD])
    hm = sb("s_hm", [P, KT, HD])
    fc = sb("s_fc", [P, H, DH])
    fcs = sb("s_fcs", [P, H])
    dec = sb("s_dec", [P, H])
    fe = sb("s_fe", [P, 2, H])
    h1, h1s, h1v = sb("s_h1", [H, DH]), sb("s_h1s", [H, 6]), sb("s_h1v", [H, 4])
    h1T = sb("s_h1T", [DH, H])
    lg = sb("s_lg", [H, 8])
    dgw = sb("s_dgw", [H, 3, H])
    mix = sb("s_mix", [P, 3, H])

    gram_ps = [ps(f"s_gram{k}", [P, 512]) for k in range(KT)]
    t_ps = ps("s_tps", [P, KT, 512])
    f_ps = ps("s_fps", [P, 4, 512])

    loaded = sem("s_loaded")
    x_loaded = [sem("s_xl0"), sem("s_xl1")]
    var_ready = [sem("s_vr0"), sem("s_vr1")]
    rstd_ready = [sem("s_rr0"), sem("s_rr1")]
    z_ready = [sem("s_zr0"), sem("s_zr1")]
    scaled = [sem("s_sc0"), sem("s_sc1")]
    xa_ready = [sem("s_xa0"), sem("s_xa1")]
    grammed = [sem("s_gm0"), sem("s_gm1")]
    c_loaded, c_var, c_rstd, cz_ready = sem("s_cl"), sem("s_cvr"), sem("s_crr"), sem("s_czr")
    ct_ps, ct_ready, zc_kept = sem("s_ctp"), sem("s_ctr"), sem("s_zck")
    f_ready, f_used, ksq_ready, rk_ready = sem("s_fr"), sem("s_fu"), sem("s_ksq"), sem("s_rk")
    kst_ready, kT_ps, kT_ready, kT_stored = sem("s_kstr"), sem("s_kTp"), sem("s_kTr"), sem("s_kTs")
    consts, step, turns = sem("s_consts"), sem("s_step"), sem("s_turns")
    pe_step, act_step, pool_step = sem("s_pe"), sem("s_act"), sem("s_pool")
    N_LOADS = 22
    NC2 = CT // 2

    with nc.Block() as block:
        @block.sync
        def _(sp):
            def sp_wait(ready, value):
                sp.wait_ge(ready, value)
                sp.sem_inc(turns, 1)

            def load(dst, src):
                sp.dma_start(dst, src).then_inc(loaded, 16)

            def load_x(half, i):
                sp.dma_start(xin[:, half, :, :], x_rows[bass.ds((i * 2 + half) * (XT * P), XT * P), :]
                             .rearrange("(t p) d -> p t d", p=P)).then_inc(x_loaded[half], 16)

            for waited in (grammed[0], grammed[1], kT_ready, kT_stored):
                sp.sem_inc(waited, START)
            with nc.allow_non_contiguous_dma(reason="columns of a few values"):
                for half in range(2):
                    load_x(half, 0)
                load(w["gcol"][:], a["ln_g"].rearrange("(k p) -> p k", p=P))
                load(w["bcol"][:], a["ln_b"].rearrange("(k p) -> p k", p=P))
                load(g_bc[:], a["ln_g"].partition_broadcast(P))
                load(b_bc[:], a["ln_b"].partition_broadcast(P))
                load(gates[:, 0:1], a["g_x"].partition_broadcast(P))
                load(gates[:, 1:2], a["g_f"].partition_broadcast(P))
                load(w["wT"][:], a["w_inT"].rearrange("(k p) c -> p k c", p=P))
                load(w["wN"][:], a["w_in"].rearrange("(h d) k -> d h k", d=DH))
                load(w["woutT"][:], a["w_outT"].rearrange("(h d) o -> d h o", d=DH))
                load(w["tb"][:], a["b_out"].partition_broadcast(P))
                for name in ("wq", "wk", "wv"):
                    load(w[name][:], a[name].rearrange("(k p) c -> p k c", p=P))
                load(w["wof"][:, :, 0:DIM], a["wo"].rearrange("(k p) c -> p k c", p=P))
                load(woT_sb[:], a["woT"].rearrange("(k p) c -> p k c", p=P))
                load(wff_sb[:], a["wff"].rearrange("(k p) c -> p k c", p=P))
                load(w1T_sb[:], a["w1T"].rearrange("(k p) c -> p k c", p=P))
                load(w2T_sb[:], a["w2T"])
                for j, name in enumerate(("b1", "wln_g", "wln_b")):
                    load(rows8[:, j, :], a[name].partition_broadcast(H))
                load(b2row[:], a["b2"].partition_broadcast(H))
                with sp.Fori(0, NX - 1) as i:
                    for half in range(2):
                        sp_wait(z_ready[half], i + 1)
                        load_x(half, i + 1)

                def load_c(i):
                    sp.dma_start(cin[:], c_rows[bass.ds(i * (2 * CR), 2 * CR), :]
                                 .rearrange("(t p) d -> p t d", p=CR)).then_inc(c_loaded, 16)

                def store_k(i):
                    sp_wait(kT_ready, i + 1 + START)
                    sp.dma_start(kstat[:, bass.ds(i * (2 * CR), 2 * CR)].rearrange("h (t p) -> h t p", p=CR),
                                 kstT[:]).then_inc(kT_stored, 16)

                load_c(0)
                with sp.Fori(0, NC2 - 1) as i:
                    sp_wait(cz_ready, i + 1)
                    load_c(i + 1)
                    store_k(i)
                store_k(NC2 - 1)
                sp.wait_ge(kT_stored, 16 * NC2 + START)

        @block.gpsimd
        def _(pool):
            nc.gpsimd.memset(w["ident"][:], 0.0).then_inc(pool_step, 1)
            nc.gpsimd.memset(offdiag[:], 1.0).then_inc(pool_step, 1)
            nc.gpsimd.memset(w["mhalf"][:], -0.5).then_inc(consts, 1)
            nc.gpsimd.memset(w["phalf"][:], 0.5).then_inc(consts, 1)
            nc.gpsimd.memset(ones[:], 1.0).then_inc(consts, 1)
            nc.gpsimd.memset(zeros[:], 0.0).then_inc(consts, 1)
            nc.gpsimd.memset(xa[:, :, :, DIM:DIM + 4], 1.0).then_inc(consts, 1)
            pool.wait_ge(pool_step, 2)
            nc.gpsimd.affine_select(out=w["ident"][:], in_=w["ident"][:], compare_op=ALU.not_equal, fill=1.0,
                                    base=0, pattern=[[-1, P]], channel_multiplier=1).then_inc(consts, 1)
            nc.gpsimd.affine_select(out=offdiag[:], in_=offdiag[:], compare_op=ALU.not_equal, fill=0.0,
                                    base=0, pattern=[[-1, P]], channel_multiplier=1).then_inc(consts, 1)
            pool.wait_ge(loaded, 16 * N_LOADS)
            pool.wait_ge(consts, 7)
            with pool.Fori(0, NX) as i:
                for half in range(2):
                    pool.wait_ge(var_ready[half], i + 1)
                    nc.gpsimd.tensor_tensor(xrs[:, half, :], xvar[:, half, :], w["mhalf"][:, 0:XT],
                                            ALU.pow).then_inc(rstd_ready[half], 1)
                for half in range(2):
                    pool.wait_ge(z_ready[half], i + 1)
                    nc.gpsimd.tensor_tensor(xa[:, half, :, 0:DIM], xa[:, half, :, 0:DIM],
                                            bc(g_bc[:].unsqueeze(1), [P, XT, DIM]),
                                            ALU.mult).then_inc(scaled[half], 1)
            with pool.Fori(0, NC2) as i:
                pool.wait_ge(c_var, i + 1)
                nc.gpsimd.tensor_tensor(crs[:], cvar[:], w["mhalf"][0:CR, 0:2], ALU.pow).then_inc(c_rstd, 1)
                pool.wait_ge(ksq_ready, i + 1)
                nc.gpsimd.tensor_tensor(kst[:, :, 0, :], ft[:, 0, :, :],
                                        w["mhalf"][0:CR, 0:2 * H].rearrange("p (t h) -> p t h", h=H),
                                        ALU.pow).then_inc(rk_ready, 1)
            pool.wait_ge(step, DVE_TAIL["fcs"])
            nc.gpsimd.tensor_tensor(dec[:], dec[:], w["phalf"][:], ALU.pow).then_inc(pool_step, 1)
            pool.wait_ge(step, DVE_TAIL["h1var"])
            nc.gpsimd.tensor_tensor(h1v[:, 2:3], h1v[:, 1:2], w["mhalf"][0:H, 0:1], ALU.pow).then_inc(pool_step, 1)

        @block.vector
        def _(dve):
            done = [0]

            def link(ins):
                done[0] += 1
                ins.then_inc(step, 1)
                dve.wait_ge(step, done[0])

            base = [0]

            def in_loop(i, per, k, ins):
                ins.then_inc(step, 1)
                dve.wait_ge(step, base[0] + i * per + k)

            X_STEPS = 10
            dve.wait_ge(consts, 7)
            dve.wait_ge(loaded, 16 * N_LOADS)
            with dve.Fori(0, NX) as i:
                for half in range(2):
                    dve.wait_ge(x_loaded[half], i * 16 + 16)
                    for t in range(XT):
                        last = nc.vector.bn_stats(xst[:, half, t, :], xin[:, half, t, :])
                    def x_link(k, ins):
                        in_loop(i, X_STEPS, 5 * half + k, ins)

                    x_link(1, last)
                    row_moments(nc, x_link, 2, xst[:, half], xmv[:, half], xtmp[:, half])
                    nc.vector.tensor_scalar(xvar[:, half, :], xtmp[:, half, :, 1], (1.0 + EPS) / DIM, EPS * EPS,
                                            ALU.mult, ALU.add).then_inc(var_ready[half], 1)
                    x_link(5,
                            nc.vector.tensor_copy(w["stats"][:, bass.ds((i * 2 + half) * XT, XT), 0],
                                                  xmv[:, half, :, 0]))
                for half in range(2):
                    dve.wait_ge(rstd_ready[half], i + 1)
                    dve.wait_ge(grammed[half], i + START)
                    nc.vector.tensor_copy(w["stats"][:, bass.ds((i * 2 + half) * XT, XT), 1], xrs[:, half, :])
                    for t in range(XT):
                        last = nc.vector.tensor_scalar(xa[:, half, t, 0:DIM], xin[:, half, t, :],
                                                       xmv[:, half, t, 0:1], xrs[:, half, t:t + 1],
                                                       ALU.subtract, ALU.mult)
                    last.then_inc(z_ready[half], 1)
                for half in range(2):
                    dve.wait_ge(scaled[half], i + 1)
                    nc.vector.tensor_tensor(xa[:, half, :, 0:DIM], xa[:, half, :, 0:DIM],
                                            bc(b_bc[:].unsqueeze(1), [P, XT, DIM]), ALU.add).then_inc(xa_ready[half], 1)
            base[0] = NX * X_STEPS
            C_STEPS = 14
            with dve.Fori(0, NC2) as i:
                def c_link(k, ins):
                    in_loop(i, C_STEPS, k, ins)

                dve.wait_ge(c_loaded, i * 16 + 16)
                for t in range(2):
                    last = nc.vector.bn_stats(cst[:, t, :], cin[:, t, :])
                c_link(1, last)
                row_moments(nc, c_link, 2, cst[:], cmv, ctmp)
                nc.vector.tensor_scalar(cvar[:], ctmp[:, :, 1], 1.0 / DIM, EPS, ALU.mult, ALU.add).then_inc(c_var, 1)
                dve.wait_ge(c_rstd, i + 1)
                for t in range(2):
                    last = nc.vector.tensor_scalar(cz[:, t, :], cin[:, t, :], cmv[:, t, 0:1], crs[:, t:t + 1],
                                                   ALU.subtract, ALU.mult)
                last.then_inc(cz_ready, 1)
                dve.wait_ge(f_ready, i + 1)
                for t in range(2):
                    for h in range(H):
                        last = nc.vector.bn_stats(fst[:, t, h, :],
                                                  f_ps[0:CR, 2 * t + h // 4, (h % 4) * DH:(h % 4 + 1) * DH])
                c_link(5, last)
                moments(nc, c_link, 6, fst[:], ft)
                dve.sem_inc(ksq_ready, 1)
                c_link(11, ratio_num(nc, ft))
                c_link(12, ratio_den(nc, ft))
                c_link(13, nc.vector.reciprocal(ft[:, 3, :, :], ft[:, 3, :, :]))
                dve.wait_ge(rk_ready, i + 1)
                c_link(14, nc.vector.tensor_tensor(kst[:, :, 1, :], ft[:, 2, :, :], ft[:, 3, :, :], ALU.mult))
                dve.sem_inc(kst_ready, 1)
            done[0] = NX * X_STEPS + NC2 * C_STEPS
            assert done[0] == DVE_LOOPS
            dve.wait_ge(zc_kept, NC2)
            link(nc.vector.tensor_reduce(csum[:], w["zcT"][:], AX.X, ALU.add))
            dve.wait_ge(pe_step, 1)
            for k in range(KT):
                nc.vector.tensor_copy(gram[:, k, :], gram_ps[k][:, 0:DIM + 1])
            link(nc.vector.tensor_reduce(wmean[:], w["wT"][:].rearrange("p k (h d) -> p (k h) d", d=DH), AX.X, ALU.add))
            link(nc.vector.tensor_scalar(wmean[:], wmean[:], -1.0 / DH, None, ALU.mult))
            link(nc.vector.tensor_tensor(wcT[:].rearrange("p k (h d) -> p (k h) d", d=DH),
                                         w["wT"][:].rearrange("p k (h d) -> p (k h) d", d=DH),
                                         bc(wmean[:].unsqueeze(2), [P, KT * H, DH]), ALU.add))
            assert done[0] == DVE_TAIL["wcT"]
            dve.wait_ge(pe_step, 2)
            link(nc.vector.tensor_copy(hm[:].rearrange("p k (c n) -> p (k c) n", n=512), f_ps[:]))
            assert done[0] == DVE_TAIL["hm"]
            dve.wait_ge(pe_step, 3)
            link(nc.vector.tensor_tensor(fc[:].rearrange("p (a h) d -> p a h d", a=2),
                                         f_ps[:, 0:2, :].rearrange("p a (h d) -> p a h d", d=DH),
                                         bc(offdiag[:].unsqueeze(1).unsqueeze(1), [P, 2, 4, DH]), ALU.mult))
            link(nc.vector.tensor_tensor(fc[:], fc[:], fc[:], ALU.mult))
            link(nc.vector.tensor_reduce(fcs[:], fc[:], AX.X, ALU.add))
            assert done[0] == DVE_TAIL["fcsum"]
            nc.vector.tensor_scalar(fe[:, 0, :], t_ps[:, 0, 0:H], 1.0 / ROWS, None, ALU.mult)
            link(nc.vector.tensor_scalar(fe[:, 1, :], t_ps[:, 0, H:2 * H], 1.0 / CROWS, None, ALU.mult))
            assert done[0] == DVE_TAIL["fe"]
            dve.wait_ge(pe_step, 4)
            link(nc.vector.tensor_copy(dec[:], t_ps[:, 1, 0:H]))
            assert done[0] == DVE_TAIL["fcs"]
            dve.wait_ge(pe_step, 5)
            link(nc.vector.tensor_tensor(h1[:], t_ps[0:H, 0, 0:DH], rows8[:, 0, :], ALU.add))
            link(nc.vector.bn_stats(h1s[:], h1[:]))
            link(nc.vector.bn_aggr(h1v[:, 0:2], h1s[:]))
            link(nc.vector.tensor_scalar(h1v[:, 1:2], h1v[:, 1:2], EPS, None, ALU.add))
            assert done[0] == DVE_TAIL["h1var"]
            dve.wait_ge(pool_step, 4)
            link(nc.vector.tensor_scalar(h1[:], h1[:], h1v[:, 0:1], h1v[:, 2:3], ALU.subtract, ALU.mult))
            link(nc.vector.tensor_tensor(h1[:], h1[:], rows8[:, 1, :], ALU.mult))
            link(nc.vector.tensor_tensor(h1[:], h1[:], rows8[:, 2, :], ALU.add))
            link(nc.vector.tensor_scalar(h1[:], h1[:], 0.0, None, ALU.max))
            assert done[0] == DVE_TAIL["h1"]
            dve.wait_ge(pe_step, 6)
            link(nc.vector.tensor_copy(h1T[:], t_ps[:, 1, 0:H]))
            assert done[0] == DVE_TAIL["h1T"]
            dve.wait_ge(pe_step, 7)
            link(nc.vector.tensor_tensor(lg[:, 0:3], t_ps[0:H, 0, 0:3], b2row[:], ALU.add))
            link(nc.vector.tensor_reduce(lg[:, 3:4], lg[:, 0:3], AX.X, ALU.max, negate=True))
            assert done[0] == DVE_TAIL["lmax"]
            dve.wait_ge(act_step, 3)
            link(nc.vector.reciprocal(lg[:, 4:5], lg[:, 4:5]))
            link(nc.vector.tensor_scalar(lg[:, 5:8], lg[:, 5:8], lg[:, 4:5], None, ALU.mult))
            for j in range(3):
                last = nc.vector.tensor_scalar(dgw[:, j, :], w["ident"][0:H, 0:H], lg[:, 5 + j:6 + j], None, ALU.mult)
            link(last)
            assert done[0] == DVE_TAIL["dgw"]
            dve.wait_ge(pe_step, 8)
            link(nc.vector.tensor_copy(mix[:].rearrange("p a h -> p (a h)"), t_ps[:, 1, 0:3 * H]))
            dve.wait_ge(act_step, 2)
            link(nc.vector.tensor_tensor(dec[:], dec[:], mix[:, 1, :], ALU.mult))
            nc.vector.tensor_tensor(w["cvec"][:], dec[:], mix[:, 0, :], ALU.add)
            nc.vector.tensor_copy(w["wwv"][:], mix[:, 2, :])
            dve.wait_ge(act_step, 1)
            nc.vector.tensor_scalar(w["woutT"][:], w["woutT"][:], w["tg"][:, 0:1], None, ALU.mult)
            nc.vector.tensor_scalar(w["tb"][:], w["tb"][:], w["tg"][:, 0:1], None, ALU.mult)
            dve.wait_ge(pe_step, 9)
            for k in range(KT):
                last = nc.vector.tensor_copy(w["wof"][:, k, DIM:2 * DIM], f_ps[:, k, 0:DIM])
            link(last)

        @block.scalar
        def _(act):
            act.wait_ge(loaded, 16 * N_LOADS)
            nc.scalar.activation(w["tg"][:], gates[:], ACT.Tanh).then_inc(act_step, 1)
            with act.Fori(0, NC2) as i:
                act.wait_ge(ct_ps, i + 1)
                for k in range(KT):
                    last = nc.scalar.activation(cT[:, k, :], t_ps[:, k, 0:2 * CR], ACT.Identity,
                                                scale=w["gcol"][:, k:k + 1], bias=w["bcol"][:, k:k + 1])
                last.then_inc(ct_ready, 1)
                for k in range(KT):
                    last = nc.scalar.activation(w["zcT"][:, k, bass.ds(i * (2 * CR), 2 * CR)], t_ps[:, k, 0:2 * CR],
                                                ACT.Identity, scale=w["gcol"][:, k:k + 1], bias=w["bcol"][:, k:k + 1])
                last.then_inc(zc_kept, 1)
                act.wait_ge(kT_ps, i + 1)
                act.wait_ge(kT_stored, i * 16 + START)
                nc.scalar.activation(kstT[:], t_ps[0:2 * H, 0, 0:2 * CR].rearrange("h (t p) -> h t p", p=CR),
                               ACT.Copy).then_inc(kT_ready, 1)
            act.wait_ge(pool_step, 3)
            nc.scalar.activation(dec[:], dec[:], ACT.Exp, scale=-5.0 / (ROWS * DH * DH)).then_inc(act_step, 1)
            act.wait_ge(step, DVE_TAIL["lmax"])
            nc.scalar.activation(lg[:, 5:8], lg[:, 0:3], ACT.Exp, bias=lg[:, 3:4],
                                 accum_out=lg[:, 4:5]).then_inc(act_step, 1)

        @block.tensor
        def _(pe):
            pe.wait_ge(consts, 7)
            pe.wait_ge(loaded, 16 * N_LOADS)
            for k in range(KT):
                nc.tensor.matmul(gram_ps[k][:, 0:DIM + 1], zeros[:, 0:P], zeros[:, :], start=True, stop=False)
            with pe.Fori(0, NX) as i:
                for half in range(2):
                    pe.wait_ge(xa_ready[half], i + 1)
                    for t in range(XT):
                        for k in range(KT):
                            last = nc.tensor.matmul(gram_ps[k][:, 0:DIM + 1], xa[:, half, t, k * P:(k + 1) * P],
                                                    xa[:, half, t, 0:DIM + 1], start=False, stop=False)
                    last.then_inc(grammed[half], 1)
            for k in range(KT):
                last = nc.tensor.matmul(gram_ps[k][:, 0:DIM + 1], zeros[:, 0:P], zeros[:, :], start=False, stop=True)
            last.then_inc(pe_step, 1)
            with pe.Fori(0, NC2) as i:
                pe.wait_ge(cz_ready, i + 1)
                pe.wait_ge(kT_ready, i + START)
                for t in range(2):
                    for k in range(KT):
                        last = nc.tensor.transpose(t_ps[:, k, t * CR:(t + 1) * CR], cz[:, t, k * P:(k + 1) * P],
                                                   w["ident"][0:CR, 0:CR])
                last.then_inc(ct_ps, 1)
                pe.wait_ge(ct_ready, i + 1)
                for t in range(2):
                    for c in range(2):
                        for k in range(KT):
                            last = nc.tensor.matmul(f_ps[0:CR, 2 * t + c, :], cT[:, k, t * CR:(t + 1) * CR],
                                                    w["wT"][:, k, c * 512:(c + 1) * 512],
                                                    start=(k == 0), stop=(k == KT - 1))
                last.then_inc(f_ready, 1)
                pe.wait_ge(kst_ready, i + 1)
                pe.wait_ge(zc_kept, i + 1)
                for t in range(2):
                    last = nc.tensor.transpose(t_ps[0:2 * H, 0, t * CR:(t + 1) * CR],
                                               kst[:, t, :, :].rearrange("p a h -> p (a h)"), w["ident"][0:CR, 0:CR])
                last.then_inc(kT_ps, 1)
            pe.wait_ge(step, DVE_TAIL["wcT"])
            for m in range(KT):
                for c in range(2):
                    for k in range(KT):
                        last = nc.tensor.matmul(f_ps[:, 2 * m + c, :], gram[:, k, m * P:(m + 1) * P],
                                                wcT[:, k, c * 512:(c + 1) * 512], start=(k == 0), stop=(k == KT - 1))
            last.then_inc(pe_step, 1)
            pe.wait_ge(step, DVE_TAIL["hm"])
            pe.wait_ge(kT_ready, NC2 + START)
            for h in range(H):
                for k in range(KT):
                    nc.tensor.matmul(t_ps[:, 0, h:h + 1], w["wT"][:, k, h * DH:(h + 1) * DH],
                                     gram[:, k, DIM:DIM + 1], start=(k == 0), stop=(k == KT - 1))
            for h in range(H):
                for k in range(KT):
                    nc.tensor.matmul(t_ps[:, 0, H + h:H + h + 1], w["wT"][:, k, h * DH:(h + 1) * DH],
                                     csum[:, k:k + 1], start=(k == 0), stop=(k == KT - 1))
            for h in range(H):
                for k in range(KT):
                    last = nc.tensor.matmul(f_ps[:, h // 4, (h % 4) * DH:(h % 4 + 1) * DH],
                                            wcT[:, k, h * DH:(h + 1) * DH], hm[:, k, h * DH:(h + 1) * DH],
                                            start=(k == 0), stop=(k == KT - 1))
            last.then_inc(pe_step, 1)
            pe.wait_ge(step, DVE_TAIL["fcsum"])
            nc.tensor.matmul(t_ps[:, 1, 0:H], ones[:], fcs[:], start=True, stop=True).then_inc(pe_step, 1)
            pe.wait_ge(step, DVE_TAIL["fe"])
            for k in range(2):
                last = nc.tensor.matmul(t_ps[0:H, 0, 0:DH], fe[:, k, :], w1T_sb[:, k, :], start=(k == 0), stop=(k == 1))
            last.then_inc(pe_step, 1)
            pe.wait_ge(step, DVE_TAIL["h1"])
            nc.tensor.transpose(t_ps[:, 1, 0:H], h1[:], w["ident"][0:H, 0:H]).then_inc(pe_step, 1)
            pe.wait_ge(step, DVE_TAIL["h1T"])
            nc.tensor.matmul(t_ps[0:H, 0, 0:3], h1T[:], w2T_sb[:], start=True, stop=True).then_inc(pe_step, 1)
            pe.wait_ge(step, DVE_TAIL["dgw"])
            nc.tensor.matmul(t_ps[:, 1, 0:3 * H], ones[0:H, :], dgw[:].rearrange("p a h -> p (a h)"),
                             start=True, stop=True).then_inc(pe_step, 1)
            for m in range(KT):
                for k in range(KT):
                    last = nc.tensor.matmul(f_ps[:, m, 0:DIM], woT_sb[:, k, m * P:(m + 1) * P], wff_sb[:, k, :],
                                            start=(k == 0), stop=(k == KT - 1))
            last.then_inc(pe_step, 1)


DVE_LOOPS = 4 * 10 + 11 * 14
_TAIL = ["csum", "wsum", "wmean", "wcT", "hm", "fcmask", "fcsq", "fcsum", "fe", "fcs", "h1add", "h1bn", "h1aggr",
         "h1var", "h1norm", "h1g", "h1b", "h1", "h1T", "ladd", "lmax", "lrec", "lscale", "dgw"]
DVE_TAIL = {name: DVE_LOOPS + 1 + n for n, name in enumerate(_TAIL)}


def moments(nc, link, k0, st, ft):
    half = DH // 2
    me, qe, mo, qo = (st[:, :, :, j] for j in (1, 2, 4, 5))
    nc.vector.tensor_tensor(ft[:, 0, :, :], me, mo, ALU.add)
    nc.vector.tensor_tensor(ft[:, 1, :, :], me, mo, ALU.subtract)
    link(k0, nc.vector.tensor_tensor(ft[:, 2, :, :], qe, qo, ALU.add))
    nc.vector.tensor_tensor(ft[:, 3, :, :], ft[:, 1, :, :], ft[:, 1, :, :], ALU.mult)
    link(k0 + 1, nc.vector.tensor_tensor(ft[:, 4, :, :], ft[:, 0, :, :], ft[:, 0, :, :], ALU.mult))
    link(k0 + 2, nc.vector.scalar_tensor_tensor(ft[:, 2, :, :], ft[:, 3, :, :], half / 2.0, ft[:, 2, :, :],
                                                ALU.mult, ALU.add))
    nc.vector.tensor_scalar(ft[:, 1, :, :], ft[:, 2, :, :], 1.0 / (DH - 1), None, ALU.mult)
    link(k0 + 3, nc.vector.scalar_tensor_tensor(ft[:, 0, :, :], ft[:, 4, :, :], DH / 4.0, ft[:, 2, :, :],
                                                ALU.mult, ALU.add))
    link(k0 + 4, nc.vector.tensor_copy(ft[:, 5, :, :], ft[:, 1, :, :]))


def row_moments(nc, link, k0, st, mv, tmp):
    me, qe, mo, qo = (st[:, :, j] for j in (1, 2, 4, 5))
    nc.vector.tensor_tensor(mv[:, :, 0], me, mo, ALU.add)
    nc.vector.tensor_tensor(tmp[:, :, 0], me, mo, ALU.subtract)
    link(k0, nc.vector.tensor_tensor(tmp[:, :, 1], qe, qo, ALU.add))
    nc.vector.tensor_scalar(mv[:, :, 0], mv[:, :, 0], 0.5, None, ALU.mult)
    link(k0 + 1, nc.vector.tensor_tensor(tmp[:, :, 0], tmp[:, :, 0], tmp[:, :, 0], ALU.mult))
    link(k0 + 2, nc.vector.scalar_tensor_tensor(tmp[:, :, 1], tmp[:, :, 0], DIM / 4.0, tmp[:, :, 1], ALU.mult, ALU.add))


def ratio_num(nc, ft):
    return nc.vector.tensor_scalar(ft[:, 2, :, :], ft[:, 1, :, :], 1.0, 2.0, ALU.min, ALU.mult)


def ratio_den(nc, ft):
    return nc.vector.tensor_scalar(ft[:, 3, :, :], ft[:, 1, :, :], 1.0, None, ALU.add)


A_CHUNKS = (["zT0", "zT1", "fk0", "fk1", "fk2"] + [f"q{c}" for c in range(2 * PT)] + [f"G{c}" for c in range(6)]
            + [f"V{c}" for c in range(6)] + ["d0", "d1", "d2", "d3", "m0", "m1", "m2", "d4", "d5", "d6", "d7", "y0",
                                             "m3", "m4", "m5", "y1"]
            + ["zz0", "zz1", "pq0", "pq1", "pk0", "pk1", "pv0", "pv1"])
A_INDEX = {name: k for k, name in enumerate(A_CHUNKS)}
WORK = 2
WORK_USES = [len(range(s, len(A_CHUNKS), WORK)) for s in range(WORK)]
GROUPS = 2 * FH * KT // 4
PG = 2
SC = 3
LAG = 1
START = 1
EXP_CREDIT, PV_CREDIT, OT_CREDIT = 6, PG, 2
A_STEPS, B_STEPS = 14, GROUPS + 5


def a_events():
    out = ["z"]
    for name in A_CHUNKS:
        out.append(name)
        if name == "q7":
            out.append("qstat")
        if name == "y1":
            out.append("ln2")
    return [("A", e) for e in out]


def b_events():
    out = []
    for g in range(GROUPS + LAG):
        if g < GROUPS:
            out += [("S", 2 * g), ("S", 2 * g + 1)]
        p = g - LAG
        if p >= 0:
            out.append(("P", p))
            if p % 4 == 3:
                out.append(("E", p // 4))
            if p % 8 == 7:
                out += [("O", p // 8 * 2), ("O", p // 8 * 2 + 1)]
    return out + [("F", 0)]


def merged(ahead=9):
    a, b = a_events(), b_events()
    out, a = a[:ahead], a[ahead:]
    n = 0
    for k, e in enumerate(b):
        out.append(e)
        while n < len(a) and n * len(b) < (k + 1) * len(a):
            out.append(a[n])
            n += 1
    return out + a[n:]


def unit(group):
    return group // 8, group % 8 // 4, group % 4 // 2, group % 2


def window(t, h):
    return 127 + P * t - MK * h


def tile_heads(t):
    return [h for h in range(H) if MK * h < P * (t + 1) and MK * (h + 1) > P * t]


def main_phase(nc, ctx, w, x_rows, out_rows, kstat, parts):
    def sb(name, shape, dt=F32):
        return ctx.enter_context(nc.sbuf_tensor(name, shape, dt))

    def ps(name, shape):
        return ctx.enter_context(nc.psum_tensor(name, shape, F32))

    def sem(name):
        return ctx.enter_context(nc.semaphore(name))

    xin, xb = sb("xin", [P, PT, DIM]), sb("xb", [P, PT, DIM])
    z, xT = sb("z", [P, PT, DIM]), sb("xT", [P, KT, PR])
    rkb, krb = sb("rkb", [P, H, PM]), sb("krb", [P, H, PM])
    fvp, kT = sb("fvp", [P, 2, H, PADW]), sb("kT", [P, H, PM])
    G, Vp = sb("G", [P, KT, 2, HM]), sb("Vp", [P, 2, HT, DIM])
    mixed, tmp = sb("mixed", [P, 2, HM]), sb("tmp", [P, HM])
    mT = sb("mT", [P, HT, 2 * P])
    st4, qst, qft = sb("st4", [P, PT, 2]), sb("qst", [P, PT, H, 6]), sb("qft", [P, 6, PT, H])
    rq, sq, wqr = sb("rq", [P, PT, H]), sb("sq", [P, PT, H]), sb("wqr", [P, PT, H])
    x2S, l2s, l2m = sb("x2S", [P, PT, DIM]), sb("l2s", [P, PT, 6]), sb("l2m", [P, PT, 2])
    l2t = sb("l2t", [P, PT, 2])
    l2v, l2r = sb("l2v", [P, PT]), sb("l2r", [P, PT])
    zzT = sb("zzT", [P, KT, PR])
    hi = {a: sb(a + "h", [P, 2, PR], F16) for a in "qk"}
    lo = {a: sb(a + "l", [P, 2, PR], F16) for a in "qk"}
    vS, v = sb("vS", [P, PT, DIM]), sb("v", [P, PT, DIM])
    stack = {a: sb(a + "stack", [P, FH // 2, PR], F16) for a in "qk"}
    x2 = sb("x2", [P, PT, DIM])
    prob, vsp = sb("prob", [P, PG * 4, NQ]), sb("vsp", [P, KT, 4, 3 * FD])
    nm, sums, rs = sb("nm", [P, 4 * GROUPS]), sb("sums", [P, 4 * GROUPS]), sb("rs", [P, 4 * GROUPS])
    oT, zb, junk = sb("oT", [P, 2, PR]), sb("zb", [P, PT, DIM]), sb("junk", [P, 2, DIM])
    nrm, nrs, fac = sb("nrm", [P, 2, PT]), sb("nrs", [P, 2, PT]), sb("fac", [P, 5, PT])

    work = [ps(f"work{s}", [P, 512]) for s in range(WORK)]
    sc = [ps(f"score{s}", [P, 512]) for s in range(SC)]
    pvb = [ps(f"attended{s}", [P, 512]) for s in range(2)]
    fin = ps("fin", [P, 512])

    filled, drained = [sem(f"filled{s}") for s in range(WORK)], [sem(f"drained{s}") for s in range(WORK)]
    init, x_ready, rk_in, kr_in = sem("init"), sem("x_ready"), sem("rk_in"), sem("kr_in")
    z_ready, xb_ready, kT_ready = sem("z_ready"), sem("xb_ready"), sem("kT_ready")
    qsq_ready, rq_ready, wqr_ready, mixed_ready = sem("qsq"), sem("rq_ready"), sem("wqr_ready"), sem("mixed_ready")
    v2_ready, r2_ready, zz_ready, hi_ready = sem("v2_ready"), sem("r2_ready"), sem("zz_ready"), sem("hi_ready")
    parts_stored, stack_in, v_in, x2_in = sem("parts_stored"), sem("stack_in"), sem("v_in"), sem("x2_in")
    sc_ready, max_ready, exp_done = sem("sc_ready"), sem("max_ready"), sem("exp_done")
    vs_ready, pv_done, ot_done = sem("vs_ready"), sem("pv_done"), sem("ot_done")
    fin_ready, fin_free, nrm_ready, fac_ready = sem("fin_ready"), sem("fin_free"), sem("nrm_ready"), sem("fac_ready")
    gelu_ready, ob_ready, stored = sem("gelu_ready"), sem("ob_ready"), sem("stored")
    a_step, b_step, tmp_ready, turns = sem("a_step"), sem("b_step"), sem("tmp_ready"), sem("turns")

    def bank(name):
        return work[A_INDEX[name] % WORK]

    def uses(name, a):
        k = A_INDEX[name]
        return a * WORK_USES[k % WORK] + k // WORK

    def wait_filled(eng, name, a):
        eng.wait_ge(filled[A_INDEX[name] % WORK], uses(name, a) + 1)

    def wait_drained(eng, name, a):
        eng.wait_ge(drained[A_INDEX[name] % WORK], uses(name, a) + 1)

    def wait_free(eng, name, a):
        eng.wait_ge(drained[A_INDEX[name] % WORK], uses(name, a))

    def fill(ins, name):
        ins.then_inc(filled[A_INDEX[name] % WORK], 1)

    def drain(ins, name):
        ins.then_inc(drained[A_INDEX[name] % WORK], 1)

    def key_rows(ap):
        return ap.rearrange("p h (b m) -> p h b m", m=MK)

    ORDER = merged()

    def run(eng, a_part, b_part):
        for _, e in a_events():
            a_part(e, 0)
        with eng.Fori(0, NPAIR - 1) as i:
            for kind, e in ORDER:
                if kind == "A":
                    a_part(e, i + 1)
                else:
                    b_part(kind, e, i)
        for kind, e in b_events():
            b_part(kind, e, NPAIR - 1)

    with nc.Block() as block:
        @block.sync
        def _(sp):
            for waited in (stack_in, ob_ready, vs_ready, sc_ready, stored, fin_ready, fin_free):
                sp.sem_inc(waited, START)
            sp.sem_inc(exp_done, EXP_CREDIT)
            sp.sem_inc(pv_done, PV_CREDIT)
            sp.sem_inc(ot_done, OT_CREDIT)

            def sp_wait(ready, value):
                sp.wait_ge(ready, value)
                sp.sem_inc(turns, 1)

            def drained_at(name, i):
                return drained[A_INDEX[name] % WORK], uses(name, i) + 1

            def load(a):
                sp_wait(z_ready, a)
                sp_wait(xb_ready, a)
                sp.dma_start(xin[:], x_rows[bass.ds(a * PR, PR), :].rearrange("(t p) d -> p t d", p=P)).then_inc(x_ready, 16)
                sp_wait(kT_ready, a * 3)
                sp.dma_start(rkb[:], kstat[0:H, bass.ds(a * PM, PM)].partition_broadcast(P)).then_inc(rk_in, 16)
                sp_wait(mixed_ready, a * PT)
                sp.dma_start(krb[:], kstat[H:2 * H, bass.ds(a * PM, PM)].partition_broadcast(P)).then_inc(kr_in, 16)

            def move(i):
                sp_wait(*drained_at("pk0", i))
                sp_wait(*drained_at("pk1", i))
                sp_wait(stack_in, i * 256 + START)
                for n, t in enumerate((hi["q"], lo["q"], hi["k"], lo["k"])):
                    sp.dma_start(parts[n].rearrange("(t p) n -> p t n", p=P), t[:]).then_inc(parts_stored, 16)
                sp_wait(*drained_at("y1", i))
                sp_wait(ob_ready, i + START)
                sp.dma_start(x2[:], x2S[:]).then_inc(x2_in, 16)
                sp_wait(*drained_at("pv0", i))
                sp_wait(*drained_at("pv1", i))
                sp_wait(vs_ready, i * GROUPS + START)
                sp.dma_start(v[:], vS[:]).then_inc(v_in, 16)
                sp_wait(parts_stored, i * 64 + 64)
                sp_wait(sc_ready, i * 2 * GROUPS + START)
                for c in range(4):
                    for e in range(2):
                        for a, n in (("k", 2 + c // 2), ("q", c % 2)):
                            src = parts[n].rearrange("(q e d) n -> e d q n", e=2, d=FD)[e]
                            sp.dma_start(stack[a][64 * e + FD * c:64 * e + FD * (c + 1), :, :], src).then_inc(stack_in, 16)

            def store(i):
                sp_wait(ob_ready, i + 1 + START)
                sp.dma_start(out_rows[bass.ds(i * PR, PR), :].rearrange("(t p) d -> p t d", p=P), zb[:]).then_inc(stored, 16)

            load(0)
            load(1)
            with sp.Fori(0, NPAIR - 2) as i:
                move(i)
                load(i + 2)
                store(i)
            for i in (NPAIR - 2, NPAIR - 1):
                move(i)
                store(i)
            sp.wait_ge(stored, 16 * NPAIR + START)

        @block.tensor
        def _(pe):
            ident = w["ident"]

            def a_part(e, a):
                if e in ("z", "qstat", "ln2"):
                    return
                kind, c = e[:-1], int(e[-1])
                bk = bank(e)
                wait_free(pe, e, a)
                if kind in ("zT", "zz"):
                    src = z
                    pe.wait_ge(z_ready if kind == "zT" else zz_ready, a + 1)
                    for t in range(PT):
                        last = nc.tensor.transpose(bk[:, t * P:(t + 1) * P], src[:, t, c * P:(c + 1) * P], ident[:])
                elif kind == "fk":
                    lo_h, hi_h = HEAD_PARTS[c]
                    for h in range(lo_h, hi_h):
                        for k in range(KT):
                            last = nc.tensor.matmul(bk[:, (h - lo_h) * PM:(h - lo_h + 1) * PM],
                                                    w["wT"][:, k, h * DH:(h + 1) * DH],
                                                    w["zcT"][:, k, bass.ds(a * PM, PM)], start=(k == 0), stop=(k == KT - 1))
                elif kind == "q":
                    if c == 0:
                        wait_drained(pe, "zT0", a)
                        wait_drained(pe, "zT1", a)
                    t, half = c // 2, c % 2
                    for k in range(KT):
                        last = nc.tensor.matmul(bk[:, :], xT[:, k, t * P:(t + 1) * P],
                                                w["wT"][:, k, half * 512:(half + 1) * 512], start=(k == 0), stop=(k == KT - 1))
                elif kind == "G":
                    k, (lo_h, hi_h) = c // 3, HEAD_PARTS[c % 3]
                    pe.wait_ge(kT_ready, a * 3 + c % 3 + 1)
                    for h in range(lo_h, hi_h):
                        last = nc.tensor.matmul(bk[:, (h - lo_h) * PM:(h - lo_h + 1) * PM], w["wN"][:, h, k * P:(k + 1) * P],
                                                kT[:, h, :], start=True, stop=True)
                elif kind == "V":
                    b2, tiles = c // 3, HM_TILES[c % 3]
                    for n, t in enumerate(tiles):
                        heads = tile_heads(t)
                        for h in heads:
                            last = nc.tensor.matmul(bk[:, n * DIM:(n + 1) * DIM], fvp[:, b2, h, window(t, h):window(t, h) + P],
                                                    w["woutT"][:, h, :], start=(h == heads[0]), stop=(h == heads[-1]))
                elif kind == "d":
                    t, half = c // 2, c % 2
                    if c == 0:
                        wait_drained(pe, "G4", a)
                        wait_drained(pe, "G5", a)
                    for k in range(KT):
                        last = nc.tensor.matmul(bk[:, 0:HM // 2], xT[:, k, t * P:(t + 1) * P],
                                                G[:, k, t // 2, half * (HM // 2):(half + 1) * (HM // 2)],
                                                start=(k == 0), stop=(k == KT - 1))
                elif kind == "m":
                    b2, tiles = c // 3, HM_TILES[c % 3]
                    pe.wait_ge(mixed_ready, a * PT + 2 * b2 + 2)
                    for n, t in enumerate(tiles):
                        for r in range(2):
                            last = nc.tensor.transpose(bk[0:HM_ROWS[t], (2 * n + r) * P:(2 * n + r + 1) * P],
                                                       mixed[:, r, t * P:t * P + HM_ROWS[t]], ident[:])
                elif kind == "y":
                    wait_drained(pe, f"m{3 * c + 2}", a)
                    for r in range(2):
                        for t in range(HT):
                            last = nc.tensor.matmul(bk[:, r * DIM:(r + 1) * DIM], mT[0:HM_ROWS[t], t, r * P:(r + 1) * P],
                                                    Vp[0:HM_ROWS[t], c, t, :], start=(t == 0), stop=(t == HT - 1))
                elif kind in ("pq", "pk"):
                    if e == "pq0":
                        wait_drained(pe, "zz0", a)
                        wait_drained(pe, "zz1", a)
                    for k in range(KT):
                        last = nc.tensor.matmul(bk[:, :], w["w" + kind[1]][:, k, c * P:(c + 1) * P], zzT[:, k, :],
                                                start=(k == 0), stop=(k == KT - 1))
                elif kind == "pv":
                    for r in range(2):
                        for k in range(KT):
                            last = nc.tensor.matmul(bk[:, r * DIM:(r + 1) * DIM], zzT[:, k, (2 * c + r) * P:(2 * c + r + 1) * P],
                                                    w["wv"][:, k, :], start=(k == 0), stop=(k == KT - 1))
                fill(last, e)

            def b_part(kind, n, b):
                if kind == "S":
                    b2, t, e, k = unit(n // 2)
                    if n == 0:
                        pe.wait_ge(stack_in, b * 256 + 256 + START)
                    back = 3 if n >= 3 else 2 if n < 2 else 5
                    pe.wait_ge(exp_done, b * 4 * GROUPS + 2 * (n - back) + 2 + EXP_CREDIT)
                    for jj in range(2):
                        j = 4 * t + 2 * (n % 2) + jj
                        last = nc.tensor.matmul(sc[n % SC][:, jj * NQ:(jj + 1) * NQ],
                                                stack["k"][64 * e:64 * e + 64, j, b2 * NQ + k * P:b2 * NQ + (k + 1) * P],
                                                stack["q"][64 * e:64 * e + 64, j, b2 * NQ:(b2 + 1) * NQ],
                                                start=True, stop=True)
                    last.then_inc(sc_ready, 1)
                elif kind == "P":
                    b2, t, e, k = unit(n)
                    pe.wait_ge(vs_ready, b * GROUPS + n + 1 + START)
                    if n % 4 == 0:
                        pe.wait_ge(ot_done, b * 4 + n // 4 + 1)
                    lo_c = FD * (1 - e)
                    for j in range(4):
                        last = nc.tensor.matmul(pvb[t][32 * j:32 * j + 32, 0:NQ], vsp[:, k, j, lo_c:lo_c + 2 * FD],
                                                prob[:, (n % PG) * 4 + j, :], start=(n % 4 == 0), stop=(n % 4 == 3))
                    last.then_inc(pv_done, 1)
                elif kind == "O":
                    pe.wait_ge(ot_done, b * 4 + 2 * (n // 2) + 2 + OT_CREDIT)
                    pe.wait_ge(fin_free, b * PT + n + START)
                    for k in range(2):
                        last = nc.tensor.matmul(fin[:, :], oT[:, k, n * P:(n + 1) * P], w["wof"][:, k, :],
                                                start=(k == 0), stop=(k == 1))
                    last.then_inc(fin_ready, 1)

            pe.wait_ge(init, 3)
            run(pe, a_part, b_part)

        @block.scalar
        def _(act):
            act.wait_ge(init, 3)

            def a_part(e, a):
                kind, c = e[:-1], e[-1]
                if kind not in ("zT", "fk", "G", "V", "m", "zz", "pq", "pk", "pv"):
                    return
                c, bk = int(c), bank(e)
                wait_filled(act, e, a)
                if kind == "zT":
                    ins = nc.scalar.activation(xT[:, c, :], bk[:, :], ACT.Identity,
                                               scale=w["gcol"][:, c:c + 1], bias=w["bcol"][:, c:c + 1])
                elif kind == "fk":
                    lo_h, hi_h = HEAD_PARTS[c]
                    ins = nc.scalar.activation(fvp[:, :, lo_h:hi_h, 127:127 + MK].rearrange("p b h m -> p h b m"),
                                               bk[:, 0:(hi_h - lo_h) * PM].rearrange("p (h b m) -> p h b m", b=2, m=MK),
                                               ACT.Copy)
                elif kind == "G":
                    lo_h, hi_h = HEAD_PARTS[c % 3]
                    dst = G[:, c // 3, :, lo_h * MK:hi_h * MK].rearrange("p b (h m) -> p h b m", m=MK)
                    ins = nc.scalar.activation(dst, bk[:, 0:(hi_h - lo_h) * PM].rearrange("p (h b m) -> p h b m", b=2, m=MK),
                                               ACT.Copy)
                elif kind == "V":
                    tiles = HM_TILES[c % 3]
                    ins = nc.scalar.activation(Vp[:, c // 3, tiles[0]:tiles[-1] + 1, :],
                                               bk[:, 0:len(tiles) * DIM].rearrange("p (t o) -> p t o", o=DIM), ACT.Copy)
                elif kind == "m":
                    tiles = HM_TILES[c % 3]
                    r = HM_ROWS[tiles[0]]
                    ins = nc.scalar.activation(mT[0:r, tiles[0]:tiles[-1] + 1, :],
                                               bk[0:r, 0:len(tiles) * 2 * P].rearrange("p (t n) -> p t n", n=2 * P), ACT.Copy)
                elif kind == "zz":
                    ins = nc.scalar.activation(zzT[:, c, :], bk[:, :], ACT.Copy)
                elif kind in ("pq", "pk"):
                    act.wait_ge(parts_stored, a * 64)
                    nc.scalar.activation(hi[kind[1]][:, c, :], bk[:, :], ACT.Copy,
                                         scale=1.0 / 16 if kind == "pq" else 1.0).then_inc(hi_ready, 1)
                    return
                elif kind == "pv":
                    act.wait_ge(v_in, a * 16)
                    ins = nc.scalar.activation(vS[:, 2 * c:2 * c + 2, :], bk[:, :].rearrange("p (t o) -> p t o", o=DIM), ACT.Copy)
                drain(ins, e)

            def b_part(kind, n, b):
                if kind == "S":
                    g = n // 2
                    act.wait_ge(max_ready, b * 2 * GROUPS + n + 1)
                    if n % 2 == 0:
                        act.wait_ge(pv_done, b * GROUPS + g - PG + 1 + PV_CREDIT)
                    for jj in range(2):
                        u = 2 * n + jj
                        nc.scalar.activation(prob[:, u % (4 * PG), :], sc[n % SC][:, jj * NQ:(jj + 1) * NQ], ACT.Exp,
                                             bias=nm[:, u:u + 1], accum_out=sums[:, u:u + 1]).then_inc(exp_done, 1)
                elif kind == "E":
                    act.wait_ge(pv_done, b * GROUPS + 4 * n + 4 + PV_CREDIT)
                    act.wait_ge(fin_ready, b * PT + START)
                    nc.scalar.activation(oT[:, n % 2, (n // 2) * NQ:(n // 2 + 1) * NQ], pvb[n % 2][:, 0:NQ],
                                         ACT.Copy).then_inc(ot_done, 1)
                elif kind == "O":
                    act.wait_ge(fin_ready, b * PT + n + 1 + START)
                    if n == 0:
                        act.wait_ge(stored, b * 16 + START)
                    for j in range(2):
                        nc.scalar.activation(junk[:, j, :], fin[:, j * DIM:(j + 1) * DIM], ACT.Square, accum_out=nrm[:, j, n:n + 1])
                    nc.scalar.activation(zb[:, n, :], fin[:, DIM:2 * DIM], ACT.Copy).then_inc(fin_free, 1)
                elif kind == "F":
                    act.wait_ge(fac_ready, b + 1)
                    for t in range(PT):
                        last = nc.scalar.activation(zb[:, t, :], zb[:, t, :], ACT.Gelu, scale=fac[:, 4, t:t + 1])
                    last.then_inc(gelu_ready, 1)

            run(act, a_part, b_part)

        @block.gpsimd
        def _(pool):
            def a_part(e, a):
                if e == "z":
                    pool.wait_ge(x_ready, a * 16 + 16)
                    pool.wait_ge(v2_ready, a)
                    nc.gpsimd.tensor_tensor(xb[:], xin[:], bc(w["tb"][:].unsqueeze(1), [P, PT, DIM]),
                                            ALU.add).then_inc(xb_ready, 1)
                elif e == "qstat":
                    pool.wait_ge(qsq_ready, a + 1)
                    nc.gpsimd.tensor_tensor(rq[:], qft[:, 0, :, :], w["mhalf"][:].rearrange("p (t h) -> p t h", h=H),
                                            ALU.pow).then_inc(rq_ready, 1)
                elif e in ("d1", "d3", "d5", "d7"):
                    t = int(e[1]) // 2
                    pool.wait_ge(kr_in, a * 16 + 16)
                    pool.wait_ge(wqr_ready, a + 1)
                    pool.wait_ge(mixed_ready, a * PT + t)
                    nc.gpsimd.tensor_tensor(tmp[:].rearrange("p (h m) -> p h m", m=MK),
                                            krb[:, :, (t // 2) * MK:(t // 2 + 1) * MK],
                                            bc(wqr[:, t, :].unsqueeze(2), [P, H, MK]), ALU.mult).then_inc(tmp_ready, 1)
                    pool.wait_ge(tmp_ready, a * PT + t + 1)
                    wait_drained(pool, f"d{2 * t}", a)
                    wait_drained(pool, f"d{2 * t + 1}", a)
                    nc.gpsimd.tensor_tensor(mixed[:, t % 2, :], mixed[:, t % 2, :], tmp[:], ALU.add).then_inc(mixed_ready, 1)
                elif e == "ln2":
                    pool.wait_ge(v2_ready, a + 1)
                    nc.gpsimd.tensor_tensor(l2r[:], l2v[:], w["mhalf"][:, 0:PT], ALU.pow).then_inc(r2_ready, 1)

            def b_part(kind, n, b):
                if kind == "F":
                    pool.wait_ge(fin_free, b * PT + PT + START)
                    nc.gpsimd.tensor_tensor(nrs[:].rearrange("p j t -> p (j t)"), nrm[:].rearrange("p j t -> p (j t)"),
                                            w["phalf"][:, 0:2 * PT], ALU.pow).then_inc(nrm_ready, 1)

            run(pool, a_part, b_part)

        @block.vector
        def _(dve):
            nc.vector.memset(vsp[:], 0.0).then_inc(init, 1)
            nc.vector.memset(fvp[:, 0, :, :], 0.0).then_inc(init, 1)
            nc.vector.memset(fvp[:, 1, :, :], 0.0).then_inc(init, 1)

            def a_part(e, a):
                def link(k, ins):
                    ins.then_inc(a_step, 1)
                    dve.wait_ge(a_step, a * A_STEPS + k)

                kind, c = e[:-1], e[-1]
                if e == "z":
                    dve.wait_ge(x_ready, a * 16 + 16)
                    link(1, nc.vector.tensor_copy(st4[:], w["stats"][:, bass.ds(a * PT, PT), :]))
                    for t in range(PT):
                        last = nc.vector.tensor_scalar(z[:, t, :], xin[:, t, :], st4[:, t, 0:1], st4[:, t, 1:2],
                                                       ALU.subtract, ALU.mult)
                    last.then_inc(z_ready, 1)
                elif kind == "fk":
                    lo_h, hi_h = HEAD_PARTS[int(c)]
                    wait_drained(dve, e, a)
                    dve.wait_ge(rk_in, a * 16 + 16)
                    nc.vector.tensor_tensor(key_rows(kT[:, lo_h:hi_h, :]),
                                            fvp[:, :, lo_h:hi_h, 127:127 + MK].rearrange("p b h m -> p h b m"),
                                            key_rows(rkb[:, lo_h:hi_h, :]), ALU.mult).then_inc(kT_ready, 1)
                elif kind == "q":
                    t, half = int(c) // 2, int(c) % 2
                    wait_filled(dve, e, a)
                    for h in range(4):
                        last = nc.vector.bn_stats(qst[:, t, 4 * half + h, :], bank(e)[:, h * DH:(h + 1) * DH])
                    drain(last, e)
                elif e == "qstat":
                    wait_drained(dve, "q6", a)
                    wait_drained(dve, "q7", a)
                    moments(nc, link, 2, qst[:], qft)
                    dve.sem_inc(qsq_ready, 1)
                    ratio_num(nc, qft)
                    link(7, ratio_den(nc, qft))
                    link(8, nc.vector.reciprocal(qft[:, 3, :, :], qft[:, 3, :, :]))
                    link(9, nc.vector.tensor_tensor(qft[:, 2, :, :], qft[:, 2, :, :], qft[:, 3, :, :], ALU.mult))
                    nc.vector.tensor_tensor(wqr[:], qft[:, 2, :, :], bc(w["wwv"][:].unsqueeze(1), [P, PT, H]),
                                            ALU.mult).then_inc(wqr_ready, 1)
                    dve.wait_ge(rq_ready, a + 1)
                    link(10, nc.vector.tensor_tensor(sq[:], rq[:], bc(w["cvec"][:].unsqueeze(1), [P, PT, H]), ALU.mult))
                elif kind == "d":
                    t, half = int(c) // 2, int(c) % 2
                    wait_filled(dve, e, a)
                    drain(nc.vector.tensor_tensor(
                        mixed[:, t % 2, half * (HM // 2):(half + 1) * (HM // 2)].rearrange("p (h m) -> p h m", m=MK),
                        bank(e)[:, 0:HM // 2].rearrange("p (h m) -> p h m", m=MK),
                        bc(sq[:, t, 4 * half:4 * half + 4].unsqueeze(2), [P, 4, MK]), ALU.mult), e)
                elif kind == "y":
                    c = int(c)
                    wait_filled(dve, e, a)
                    dve.wait_ge(xb_ready, a + 1)
                    dve.wait_ge(x2_in, a * 16)
                    drain(nc.vector.tensor_tensor(x2S[:, 2 * c:2 * c + 2, :], bank(e)[:, :].rearrange("p (t o) -> p t o", o=DIM),
                                                  xb[:, 2 * c:2 * c + 2, :], ALU.add), e)
                elif e == "ln2":
                    wait_drained(dve, "y0", a)
                    wait_drained(dve, "y1", a)
                    for t in range(PT):
                        last = nc.vector.bn_stats(l2s[:, t, :], x2S[:, t, :])
                    link(11, last)
                    row_moments(nc, link, 12, l2s, l2m, l2t)
                    nc.vector.tensor_scalar(l2v[:], l2t[:, :, 1], 1.0 / DIM, EPS, ALU.mult, ALU.add).then_inc(v2_ready, 1)
                    dve.wait_ge(r2_ready, a + 1)
                    for t in range(PT):
                        last = nc.vector.tensor_scalar(z[:, t, :], x2S[:, t, :], l2m[:, t, 0:1], l2r[:, t:t + 1],
                                                       ALU.subtract, ALU.mult)
                    last.then_inc(zz_ready, 1)
                elif kind in ("pq", "pk"):
                    n = ("pq0", "pq1", "pk0", "pk1").index(e)
                    dve.wait_ge(hi_ready, a * 4 + n + 1)
                    drain(nc.vector.scalar_tensor_tensor(lo[kind[1]][:, int(c), :], bank(e)[:, :],
                                                         1.0 / 16 if kind == "pq" else 1.0, hi[kind[1]][:, int(c), :],
                                                         ALU.mult, ALU.subtract), e)

            def b_part(kind, n, b):
                def link(k, ins):
                    ins.then_inc(b_step, 1)
                    dve.wait_ge(b_step, b * B_STEPS + k)

                if kind == "S":
                    dve.wait_ge(sc_ready, b * 2 * GROUPS + n + 1 + START)
                    nc.vector.tensor_reduce(nm[:, 2 * n:2 * n + 2], sc[n % SC][:, :].rearrange("p (u q) -> p u q", q=NQ),
                                            AX.X, ALU.max, negate=True).then_inc(max_ready, 1)
                elif kind == "P":
                    b2, t, e, k = unit(n)
                    dve.wait_ge(exp_done, b * 4 * GROUPS + 4 * n + 4 + EXP_CREDIT)
                    link(n + 1, nc.vector.reciprocal(rs[:, 4 * n:4 * n + 4], sums[:, 4 * n:4 * n + 4]))
                    if n == 0:
                        dve.wait_ge(v_in, b * 16 + 16)
                    dve.wait_ge(pv_done, b * GROUPS + n - 1 + PV_CREDIT)
                    src = v[:, 2 * b2 + k, t * P:(t + 1) * P].rearrange("p (j e d) -> p e j d", e=2, d=FD)[:, e]
                    nc.vector.tensor_tensor(vsp[:, k, :, FD:2 * FD], src,
                                            bc(rs[:, 4 * n:4 * n + 4].unsqueeze(2), [P, 4, FD]), ALU.mult).then_inc(vs_ready, 1)
                elif kind == "F":
                    dve.wait_ge(nrm_ready, b + 1)
                    base = GROUPS
                    link(base + 1, nc.vector.tensor_scalar(fac[:, 0, :], nrs[:, 0, :], L2_EPS, None, ALU.max))
                    link(base + 2, nc.vector.reciprocal(fac[:, 1, :], fac[:, 0, :]))
                    link(base + 3, nc.vector.tensor_tensor(fac[:, 2, :], nrs[:, 1, :], fac[:, 1, :], ALU.mult))
                    link(base + 4, nc.vector.tensor_scalar(fac[:, 2, :], fac[:, 2, :], L2_EPS, None, ALU.max))
                    link(base + 5, nc.vector.reciprocal(fac[:, 3, :], fac[:, 2, :]))
                    nc.vector.tensor_tensor(fac[:, 4, :], fac[:, 1, :], fac[:, 3, :], ALU.mult).then_inc(fac_ready, 1)
                    dve.wait_ge(gelu_ready, b + 1)
                    dve.wait_ge(x2_in, b * 16 + 16)
                    nc.vector.scalar_tensor_tensor(zb[:].rearrange("p t o -> p (t o)"), zb[:].rearrange("p t o -> p (t o)"),
                                                   w["tg"][:, 1:2], x2[:].rearrange("p t o -> p (t o)"),
                                                   ALU.mult, ALU.add).then_inc(ob_ready, 1)

            dve.wait_ge(init, 3)
            run(dve, a_part, b_part)


def kernel(**inputs):
    import numpy as np
    import concourse.bacc as bacc
    from concourse.bass_utils import run_bass_kernel_spmd

    def turned(name):
        return np.ascontiguousarray(np.asarray(inputs[name]).T)

    def given(name):
        return np.ascontiguousarray(np.asarray(inputs[name]))

    nc = bacc.Bacc("TRN2", target_bir_lowering=False, num_devices=1)
    arrays = {
        "x": given("x"), "ctx_in": given("ctx_1024"), "g_x": given("g_xattn"), "g_f": given("g_ffn"),
        "ln_g": given("L0_xattn_ln_g"), "ln_b": given("L0_xattn_ln_b"),
        "w_in": given("L0_xattn_w_in"), "w_inT": turned("L0_xattn_w_in"),
        "w1T": turned("L0_xattn_wp_w1"), "b1": given("L0_xattn_wp_b1"),
        "wln_g": given("L0_xattn_wp_ln_g"), "wln_b": given("L0_xattn_wp_ln_b"),
        "w2T": turned("L0_xattn_wp_w2"), "b2": given("L0_xattn_wp_b2"),
        "w_outT": turned("L0_xattn_w_out"), "b_out": given("L0_xattn_b_out"),
        "wq": given("L0_ffn_Wq"), "wk": given("L0_ffn_Wk"), "wv": given("L0_ffn_Wv"),
        "wo": given("L0_ffn_Wo"), "woT": turned("L0_ffn_Wo"), "wff": given("L0_ffn_Wff"),
    }
    aps = {name: nc.dram_tensor(f"in_{name}", a.shape, mybir.dt.from_np(a.dtype), kind="ExternalInput").ap()
           for name, a in arrays.items()}
    out = nc.dram_tensor("out_0", (NB, NQ, DIM), F32, kind="ExternalOutput").ap()
    build(nc, out=out, **aps)
    r = run_bass_kernel_spmd(nc, [{f"in_{name}": a for name, a in arrays.items()}], core_ids=[0])
    return r.results[0]["out_0"]
```

```python
import concourse.bass as bass
from concourse import mybir
from contextlib import ExitStack

F32 = mybir.dt.float32
F16 = mybir.dt.float16
ALU = mybir.AluOpType
ACT = mybir.ActivationFunctionType
AX = mybir.AxisListType

P = 128
NB, NQ, DIM = 32, 256, 256
MK = 77
H, DH = 8, 128
FH, FD = 16, 16
KT = DIM // P
HD = H * DH
ROWS = NB * NQ
NT = ROWS // P
NPAIR = NB // 2
PR = 2 * NQ
PT = PR // P
PM = 2 * MK
HM = H * MK
HT = -(-HM // P)
CROWS = NB * MK
CR = 112
CT = CROWS // CR
EPS = 1e-5
L2_EPS = 1e-12
PADW = 2 * 127 + MK

HEAD_PARTS = [(0, 3), (3, 6), (6, 8)]
HM_TILES = [(0, 1), (2, 3), (4,)]
HM_ROWS = [min(P, HM - P * t) for t in range(HT)]


def bc(ap, shape):
    return ap.to_broadcast(shape)


def build(nc, x, ctx_in, g_x, g_f, ln_g, ln_b, w_in, w_inT, w1T, b1, wln_g, wln_b, w2T, b2, w_outT, b_out,
          wq, wk, wv, wo, woT, wff, out):
    kstat = nc.dram_tensor("kstat", (2 * H, CROWS), F32, kind="Internal").ap()
    parts = nc.dram_tensor("parts", (4, DIM, PR), F16, kind="Internal").ap()
    x_rows = x.rearrange("b n d -> (b n) d")
    out_rows = out.rearrange("b n d -> (b n) d")
    c_rows = ctx_in.rearrange("b m d -> (b m) d")

    with ExitStack() as keep:
        def sb(name, shape, dt=F32, where=keep):
            return where.enter_context(nc.sbuf_tensor(name, shape, dt))

        w = {
            "wT": sb("wT", [P, KT, HD]), "wN": sb("wN", [P, H, DIM]), "woutT": sb("woutT", [P, H, DIM]),
            "wq": sb("wq", [P, KT, DIM]), "wk": sb("wk", [P, KT, DIM]), "wv": sb("wv", [P, KT, DIM]),
            "wof": sb("wof", [P, KT, 2 * DIM]), "ident": sb("ident", [P, P]),
            "gcol": sb("gcol", [P, KT]), "bcol": sb("bcol", [P, KT]), "tb": sb("tb", [P, DIM]),
            "tg": sb("tg", [P, 2]), "cvec": sb("cvec", [P, H]), "wwv": sb("wwv", [P, H]),
            "stats": sb("stats", [P, NT, 2]), "zcT": sb("zcT", [P, KT, CROWS]),
            "mhalf": sb("mhalf", [P, PT * H]), "phalf": sb("phalf", [P, H]),
        }
        with ExitStack() as first:
            setup_phase(nc, first, w, locals())
        with ExitStack() as second:
            main_phase(nc, second, w, x_rows, out_rows, kstat, parts)


def setup_phase(nc, ctx, w, a):
    x_rows, c_rows, kstat = a["x_rows"], a["c_rows"], a["kstat"]

    def sb(name, shape, dt=F32):
        return ctx.enter_context(nc.sbuf_tensor(name, shape, dt))

    def ps(name, shape):
        return ctx.enter_context(nc.psum_tensor(name, shape, F32))

    def sem(name):
        return ctx.enter_context(nc.semaphore(name))

    XT = 8
    NX = NT // (2 * XT)
    xin = sb("s_xin", [P, 2, XT, DIM])
    xa = sb("s_xa", [P, 2, XT, DIM + 4])
    xst = sb("s_xst", [P, 2, XT, 6])
    xmv = sb("s_xmv", [P, 2, XT, 2])
    xtmp, ctmp = sb("s_xtmp", [P, 2, XT, 2]), sb("s_ctmp", [CR, 2, 2])
    xrs = sb("s_xrs", [P, 2, XT])
    xvar = sb("s_xvar", [P, 2, XT])
    g_bc, b_bc = sb("s_gbc", [P, DIM]), sb("s_bbc", [P, DIM])
    cin = sb("s_cin", [CR, 2, DIM])
    cz = sb("s_cz", [CR, 2, DIM])
    cT = sb("s_cT", [P, KT, 2 * CR])
    cst, cmv = sb("s_cst", [CR, 2, 6]), sb("s_cmv", [CR, 2, 2])
    cvar, crs = sb("s_cvar", [CR, 2]), sb("s_crs", [CR, 2])
    fst = sb("s_fst", [CR, 2, H, 6])
    ft = sb("s_ft", [CR, 6, 2, H])
    kst = sb("s_kst", [CR, 2, 2, H])
    kstT = sb("s_kstT", [2 * H, 2, CR])
    zeros = sb("s_zeros", [1, DIM + 1])
    ones = sb("s_ones", [P, P])
    offdiag = sb("s_off", [P, P])
    gates = sb("s_gates", [P, 2])
    woT_sb, wff_sb = sb("s_woT", [P, KT, DIM]), sb("s_wff", [P, KT, DIM])
    w1T_sb, w2T_sb = sb("s_w1T", [P, 2, DH]), sb("s_w2T", [DH, 3])
    rows8 = sb("s_rows8", [H, 3, DH])
    b2row = sb("s_b2", [H, 3])
    gram = sb("s_gram", [P, KT, DIM + 1])
    csum = sb("s_csum", [P, KT])
    wmean = sb("s_wmean", [P, KT * H])
    wcT = sb("s_wcT", [P, KT, HD])
    hm = sb("s_hm", [P, KT, HD])
    fc = sb("s_fc", [P, H, DH])
    fcs = sb("s_fcs", [P, H])
    dec = sb("s_dec", [P, H])
    fe = sb("s_fe", [P, 2, H])
    h1, h1s, h1v = sb("s_h1", [H, DH]), sb("s_h1s", [H, 6]), sb("s_h1v", [H, 4])
    h1T = sb("s_h1T", [DH, H])
    lg = sb("s_lg", [H, 8])
    dgw = sb("s_dgw", [H, 3, H])
    mix = sb("s_mix", [P, 3, H])

    gram_ps = [ps(f"s_gram{k}", [P, 512]) for k in range(KT)]
    t_ps = ps("s_tps", [P, KT, 512])
    f_ps = ps("s_fps", [P, 4, 512])

    loaded = sem("s_loaded")
    x_loaded = [sem("s_xl0"), sem("s_xl1")]
    var_ready = [sem("s_vr0"), sem("s_vr1")]
    rstd_ready = [sem("s_rr0"), sem("s_rr1")]
    z_ready = [sem("s_zr0"), sem("s_zr1")]
    scaled = [sem("s_sc0"), sem("s_sc1")]
    xa_ready = [sem("s_xa0"), sem("s_xa1")]
    grammed = [sem("s_gm0"), sem("s_gm1")]
    c_loaded, c_var, c_rstd, cz_ready = sem("s_cl"), sem("s_cvr"), sem("s_crr"), sem("s_czr")
    ct_ps, ct_ready, zc_kept = sem("s_ctp"), sem("s_ctr"), sem("s_zck")
    f_ready, f_used, ksq_ready, rk_ready = sem("s_fr"), sem("s_fu"), sem("s_ksq"), sem("s_rk")
    kst_ready, kT_ps, kT_ready, kT_stored = sem("s_kstr"), sem("s_kTp"), sem("s_kTr"), sem("s_kTs")
    consts, step, turns = sem("s_consts"), sem("s_step"), sem("s_turns")
    pe_step, act_step, pool_step = sem("s_pe"), sem("s_act"), sem("s_pool")
    N_LOADS = 22
    NC2 = CT // 2

    with nc.Block() as block:
        @block.sync
        def _(sp):
            def sp_wait(ready, value):
                sp.wait_ge(ready, value)
                sp.sem_inc(turns, 1)

            def load(dst, src):
                sp.dma_start(dst, src).then_inc(loaded, 16)

            def load_x(half, i):
                sp.dma_start(xin[:, half, :, :], x_rows[bass.ds((i * 2 + half) * (XT * P), XT * P), :]
                             .rearrange("(t p) d -> p t d", p=P)).then_inc(x_loaded[half], 16)

            for waited in (grammed[0], grammed[1], kT_ready, kT_stored):
                sp.sem_inc(waited, START)
            with nc.allow_non_contiguous_dma(reason="columns of a few values"):
                for half in range(2):
                    load_x(half, 0)
                load(w["gcol"][:], a["ln_g"].rearrange("(k p) -> p k", p=P))
                load(w["bcol"][:], a["ln_b"].rearrange("(k p) -> p k", p=P))
                load(g_bc[:], a["ln_g"].partition_broadcast(P))
                load(b_bc[:], a["ln_b"].partition_broadcast(P))
                load(gates[:, 0:1], a["g_x"].partition_broadcast(P))
                load(gates[:, 1:2], a["g_f"].partition_broadcast(P))
                load(w["wT"][:], a["w_inT"].rearrange("(k p) c -> p k c", p=P))
                load(w["wN"][:], a["w_in"].rearrange("(h d) k -> d h k", d=DH))
                load(w["woutT"][:], a["w_outT"].rearrange("(h d) o -> d h o", d=DH))
                load(w["tb"][:], a["b_out"].partition_broadcast(P))
                for name in ("wq", "wk", "wv"):
                    load(w[name][:], a[name].rearrange("(k p) c -> p k c", p=P))
                load(w["wof"][:, :, 0:DIM], a["wo"].rearrange("(k p) c -> p k c", p=P))
                load(woT_sb[:], a["woT"].rearrange("(k p) c -> p k c", p=P))
                load(wff_sb[:], a["wff"].rearrange("(k p) c -> p k c", p=P))
                load(w1T_sb[:], a["w1T"].rearrange("(k p) c -> p k c", p=P))
                load(w2T_sb[:], a["w2T"])
                for j, name in enumerate(("b1", "wln_g", "wln_b")):
                    load(rows8[:, j, :], a[name].partition_broadcast(H))
                load(b2row[:], a["b2"].partition_broadcast(H))
                with sp.Fori(0, NX - 1) as i:
                    for half in range(2):
                        sp_wait(z_ready[half], i + 1)
                        load_x(half, i + 1)

                def load_c(i):
                    sp.dma_start(cin[:], c_rows[bass.ds(i * (2 * CR), 2 * CR), :]
                                 .rearrange("(t p) d -> p t d", p=CR)).then_inc(c_loaded, 16)

                def store_k(i):
                    sp_wait(kT_ready, i + 1 + START)
                    sp.dma_start(kstat[:, bass.ds(i * (2 * CR), 2 * CR)].rearrange("h (t p) -> h t p", p=CR),
                                 kstT[:]).then_inc(kT_stored, 16)

                load_c(0)
                with sp.Fori(0, NC2 - 1) as i:
                    sp_wait(cz_ready, i + 1)
                    load_c(i + 1)
                    store_k(i)
                store_k(NC2 - 1)
                sp.wait_ge(kT_stored, 16 * NC2 + START)

        @block.gpsimd
        def _(pool):
            nc.gpsimd.memset(w["ident"][:], 0.0).then_inc(pool_step, 1)
            nc.gpsimd.memset(offdiag[:], 1.0).then_inc(pool_step, 1)
            nc.gpsimd.memset(w["mhalf"][:], -0.5).then_inc(consts, 1)
            nc.gpsimd.memset(w["phalf"][:], 0.5).then_inc(consts, 1)
            nc.gpsimd.memset(ones[:], 1.0).then_inc(consts, 1)
            nc.gpsimd.memset(zeros[:], 0.0).then_inc(consts, 1)
            nc.gpsimd.memset(xa[:, :, :, DIM:DIM + 4], 1.0).then_inc(consts, 1)
            pool.wait_ge(pool_step, 2)
            nc.gpsimd.affine_select(out=w["ident"][:], in_=w["ident"][:], compare_op=ALU.not_equal, fill=1.0,
                                    base=0, pattern=[[-1, P]], channel_multiplier=1).then_inc(consts, 1)
            nc.gpsimd.affine_select(out=offdiag[:], in_=offdiag[:], compare_op=ALU.not_equal, fill=0.0,
                                    base=0, pattern=[[-1, P]], channel_multiplier=1).then_inc(consts, 1)
            pool.wait_ge(loaded, 16 * N_LOADS)
            pool.wait_ge(consts, 7)
            with pool.Fori(0, NX) as i:
                for half in range(2):
                    pool.wait_ge(var_ready[half], i + 1)
                    nc.gpsimd.tensor_tensor(xrs[:, half, :], xvar[:, half, :], w["mhalf"][:, 0:XT],
                                            ALU.pow).then_inc(rstd_ready[half], 1)
                for half in range(2):
                    pool.wait_ge(z_ready[half], i + 1)
                    nc.gpsimd.tensor_tensor(xa[:, half, :, 0:DIM], xa[:, half, :, 0:DIM],
                                            bc(g_bc[:].unsqueeze(1), [P, XT, DIM]),
                                            ALU.mult).then_inc(scaled[half], 1)
            with pool.Fori(0, NC2) as i:
                pool.wait_ge(c_var, i + 1)
                nc.gpsimd.tensor_tensor(crs[:], cvar[:], w["mhalf"][0:CR, 0:2], ALU.pow).then_inc(c_rstd, 1)
                pool.wait_ge(ksq_ready, i + 1)
                nc.gpsimd.tensor_tensor(kst[:, :, 0, :], ft[:, 0, :, :],
                                        w["mhalf"][0:CR, 0:2 * H].rearrange("p (t h) -> p t h", h=H),
                                        ALU.pow).then_inc(rk_ready, 1)
            pool.wait_ge(step, DVE_TAIL["fcs"])
            nc.gpsimd.tensor_tensor(dec[:], dec[:], w["phalf"][:], ALU.pow).then_inc(pool_step, 1)
            pool.wait_ge(step, DVE_TAIL["h1var"])
            nc.gpsimd.tensor_tensor(h1v[:, 2:3], h1v[:, 1:2], w["mhalf"][0:H, 0:1], ALU.pow).then_inc(pool_step, 1)

        @block.vector
        def _(dve):
            done = [0]

            def link(ins):
                done[0] += 1
                ins.then_inc(step, 1)
                dve.wait_ge(step, done[0])

            base = [0]

            def in_loop(i, per, k, ins):
                ins.then_inc(step, 1)
                dve.wait_ge(step, base[0] + i * per + k)

            X_STEPS = 10
            dve.wait_ge(consts, 7)
            dve.wait_ge(loaded, 16 * N_LOADS)
            with dve.Fori(0, NX) as i:
                for half in range(2):
                    dve.wait_ge(x_loaded[half], i * 16 + 16)
                    for t in range(XT):
                        last = nc.vector.bn_stats(xst[:, half, t, :], xin[:, half, t, :])
                    def x_link(k, ins):
                        in_loop(i, X_STEPS, 5 * half + k, ins)

                    x_link(1, last)
                    row_moments(nc, x_link, 2, xst[:, half], xmv[:, half], xtmp[:, half])
                    nc.vector.tensor_scalar(xvar[:, half, :], xtmp[:, half, :, 1], (1.0 + EPS) / DIM, EPS * EPS,
                                            ALU.mult, ALU.add).then_inc(var_ready[half], 1)
                    x_link(5,
                            nc.vector.tensor_copy(w["stats"][:, bass.ds((i * 2 + half) * XT, XT), 0],
                                                  xmv[:, half, :, 0]))
                for half in range(2):
                    dve.wait_ge(rstd_ready[half], i + 1)
                    dve.wait_ge(grammed[half], i + START)
                    nc.vector.tensor_copy(w["stats"][:, bass.ds((i * 2 + half) * XT, XT), 1], xrs[:, half, :])
                    for t in range(XT):
                        last = nc.vector.tensor_scalar(xa[:, half, t, 0:DIM], xin[:, half, t, :],
                                                       xmv[:, half, t, 0:1], xrs[:, half, t:t + 1],
                                                       ALU.subtract, ALU.mult)
                    last.then_inc(z_ready[half], 1)
                for half in range(2):
                    dve.wait_ge(scaled[half], i + 1)
                    nc.vector.tensor_tensor(xa[:, half, :, 0:DIM], xa[:, half, :, 0:DIM],
                                            bc(b_bc[:].unsqueeze(1), [P, XT, DIM]), ALU.add).then_inc(xa_ready[half], 1)
            base[0] = NX * X_STEPS
            C_STEPS = 14
            with dve.Fori(0, NC2) as i:
                def c_link(k, ins):
                    in_loop(i, C_STEPS, k, ins)

                dve.wait_ge(c_loaded, i * 16 + 16)
                for t in range(2):
                    last = nc.vector.bn_stats(cst[:, t, :], cin[:, t, :])
                c_link(1, last)
                row_moments(nc, c_link, 2, cst[:], cmv, ctmp)
                nc.vector.tensor_scalar(cvar[:], ctmp[:, :, 1], 1.0 / DIM, EPS, ALU.mult, ALU.add).then_inc(c_var, 1)
                dve.wait_ge(c_rstd, i + 1)
                for t in range(2):
                    last = nc.vector.tensor_scalar(cz[:, t, :], cin[:, t, :], cmv[:, t, 0:1], crs[:, t:t + 1],
                                                   ALU.subtract, ALU.mult)
                last.then_inc(cz_ready, 1)
                dve.wait_ge(f_ready, i + 1)
                for t in range(2):
                    for h in range(H):
                        last = nc.vector.bn_stats(fst[:, t, h, :],
                                                  f_ps[0:CR, 2 * t + h // 4, (h % 4) * DH:(h % 4 + 1) * DH])
                c_link(5, last)
                moments(nc, c_link, 6, fst[:], ft)
                dve.sem_inc(ksq_ready, 1)
                c_link(11, ratio_num(nc, ft))
                c_link(12, ratio_den(nc, ft))
                c_link(13, nc.vector.reciprocal(ft[:, 3, :, :], ft[:, 3, :, :]))
                dve.wait_ge(rk_ready, i + 1)
                c_link(14, nc.vector.tensor_tensor(kst[:, :, 1, :], ft[:, 2, :, :], ft[:, 3, :, :], ALU.mult))
                dve.sem_inc(kst_ready, 1)
            done[0] = NX * X_STEPS + NC2 * C_STEPS
            assert done[0] == DVE_LOOPS
            dve.wait_ge(zc_kept, NC2)
            link(nc.vector.tensor_reduce(csum[:], w["zcT"][:], AX.X, ALU.add))
            dve.wait_ge(pe_step, 1)
            for k in range(KT):
                nc.vector.tensor_copy(gram[:, k, :], gram_ps[k][:, 0:DIM + 1])
            link(nc.vector.tensor_reduce(wmean[:], w["wT"][:].rearrange("p k (h d) -> p (k h) d", d=DH), AX.X, ALU.add))
            link(nc.vector.tensor_scalar(wmean[:], wmean[:], -1.0 / DH, None, ALU.mult))
            link(nc.vector.tensor_tensor(wcT[:].rearrange("p k (h d) -> p (k h) d", d=DH),
                                         w["wT"][:].rearrange("p k (h d) -> p (k h) d", d=DH),
                                         bc(wmean[:].unsqueeze(2), [P, KT * H, DH]), ALU.add))
            assert done[0] == DVE_TAIL["wcT"]
            dve.wait_ge(pe_step, 2)
            link(nc.vector.tensor_copy(hm[:].rearrange("p k (c n) -> p (k c) n", n=512), f_ps[:]))
            assert done[0] == DVE_TAIL["hm"]
            dve.wait_ge(pe_step, 3)
            link(nc.vector.tensor_tensor(fc[:].rearrange("p (a h) d -> p a h d", a=2),
                                         f_ps[:, 0:2, :].rearrange("p a (h d) -> p a h d", d=DH),
                                         bc(offdiag[:].unsqueeze(1).unsqueeze(1), [P, 2, 4, DH]), ALU.mult))
            link(nc.vector.tensor_tensor(fc[:], fc[:], fc[:], ALU.mult))
            link(nc.vector.tensor_reduce(fcs[:], fc[:], AX.X, ALU.add))
            assert done[0] == DVE_TAIL["fcsum"]
            nc.vector.tensor_scalar(fe[:, 0, :], t_ps[:, 0, 0:H], 1.0 / ROWS, None, ALU.mult)
            link(nc.vector.tensor_scalar(fe[:, 1, :], t_ps[:, 0, H:2 * H], 1.0 / CROWS, None, ALU.mult))
            assert done[0] == DVE_TAIL["fe"]
            dve.wait_ge(pe_step, 4)
            link(nc.vector.tensor_copy(dec[:], t_ps[:, 1, 0:H]))
            assert done[0] == DVE_TAIL["fcs"]
            dve.wait_ge(pe_step, 5)
            link(nc.vector.tensor_tensor(h1[:], t_ps[0:H, 0, 0:DH], rows8[:, 0, :], ALU.add))
            link(nc.vector.bn_stats(h1s[:], h1[:]))
            link(nc.vector.bn_aggr(h1v[:, 0:2], h1s[:]))
            link(nc.vector.tensor_scalar(h1v[:, 1:2], h1v[:, 1:2], EPS, None, ALU.add))
            assert done[0] == DVE_TAIL["h1var"]
            dve.wait_ge(pool_step, 4)
            link(nc.vector.tensor_scalar(h1[:], h1[:], h1v[:, 0:1], h1v[:, 2:3], ALU.subtract, ALU.mult))
            link(nc.vector.tensor_tensor(h1[:], h1[:], rows8[:, 1, :], ALU.mult))
            link(nc.vector.tensor_tensor(h1[:], h1[:], rows8[:, 2, :], ALU.add))
            link(nc.vector.tensor_scalar(h1[:], h1[:], 0.0, None, ALU.max))
            assert done[0] == DVE_TAIL["h1"]
            dve.wait_ge(pe_step, 6)
            link(nc.vector.tensor_copy(h1T[:], t_ps[:, 1, 0:H]))
            assert done[0] == DVE_TAIL["h1T"]
            dve.wait_ge(pe_step, 7)
            link(nc.vector.tensor_tensor(lg[:, 0:3], t_ps[0:H, 0, 0:3], b2row[:], ALU.add))
            link(nc.vector.tensor_reduce(lg[:, 3:4], lg[:, 0:3], AX.X, ALU.max, negate=True))
            assert done[0] == DVE_TAIL["lmax"]
            dve.wait_ge(act_step, 3)
            link(nc.vector.reciprocal(lg[:, 4:5], lg[:, 4:5]))
            link(nc.vector.tensor_scalar(lg[:, 5:8], lg[:, 5:8], lg[:, 4:5], None, ALU.mult))
            for j in range(3):
                last = nc.vector.tensor_scalar(dgw[:, j, :], w["ident"][0:H, 0:H], lg[:, 5 + j:6 + j], None, ALU.mult)
            link(last)
            assert done[0] == DVE_TAIL["dgw"]
            dve.wait_ge(pe_step, 8)
            link(nc.vector.tensor_copy(mix[:].rearrange("p a h -> p (a h)"), t_ps[:, 1, 0:3 * H]))
            dve.wait_ge(act_step, 2)
            link(nc.vector.tensor_tensor(dec[:], dec[:], mix[:, 1, :], ALU.mult))
            nc.vector.tensor_tensor(w["cvec"][:], dec[:], mix[:, 0, :], ALU.add)
            nc.vector.tensor_copy(w["wwv"][:], mix[:, 2, :])
            dve.wait_ge(act_step, 1)
            nc.vector.tensor_scalar(w["woutT"][:], w["woutT"][:], w["tg"][:, 0:1], None, ALU.mult)
            nc.vector.tensor_scalar(w["tb"][:], w["tb"][:], w["tg"][:, 0:1], None, ALU.mult)
            dve.wait_ge(pe_step, 9)
            for k in range(KT):
                last = nc.vector.tensor_copy(w["wof"][:, k, DIM:2 * DIM], f_ps[:, k, 0:DIM])
            link(last)

        @block.scalar
        def _(act):
            act.wait_ge(loaded, 16 * N_LOADS)
            nc.scalar.activation(w["tg"][:], gates[:], ACT.Tanh).then_inc(act_step, 1)
            with act.Fori(0, NC2) as i:
                act.wait_ge(ct_ps, i + 1)
                for k in range(KT):
                    last = nc.scalar.activation(cT[:, k, :], t_ps[:, k, 0:2 * CR], ACT.Identity,
                                                scale=w["gcol"][:, k:k + 1], bias=w["bcol"][:, k:k + 1])
                last.then_inc(ct_ready, 1)
                for k in range(KT):
                    last = nc.scalar.activation(w["zcT"][:, k, bass.ds(i * (2 * CR), 2 * CR)], t_ps[:, k, 0:2 * CR],
                                                ACT.Identity, scale=w["gcol"][:, k:k + 1], bias=w["bcol"][:, k:k + 1])
                last.then_inc(zc_kept, 1)
                act.wait_ge(kT_ps, i + 1)
                act.wait_ge(kT_stored, i * 16 + START)
                nc.scalar.activation(kstT[:], t_ps[0:2 * H, 0, 0:2 * CR].rearrange("h (t p) -> h t p", p=CR),
                               ACT.Copy).then_inc(kT_ready, 1)
            act.wait_ge(pool_step, 3)
            nc.scalar.activation(dec[:], dec[:], ACT.Exp, scale=-5.0 / (ROWS * DH * DH)).then_inc(act_step, 1)
            act.wait_ge(step, DVE_TAIL["lmax"])
            nc.scalar.activation(lg[:, 5:8], lg[:, 0:3], ACT.Exp, bias=lg[:, 3:4],
                                 accum_out=lg[:, 4:5]).then_inc(act_step, 1)

        @block.tensor
        def _(pe):
            pe.wait_ge(consts, 7)
            pe.wait_ge(loaded, 16 * N_LOADS)
            for k in range(KT):
                nc.tensor.matmul(gram_ps[k][:, 0:DIM + 1], zeros[:, 0:P], zeros[:, :], start=True, stop=False)
            with pe.Fori(0, NX) as i:
                for half in range(2):
                    pe.wait_ge(xa_ready[half], i + 1)
                    for t in range(XT):
                        for k in range(KT):
                            last = nc.tensor.matmul(gram_ps[k][:, 0:DIM + 1], xa[:, half, t, k * P:(k + 1) * P],
                                                    xa[:, half, t, 0:DIM + 1], start=False, stop=False)
                    last.then_inc(grammed[half], 1)
            for k in range(KT):
                last = nc.tensor.matmul(gram_ps[k][:, 0:DIM + 1], zeros[:, 0:P], zeros[:, :], start=False, stop=True)
            last.then_inc(pe_step, 1)
            with pe.Fori(0, NC2) as i:
                pe.wait_ge(cz_ready, i + 1)
                pe.wait_ge(kT_ready, i + START)
                for t in range(2):
                    for k in range(KT):
                        last = nc.tensor.transpose(t_ps[:, k, t * CR:(t + 1) * CR], cz[:, t, k * P:(k + 1) * P],
                                                   w["ident"][0:CR, 0:CR])
                last.then_inc(ct_ps, 1)
                pe.wait_ge(ct_ready, i + 1)
                for t in range(2):
                    for c in range(2):
                        for k in range(KT):
                            last = nc.tensor.matmul(f_ps[0:CR, 2 * t + c, :], cT[:, k, t * CR:(t + 1) * CR],
                                                    w["wT"][:, k, c * 512:(c + 1) * 512],
                                                    start=(k == 0), stop=(k == KT - 1))
                last.then_inc(f_ready, 1)
                pe.wait_ge(kst_ready, i + 1)
                pe.wait_ge(zc_kept, i + 1)
                for t in range(2):
                    last = nc.tensor.transpose(t_ps[0:2 * H, 0, t * CR:(t + 1) * CR],
                                               kst[:, t, :, :].rearrange("p a h -> p (a h)"), w["ident"][0:CR, 0:CR])
                last.then_inc(kT_ps, 1)
            pe.wait_ge(step, DVE_TAIL["wcT"])
            for m in range(KT):
                for c in range(2):
                    for k in range(KT):
                        last = nc.tensor.matmul(f_ps[:, 2 * m + c, :], gram[:, k, m * P:(m + 1) * P],
                                                wcT[:, k, c * 512:(c + 1) * 512], start=(k == 0), stop=(k == KT - 1))
            last.then_inc(pe_step, 1)
            pe.wait_ge(step, DVE_TAIL["hm"])
            pe.wait_ge(kT_ready, NC2 + START)
            for h in range(H):
                for k in range(KT):
                    nc.tensor.matmul(t_ps[:, 0, h:h + 1], w["wT"][:, k, h * DH:(h + 1) * DH],
                                     gram[:, k, DIM:DIM + 1], start=(k == 0), stop=(k == KT - 1))
            for h in range(H):
                for k in range(KT):
                    nc.tensor.matmul(t_ps[:, 0, H + h:H + h + 1], w["wT"][:, k, h * DH:(h + 1) * DH],
                                     csum[:, k:k + 1], start=(k == 0), stop=(k == KT - 1))
            for h in range(H):
                for k in range(KT):
                    last = nc.tensor.matmul(f_ps[:, h // 4, (h % 4) * DH:(h % 4 + 1) * DH],
                                            wcT[:, k, h * DH:(h + 1) * DH], hm[:, k, h * DH:(h + 1) * DH],
                                            start=(k == 0), stop=(k == KT - 1))
            last.then_inc(pe_step, 1)
            pe.wait_ge(step, DVE_TAIL["fcsum"])
            nc.tensor.matmul(t_ps[:, 1, 0:H], ones[:], fcs[:], start=True, stop=True).then_inc(pe_step, 1)
            pe.wait_ge(step, DVE_TAIL["fe"])
            for k in range(2):
                last = nc.tensor.matmul(t_ps[0:H, 0, 0:DH], fe[:, k, :], w1T_sb[:, k, :], start=(k == 0), stop=(k == 1))
            last.then_inc(pe_step, 1)
            pe.wait_ge(step, DVE_TAIL["h1"])
            nc.tensor.transpose(t_ps[:, 1, 0:H], h1[:], w["ident"][0:H, 0:H]).then_inc(pe_step, 1)
            pe.wait_ge(step, DVE_TAIL["h1T"])
            nc.tensor.matmul(t_ps[0:H, 0, 0:3], h1T[:], w2T_sb[:], start=True, stop=True).then_inc(pe_step, 1)
            pe.wait_ge(step, DVE_TAIL["dgw"])
            nc.tensor.matmul(t_ps[:, 1, 0:3 * H], ones[0:H, :], dgw[:].rearrange("p a h -> p (a h)"),
                             start=True, stop=True).then_inc(pe_step, 1)
            for m in range(KT):
                for k in range(KT):
                    last = nc.tensor.matmul(f_ps[:, m, 0:DIM], woT_sb[:, k, m * P:(m + 1) * P], wff_sb[:, k, :],
                                            start=(k == 0), stop=(k == KT - 1))
            last.then_inc(pe_step, 1)


DVE_LOOPS = 4 * 10 + 11 * 14
_TAIL = ["csum", "wsum", "wmean", "wcT", "hm", "fcmask", "fcsq", "fcsum", "fe", "fcs", "h1add", "h1bn", "h1aggr",
         "h1var", "h1norm", "h1g", "h1b", "h1", "h1T", "ladd", "lmax", "lrec", "lscale", "dgw"]
DVE_TAIL = {name: DVE_LOOPS + 1 + n for n, name in enumerate(_TAIL)}


def moments(nc, link, k0, st, ft):
    half = DH // 2
    me, qe, mo, qo = (st[:, :, :, j] for j in (1, 2, 4, 5))
    nc.vector.tensor_tensor(ft[:, 0, :, :], me, mo, ALU.add)
    nc.vector.tensor_tensor(ft[:, 1, :, :], me, mo, ALU.subtract)
    link(k0, nc.vector.tensor_tensor(ft[:, 2, :, :], qe, qo, ALU.add))
    nc.vector.tensor_tensor(ft[:, 3, :, :], ft[:, 1, :, :], ft[:, 1, :, :], ALU.mult)
    link(k0 + 1, nc.vector.tensor_tensor(ft[:, 4, :, :], ft[:, 0, :, :], ft[:, 0, :, :], ALU.mult))
    link(k0 + 2, nc.vector.scalar_tensor_tensor(ft[:, 2, :, :], ft[:, 3, :, :], half / 2.0, ft[:, 2, :, :],
                                                ALU.mult, ALU.add))
    nc.vector.tensor_scalar(ft[:, 1, :, :], ft[:, 2, :, :], 1.0 / (DH - 1), None, ALU.mult)
    link(k0 + 3, nc.vector.scalar_tensor_tensor(ft[:, 0, :, :], ft[:, 4, :, :], DH / 4.0, ft[:, 2, :, :],
                                                ALU.mult, ALU.add))
    link(k0 + 4, nc.vector.tensor_copy(ft[:, 5, :, :], ft[:, 1, :, :]))


def row_moments(nc, link, k0, st, mv, tmp):
    me, qe, mo, qo = (st[:, :, j] for j in (1, 2, 4, 5))
    nc.vector.tensor_tensor(mv[:, :, 0], me, mo, ALU.add)
    nc.vector.tensor_tensor(tmp[:, :, 0], me, mo, ALU.subtract)
    link(k0, nc.vector.tensor_tensor(tmp[:, :, 1], qe, qo, ALU.add))
    nc.vector.tensor_scalar(mv[:, :, 0], mv[:, :, 0], 0.5, None, ALU.mult)
    link(k0 + 1, nc.vector.tensor_tensor(tmp[:, :, 0], tmp[:, :, 0], tmp[:, :, 0], ALU.mult))
    link(k0 + 2, nc.vector.scalar_tensor_tensor(tmp[:, :, 1], tmp[:, :, 0], DIM / 4.0, tmp[:, :, 1], ALU.mult, ALU.add))


def ratio_num(nc, ft):
    return nc.vector.tensor_scalar(ft[:, 2, :, :], ft[:, 1, :, :], 1.0, 2.0, ALU.min, ALU.mult)


def ratio_den(nc, ft):
    return nc.vector.tensor_scalar(ft[:, 3, :, :], ft[:, 1, :, :], 1.0, None, ALU.add)


WORK = 3
GROUPS = 2 * FH * KT // 4
PG = 3
SC = 3
START = 1
PV_CREDIT, OT_CREDIT = GROUPS, 2
EXP_CREDIT = 4 * GROUPS
A_STEPS, B_STEPS = 14, GROUPS + 5

ORDER = """
fk0 z fk0. zT0 zT0. fk1 zT1 fk1. zT1. q0 q0. q1 q2 fk2 S0 fk2. S1 q1. q2. S2 M0 X0 fkd0 M1 q3 fkd1 M2 S3 G0 X1 q4 q3.
S4 X2 M3 S5 G1 G0. R0 P0 M4 X3 M5 R1 X4 X5 G1. S6 M6 q4. q5 X6 S7 P1 fkd2 G2 S8 S9 M7 xb G3 q5. M8 X7 R2 X8 q6 G2. G3.
M9 R3 S10 P2 P3 M10 S11 X9 G4 S12 M11 R4 X10 X11 q6. S13 R5 q7 S14 M12 M13 M14 X12 V0 q7. X13 P4 S15 S16 G4. qs1 M15
P5 V0. G5 V1 G5. X14 M16 X15 V2 R6 R7 S17 V1. X16 V2. M17 V3 X17 P6 S18 V3. qpow S19 d0 M18 S20 d1 X18 M19 S21 R8 E0
P7 d2 qs2 d0. d1. d3 P8 V4 M20 X19 E1 x0 d2. S22 M21 d3. O0 X20 x1 S23 O1 M22 X21 V4. m0 X22 S24 R9 O0. M23 X23 S25 V5
S26 O1. R10 P9 M24 R11 m0. M25 V5. m1 P10 M26 d4 m2 X24 S27 m1. d5 X25 X26 R12 P11 d4. M27 S28 m2. X27 M28 d6 S29 d5.
E2 d6. X28 d7 S30 P12 d7. y0 S31 x2 x3 M29 m3 M30 R13 P13 X29 X30 M31 R14 m4 y0. m3. X31 m4. m5 R15 m5. P14 P15 y1 E3
y1. ln1 O2 O2. O3 lpow O3. ln2 zz0 zz1 F1 zz0. zz1. F2 pq0 pq1 pk0 F3 pq0.h pq1.h pq0.l pk1 pk0.h F4 pq1.l pk0.l pv0
pk1.h pv1 pv1. pk1.l pv0.
""".split()
CHUNKS = [s for s in ORDER if s + "." in ORDER or s + ".l" in ORDER]
HALVES = [s[:-2] for s in ORDER if s.endswith(".h")]
A_INDEX = {name: k for k, name in enumerate(CHUNKS)}
WORK_USES = [len(range(s, len(CHUNKS), WORK)) for s in range(WORK)]


def of_b(step):
    return step[0] in "SMXRPEOF"


def last_use(n, slots, count):
    return n - slots if n >= slots else max(m for m in range(count) if m % slots == n % slots) - count


def unit(group):
    return group // 8, group % 8 // 4, group % 4 // 2, group % 2


def window(t, h):
    return 127 + P * t - MK * h


def tile_heads(t):
    return [h for h in range(H) if MK * h < P * (t + 1) and MK * (h + 1) > P * t]


def main_phase(nc, ctx, w, x_rows, out_rows, kstat, parts):
    def sb(name, shape, dt=F32):
        return ctx.enter_context(nc.sbuf_tensor(name, shape, dt))

    def ps(name, shape):
        return ctx.enter_context(nc.psum_tensor(name, shape, F32))

    def sem(name):
        return ctx.enter_context(nc.semaphore(name))

    xin = sb("xin", [P, PT, DIM])
    z, xT = sb("z", [P, PT, DIM]), sb("xT", [P, KT, PR])
    rkb, krb = sb("rkb", [P, H, PM]), sb("krb", [P, H, PM])
    fvp, kT = sb("fvp", [P, 2, H, PADW]), sb("kT", [P, H, PM])
    G, Vp = sb("G", [P, KT, 2, HM]), sb("Vp", [P, 2, HT, DIM])
    mixed, tmp = sb("mixed", [P, 2, HM]), sb("tmp", [P, HM])
    mT = sb("mT", [P, HT, 2 * P])
    st4, qst, qft = sb("st4", [P, PT, 2]), sb("qst", [P, PT, H, 6]), sb("qft", [P, 6, PT, H])
    rq, sq, wqr = sb("rq", [P, PT, H]), sb("sq", [P, PT, H]), sb("wqr", [P, PT, H])
    x2S, l2s, l2m = sb("x2S", [P, PT, DIM]), sb("l2s", [P, PT, 6]), sb("l2m", [P, PT, 2])
    l2t = sb("l2t", [P, PT, 2])
    l2v, l2r = sb("l2v", [P, PT]), sb("l2r", [P, PT])
    zzT = sb("zzT", [P, KT, PR])
    hi = {a: sb(a + "h", [P, 2, PR], F16) for a in "qk"}
    lo = {a: sb(a + "l", [P, 2, PR], F16) for a in "qk"}
    vS, v = sb("vS", [P, PT, DIM]), sb("v", [P, PT, DIM])
    stack = {a: sb(a + "stack", [P, FH // 2, PR], F16) for a in "qk"}
    x2 = sb("x2", [P, PT, DIM])
    prob, vsp = sb("prob", [P, PG * 4, NQ]), sb("vsp", [P, KT, 4, 3 * FD])
    nm, sums, rs = sb("nm", [P, 4 * GROUPS]), sb("sums", [P, 4 * GROUPS]), sb("rs", [P, 4 * GROUPS])
    oT, zb, junk = sb("oT", [P, 2, PR]), sb("zb", [P, PT, DIM]), sb("junk", [P, 2, DIM], mybir.dt.bfloat16)
    nrm, nrs, fac = sb("nrm", [P, 2, PT]), sb("nrs", [P, 2, PT]), sb("fac", [P, 5, PT])

    work = [ps(f"work{s}", [P, 512]) for s in range(WORK)]
    sc = [ps(f"score{s}", [P, 512]) for s in range(SC)]
    pvb = [ps(f"attended{s}", [P, 512]) for s in range(2)]

    filled, drained = [sem(f"filled{s}") for s in range(WORK)], [sem(f"drained{s}") for s in range(WORK)]
    init, x_ready, rk_in, kr_in = sem("init"), sem("x_ready"), sem("rk_in"), sem("kr_in")
    z_ready, xb_ready, kT_ready = sem("z_ready"), sem("xb_ready"), sem("kT_ready")
    qsq_ready, rq_ready, wqr_ready, mixed_ready = sem("qsq"), sem("rq_ready"), sem("wqr_ready"), sem("mixed_ready")
    v2_ready, r2_ready, zz_ready, hi_ready = sem("v2_ready"), sem("r2_ready"), sem("zz_ready"), sem("hi_ready")
    parts_stored, stack_in, v_in, x2_in = sem("parts_stored"), sem("stack_in"), sem("v_in"), sem("x2_in")
    sc_ready, max_ready, exp_done = sem("sc_ready"), sem("max_ready"), sem("exp_done")
    vs_ready, pv_done, ot_done = sem("vs_ready"), sem("pv_done"), sem("ot_done")
    nrm_ready, fac_ready = sem("nrm_ready"), sem("fac_ready")
    gelu_ready, ob_ready, stored = sem("gelu_ready"), sem("ob_ready"), sem("stored")
    a_step, b_step, tmp_ready, turns = sem("a_step"), sem("b_step"), sem("tmp_ready"), sem("turns")

    def bank(name):
        return work[A_INDEX[name] % WORK]

    def uses(name, turn):
        k = A_INDEX[name]
        return turn * WORK_USES[k % WORK] + k // WORK

    def latest(names):
        last = {}
        for name in sorted(names, key=A_INDEX.get):
            last[A_INDEX[name] % WORK] = name
        return last.items()

    def wait_filled(eng, turn, *names):
        for s, name in latest(names):
            eng.wait_ge(filled[s], uses(name, turn) + 1)

    def wait_drained(eng, turn, *names):
        for s, name in latest(names):
            eng.wait_ge(drained[s], uses(name, turn) + 1)

    def wait_free(eng, name, turn):
        eng.wait_ge(drained[A_INDEX[name] % WORK], uses(name, turn))

    def fill(ins, name):
        ins.then_inc(filled[A_INDEX[name] % WORK], 1)

    def drain(ins, name):
        ins.then_inc(drained[A_INDEX[name] % WORK], 1)

    def key_rows(ap):
        return ap.rearrange("p h (b m) -> p h b m", m=MK)

    def run(eng, a_part, b_part, passed=None):
        for s in ORDER:
            if not of_b(s):
                a_part(s, 0)
            elif passed and s in A_INDEX:
                passed(s, 0)
        with eng.Fori(0, NPAIR - 1) as i:
            for s in ORDER:
                if of_b(s):
                    b_part(s, i)
                else:
                    a_part(s, i + 1)
        for s in ORDER:
            if of_b(s):
                b_part(s, NPAIR - 1)
            elif passed and s in A_INDEX:
                passed(s, NPAIR)

    with nc.Block() as block:
        @block.sync
        def _(sp):
            for waited in (stack_in, ob_ready, vs_ready, sc_ready, stored):
                sp.sem_inc(waited, START)
            sp.sem_inc(exp_done, EXP_CREDIT)
            sp.sem_inc(pv_done, PV_CREDIT)
            sp.sem_inc(ot_done, OT_CREDIT)

            def sp_wait(ready, value):
                sp.wait_ge(ready, value)
                sp.sem_inc(turns, 1)

            def sp_wait_drained(turn, *names):
                for s, name in latest(names):
                    sp_wait(drained[s], uses(name, turn) + 1)

            def load(a, first=False):
                if not first:
                    sp_wait_drained(a - 1, "y0", "y1")
                sp.dma_start(xin[:], x_rows[bass.ds(a * PR, PR), :].rearrange("(t p) d -> p t d", p=P)).then_inc(x_ready, 16)
                sp_wait(kT_ready, a * 3)
                sp.dma_start(rkb[:], kstat[0:H, bass.ds(a * PM, PM)].partition_broadcast(P)).then_inc(rk_in, 16)
                sp_wait(mixed_ready, a * PT)
                sp.dma_start(krb[:], kstat[H:2 * H, bass.ds(a * PM, PM)].partition_broadcast(P)).then_inc(kr_in, 16)

            def move(i):
                sp_wait_drained(i, "pq0", "pq1", "pk0", "pk1")
                sp_wait(stack_in, i * 256 + START)
                for n, t in enumerate((hi["q"], lo["q"], hi["k"], lo["k"])):
                    sp.dma_start(parts[n].rearrange("(t p) n -> p t n", p=P), t[:]).then_inc(parts_stored, 16)
                sp_wait(parts_stored, i * 64 + 64)
                sp_wait(sc_ready, i * 2 * GROUPS + START)
                for c in range(4):
                    for e in range(2):
                        for a, n in (("k", 2 + c // 2), ("q", c % 2)):
                            src = parts[n].rearrange("(q e d) n -> e d q n", e=2, d=FD)[e]
                            sp.dma_start(stack[a][64 * e + FD * c:64 * e + FD * (c + 1), :, :], src).then_inc(stack_in, 16)
                sp_wait_drained(i, "pv0", "pv1")
                sp_wait(vs_ready, i * GROUPS + START)
                sp.dma_start(v[:], vS[:]).then_inc(v_in, 16)
                sp_wait_drained(i, "y0", "y1")
                sp_wait(ob_ready, i + START)
                sp.dma_start(x2[:], x2S[:]).then_inc(x2_in, 16)

            def store(i):
                sp_wait(ob_ready, i + 1 + START)
                sp.dma_start(out_rows[bass.ds(i * PR, PR), :].rearrange("(t p) d -> p t d", p=P), zb[:]).then_inc(stored, 16)

            load(0, first=True)
            load(1)
            move(0)
            with sp.Fori(0, NPAIR - 2) as i:
                load(i + 2)
                move(i + 1)
                store(i)
            move(NPAIR - 1)
            store(NPAIR - 2)
            store(NPAIR - 1)
            sp.wait_ge(stored, 16 * NPAIR + START)

        @block.tensor
        def _(pe):
            ident = w["ident"]

            def a_part(e, a):
                if e not in A_INDEX:
                    return
                kind, c = e[:-1], int(e[-1])
                bk = bank(e)
                wait_free(pe, e, a)
                if kind in ("zT", "zz"):
                    src = z
                    pe.wait_ge(z_ready if kind == "zT" else zz_ready, a + 1)
                    for t in range(PT):
                        last = nc.tensor.transpose(bk[:, t * P:(t + 1) * P], src[:, t, c * P:(c + 1) * P], ident[:])
                elif kind == "fk":
                    lo_h, hi_h = HEAD_PARTS[c]
                    for h in range(lo_h, hi_h):
                        for k in range(KT):
                            last = nc.tensor.matmul(bk[:, (h - lo_h) * PM:(h - lo_h + 1) * PM],
                                                    w["wT"][:, k, h * DH:(h + 1) * DH],
                                                    w["zcT"][:, k, bass.ds(a * PM, PM)], start=(k == 0), stop=(k == KT - 1))
                elif kind == "q":
                    if c == 0:
                        wait_drained(pe, a, "zT0", "zT1")
                    t, half = c // 2, c % 2
                    for k in range(KT):
                        last = nc.tensor.matmul(bk[:, :], xT[:, k, t * P:(t + 1) * P],
                                                w["wT"][:, k, half * 512:(half + 1) * 512], start=(k == 0), stop=(k == KT - 1))
                elif kind == "G":
                    k, (lo_h, hi_h) = c // 3, HEAD_PARTS[c % 3]
                    pe.wait_ge(kT_ready, a * 3 + c % 3 + 1)
                    for h in range(lo_h, hi_h):
                        last = nc.tensor.matmul(bk[:, (h - lo_h) * PM:(h - lo_h + 1) * PM], w["wN"][:, h, k * P:(k + 1) * P],
                                                kT[:, h, :], start=True, stop=True)
                elif kind == "V":
                    b2, tiles = c // 3, HM_TILES[c % 3]
                    if c == 0:
                        wait_drained(pe, a, "fk0", "fk1", "fk2")
                    for n, t in enumerate(tiles):
                        heads = tile_heads(t)
                        for h in heads:
                            last = nc.tensor.matmul(bk[:, n * DIM:(n + 1) * DIM], fvp[:, b2, h, window(t, h):window(t, h) + P],
                                                    w["woutT"][:, h, :], start=(h == heads[0]), stop=(h == heads[-1]))
                elif kind == "d":
                    t, half = c // 2, c % 2
                    if c == 0:
                        wait_drained(pe, a, *(f"G{g}" for g in range(6)))
                    for k in range(KT):
                        last = nc.tensor.matmul(bk[:, 0:HM // 2], xT[:, k, t * P:(t + 1) * P],
                                                G[:, k, t // 2, half * (HM // 2):(half + 1) * (HM // 2)],
                                                start=(k == 0), stop=(k == KT - 1))
                elif kind == "m":
                    b2, tiles = c // 3, HM_TILES[c % 3]
                    pe.wait_ge(mixed_ready, a * PT + 2 * b2 + 2)
                    for n, t in enumerate(tiles):
                        for r in range(2):
                            last = nc.tensor.transpose(bk[0:HM_ROWS[t], (2 * n + r) * P:(2 * n + r + 1) * P],
                                                       mixed[:, r, t * P:t * P + HM_ROWS[t]], ident[:])
                elif kind == "y":
                    wait_drained(pe, a, *(f"{kind}{n}" for kind in "mV" for n in range(3 * c, 3 * c + 3)))
                    for r in range(2):
                        for t in range(HT):
                            last = nc.tensor.matmul(bk[:, r * DIM:(r + 1) * DIM], mT[0:HM_ROWS[t], t, r * P:(r + 1) * P],
                                                    Vp[0:HM_ROWS[t], c, t, :], start=(t == 0), stop=(t == HT - 1))
                elif kind in ("pq", "pk"):
                    if e == "pq0":
                        wait_drained(pe, a, "zz0", "zz1")
                    for k in range(KT):
                        last = nc.tensor.matmul(bk[:, :], w["w" + kind[1]][:, k, c * P:(c + 1) * P], zzT[:, k, :],
                                                start=(k == 0), stop=(k == KT - 1))
                elif kind == "pv":
                    for r in range(2):
                        for k in range(KT):
                            last = nc.tensor.matmul(bk[:, r * DIM:(r + 1) * DIM], zzT[:, k, (2 * c + r) * P:(2 * c + r + 1) * P],
                                                    w["wv"][:, k, :], start=(k == 0), stop=(k == KT - 1))
                fill(last, e)

            def b_part(step, b):
                kind, n = step[0], int(step[1:].rstrip("."))
                if step.endswith("."):
                    return
                if kind == "S":
                    b2, t, e, k = unit(n // 2)
                    if n == 0:
                        pe.wait_ge(stack_in, b * 256 + 256 + START)
                    pe.wait_ge(exp_done, b * 4 * GROUPS + 2 * last_use(n, SC, 2 * GROUPS) + 2 + EXP_CREDIT)
                    for jj in range(2):
                        j = 4 * t + 2 * (n % 2) + jj
                        last = nc.tensor.matmul(sc[n % SC][:, jj * NQ:(jj + 1) * NQ],
                                                stack["k"][64 * e:64 * e + 64, j, b2 * NQ + k * P:b2 * NQ + (k + 1) * P],
                                                stack["q"][64 * e:64 * e + 64, j, b2 * NQ:(b2 + 1) * NQ],
                                                start=True, stop=True)
                    last.then_inc(sc_ready, 1)
                elif kind == "P":
                    b2, t, e, k = unit(n)
                    pe.wait_ge(vs_ready, b * GROUPS + n + 1 + START)
                    if n % 4 == 0:
                        pe.wait_ge(ot_done, b * 4 + n // 4 + 1)
                    lo_c = FD * (1 - e)
                    for j in range(4):
                        last = nc.tensor.matmul(pvb[t][32 * j:32 * j + 32, 0:NQ], vsp[:, k, j, lo_c:lo_c + 2 * FD],
                                                prob[:, (n % PG) * 4 + j, :], start=(n % 4 == 0), stop=(n % 4 == 3))
                    last.then_inc(pv_done, 1)
                elif kind == "O":
                    wait_free(pe, step, b + 1)
                    pe.wait_ge(ot_done, b * 4 + 2 * (n // 2) + 2 + OT_CREDIT)
                    for k in range(2):
                        last = nc.tensor.matmul(bank(step)[:, :], oT[:, k, n * P:(n + 1) * P], w["wof"][:, k, :],
                                                start=(k == 0), stop=(k == 1))
                    fill(last, step)

            def passed(step, turn):
                wait_free(pe, step, turn)
                pe.sem_inc(filled[A_INDEX[step] % WORK], 1)
                pe.sem_inc(drained[A_INDEX[step] % WORK], 1)

            pe.wait_ge(init, 3)
            run(pe, a_part, b_part, passed)

        @block.scalar
        def _(act):
            act.wait_ge(init, 3)

            def a_part(e, a):
                if e.endswith(".l") or "." not in e or e[0] in "dy" or e[:-2] == "q":
                    return
                e = e.split(".")[0]
                kind, c, bk = e[:-1], int(e[-1]), bank(e)
                if e == "m3":
                    wait_filled(act, a, "m3", "y0")
                else:
                    wait_filled(act, a, e)
                if kind == "zT":
                    ins = nc.scalar.activation(xT[:, c, :], bk[:, :], ACT.Identity,
                                               scale=w["gcol"][:, c:c + 1], bias=w["bcol"][:, c:c + 1])
                elif kind == "fk":
                    lo_h, hi_h = HEAD_PARTS[c]
                    ins = nc.scalar.activation(fvp[:, :, lo_h:hi_h, 127:127 + MK].rearrange("p b h m -> p h b m"),
                                               bk[:, 0:(hi_h - lo_h) * PM].rearrange("p (h b m) -> p h b m", b=2, m=MK),
                                               ACT.Copy)
                elif kind == "G":
                    lo_h, hi_h = HEAD_PARTS[c % 3]
                    dst = G[:, c // 3, :, lo_h * MK:hi_h * MK].rearrange("p b (h m) -> p h b m", m=MK)
                    ins = nc.scalar.activation(dst, bk[:, 0:(hi_h - lo_h) * PM].rearrange("p (h b m) -> p h b m", b=2, m=MK),
                                               ACT.Copy)
                elif kind == "V":
                    tiles = HM_TILES[c % 3]
                    ins = nc.scalar.activation(Vp[:, c // 3, tiles[0]:tiles[-1] + 1, :],
                                               bk[:, 0:len(tiles) * DIM].rearrange("p (t o) -> p t o", o=DIM), ACT.Copy)
                elif kind == "m":
                    tiles = HM_TILES[c % 3]
                    r = HM_ROWS[tiles[0]]
                    ins = nc.scalar.activation(mT[0:r, tiles[0]:tiles[-1] + 1, :],
                                               bk[0:r, 0:len(tiles) * 2 * P].rearrange("p (t n) -> p t n", n=2 * P), ACT.Copy)
                elif kind == "zz":
                    ins = nc.scalar.activation(zzT[:, c, :], bk[:, :], ACT.Copy)
                elif kind in ("pq", "pk"):
                    act.wait_ge(parts_stored, a * 64)
                    nc.scalar.activation(hi[kind[1]][:, c, :], bk[:, :], ACT.Copy,
                                         scale=1.0 / 16 if kind == "pq" else 1.0).then_inc(hi_ready, 1)
                    return
                elif kind == "pv":
                    act.wait_ge(v_in, a * 16)
                    ins = nc.scalar.activation(vS[:, 2 * c:2 * c + 2, :], bk[:, :].rearrange("p (t o) -> p t o", o=DIM), ACT.Copy)
                drain(ins, e)

            def b_part(step, b):
                kind, n = step[0], int(step[1:].rstrip("."))
                if kind == "X":
                    g = n // 2
                    act.wait_ge(max_ready, b * 2 * GROUPS + n + 1)
                    if n % 2 == 0:
                        act.wait_ge(pv_done, b * GROUPS + last_use(g, PG, GROUPS) + 1 + PV_CREDIT)
                    for jj in range(2):
                        u = 2 * n + jj
                        nc.scalar.activation(prob[:, (g % PG) * 4 + u % 4, :], sc[n % SC][:, jj * NQ:(jj + 1) * NQ], ACT.Exp,
                                             bias=nm[:, u:u + 1], accum_out=sums[:, u:u + 1]).then_inc(exp_done, 1)
                elif kind == "E":
                    act.wait_ge(pv_done, b * GROUPS + 4 * n + 4 + PV_CREDIT)
                    wait_filled(act, b, f"O{n // 2 * 2 + 1}")
                    nc.scalar.activation(oT[:, n % 2, (n // 2) * NQ:(n // 2 + 1) * NQ], pvb[n % 2][:, 0:NQ],
                                         ACT.Copy).then_inc(ot_done, 1)
                elif kind == "O" and step.endswith("."):
                    bk = bank(step[:-1])
                    wait_filled(act, b + 1, step[:-1])
                    if n == 0:
                        act.wait_ge(stored, b * 16 + START)
                    else:
                        wait_drained(act, b + 1, f"O{n - 1}")
                    for j in range(2):
                        nc.scalar.activation(junk[:, j, :], bk[:, j * DIM:(j + 1) * DIM], ACT.Square, accum_out=nrm[:, j, n:n + 1])
                    drain(nc.scalar.activation(zb[:, n, :], bk[:, DIM:2 * DIM], ACT.Copy), step[:-1])
                elif step == "F3":
                    act.wait_ge(fac_ready, b + 1)
                    for t in range(PT):
                        last = nc.scalar.activation(zb[:, t, :], zb[:, t, :], ACT.Gelu, scale=fac[:, 4, t:t + 1])
                    last.then_inc(gelu_ready, 1)

            run(act, a_part, b_part)

        @block.gpsimd
        def _(pool):
            def a_part(e, a):
                if e == "xb":
                    pool.wait_ge(z_ready, a + 1)
                    nc.gpsimd.tensor_tensor(xin[:], xin[:], bc(w["tb"][:].unsqueeze(1), [P, PT, DIM]),
                                            ALU.add).then_inc(xb_ready, 1)
                elif e == "qpow":
                    pool.wait_ge(qsq_ready, a + 1)
                    nc.gpsimd.tensor_tensor(rq[:], qft[:, 0, :, :], w["mhalf"][:].rearrange("p (t h) -> p t h", h=H),
                                            ALU.pow).then_inc(rq_ready, 1)
                elif e[0] == "x":
                    t = int(e[1])
                    pool.wait_ge(kr_in, a * 16 + 16)
                    pool.wait_ge(wqr_ready, a + 1)
                    pool.wait_ge(mixed_ready, a * PT + t)
                    nc.gpsimd.tensor_tensor(tmp[:].rearrange("p (h m) -> p h m", m=MK),
                                            krb[:, :, (t // 2) * MK:(t // 2 + 1) * MK],
                                            bc(wqr[:, t, :].unsqueeze(2), [P, H, MK]), ALU.mult).then_inc(tmp_ready, 1)
                    pool.wait_ge(tmp_ready, a * PT + t + 1)
                    wait_drained(pool, a, f"d{2 * t}", f"d{2 * t + 1}")
                    nc.gpsimd.tensor_tensor(mixed[:, t % 2, :], mixed[:, t % 2, :], tmp[:], ALU.add).then_inc(mixed_ready, 1)
                elif e == "lpow":
                    pool.wait_ge(v2_ready, a + 1)
                    nc.gpsimd.tensor_tensor(l2r[:], l2v[:], w["mhalf"][:, 0:PT], ALU.pow).then_inc(r2_ready, 1)

            def b_part(step, b):
                if step == "F1":
                    wait_drained(pool, b + 1, *(f"O{n}" for n in range(PT)))
                    nc.gpsimd.tensor_tensor(nrs[:].rearrange("p j t -> p (j t)"), nrm[:].rearrange("p j t -> p (j t)"),
                                            w["phalf"][:, 0:2 * PT], ALU.pow).then_inc(nrm_ready, 1)

            run(pool, a_part, b_part)

        @block.vector
        def _(dve):
            nc.vector.memset(vsp[:], 0.0).then_inc(init, 1)
            nc.vector.memset(fvp[:, 0, :, :], 0.0).then_inc(init, 1)
            nc.vector.memset(fvp[:, 1, :, :], 0.0).then_inc(init, 1)

            def a_part(e, a):
                def link(k, ins):
                    ins.then_inc(a_step, 1)
                    dve.wait_ge(a_step, a * A_STEPS + k)

                full, e = e, e.split(".")[0]
                kind, c = e[:-1], e[-1]
                if e in A_INDEX and (full == e or full.endswith(".h")):
                    return
                if e == "z":
                    dve.wait_ge(x_ready, a * 16 + 16)
                    link(1, nc.vector.tensor_copy(st4[:], w["stats"][:, bass.ds(a * PT, PT), :]))
                    for t in range(PT):
                        last = nc.vector.tensor_scalar(z[:, t, :], xin[:, t, :], st4[:, t, 0:1], st4[:, t, 1:2],
                                                       ALU.subtract, ALU.mult)
                    last.then_inc(z_ready, 1)
                elif kind == "fkd":
                    lo_h, hi_h = HEAD_PARTS[int(c)]
                    wait_drained(dve, a, "fk" + c)
                    dve.wait_ge(rk_in, a * 16 + 16)
                    nc.vector.tensor_tensor(key_rows(kT[:, lo_h:hi_h, :]),
                                            fvp[:, :, lo_h:hi_h, 127:127 + MK].rearrange("p b h m -> p h b m"),
                                            key_rows(rkb[:, lo_h:hi_h, :]), ALU.mult).then_inc(kT_ready, 1)
                elif kind == "q":
                    t, half = int(c) // 2, int(c) % 2
                    wait_filled(dve, a, e)
                    for h in range(4):
                        last = nc.vector.bn_stats(qst[:, t, 4 * half + h, :], bank(e)[:, h * DH:(h + 1) * DH])
                    drain(last, e)
                elif e == "qs1":
                    wait_drained(dve, a, *(f"q{n}" for n in range(2 * PT)))
                    moments(nc, link, 2, qst[:], qft)
                    dve.sem_inc(qsq_ready, 1)
                    ratio_num(nc, qft)
                    link(7, ratio_den(nc, qft))
                    link(8, nc.vector.reciprocal(qft[:, 3, :, :], qft[:, 3, :, :]))
                    link(9, nc.vector.tensor_tensor(qft[:, 2, :, :], qft[:, 2, :, :], qft[:, 3, :, :], ALU.mult))
                    nc.vector.tensor_tensor(wqr[:], qft[:, 2, :, :], bc(w["wwv"][:].unsqueeze(1), [P, PT, H]),
                                            ALU.mult).then_inc(wqr_ready, 1)
                elif e == "qs2":
                    dve.wait_ge(rq_ready, a + 1)
                    link(10, nc.vector.tensor_tensor(sq[:], rq[:], bc(w["cvec"][:].unsqueeze(1), [P, PT, H]), ALU.mult))
                elif kind == "d":
                    t, half = int(c) // 2, int(c) % 2
                    if t >= 2:
                        wait_filled(dve, a, e, "m0", "m1", "m2")
                    else:
                        wait_filled(dve, a, e)
                    drain(nc.vector.tensor_tensor(
                        mixed[:, t % 2, half * (HM // 2):(half + 1) * (HM // 2)].rearrange("p (h m) -> p h m", m=MK),
                        bank(e)[:, 0:HM // 2].rearrange("p (h m) -> p h m", m=MK),
                        bc(sq[:, t, 4 * half:4 * half + 4].unsqueeze(2), [P, 4, MK]), ALU.mult), e)
                elif kind == "y":
                    c = int(c)
                    wait_filled(dve, a, e)
                    dve.wait_ge(xb_ready, a + 1)
                    dve.wait_ge(x2_in, a * 16)
                    drain(nc.vector.tensor_tensor(x2S[:, 2 * c:2 * c + 2, :], bank(e)[:, :].rearrange("p (t o) -> p t o", o=DIM),
                                                  xin[:, 2 * c:2 * c + 2, :], ALU.add), e)
                elif e == "ln1":
                    wait_drained(dve, a, "y0", "y1")
                    for t in range(PT):
                        last = nc.vector.bn_stats(l2s[:, t, :], x2S[:, t, :])
                    link(11, last)
                    row_moments(nc, link, 12, l2s, l2m, l2t)
                    nc.vector.tensor_scalar(l2v[:], l2t[:, :, 1], 1.0 / DIM, EPS, ALU.mult, ALU.add).then_inc(v2_ready, 1)
                elif e == "ln2":
                    dve.wait_ge(r2_ready, a + 1)
                    for t in range(PT):
                        last = nc.vector.tensor_scalar(z[:, t, :], x2S[:, t, :], l2m[:, t, 0:1], l2r[:, t:t + 1],
                                                       ALU.subtract, ALU.mult)
                    last.then_inc(zz_ready, 1)
                elif kind in ("pq", "pk"):
                    n = HALVES.index(e)
                    dve.wait_ge(hi_ready, a * 4 + n + 1)
                    drain(nc.vector.scalar_tensor_tensor(lo[kind[1]][:, int(c), :], bank(e)[:, :],
                                                         1.0 / 16 if kind == "pq" else 1.0, hi[kind[1]][:, int(c), :],
                                                         ALU.mult, ALU.subtract), e)

            def b_part(step, b):
                kind, n = step[0], int(step[1:].rstrip("."))

                def link(k, ins):
                    ins.then_inc(b_step, 1)
                    dve.wait_ge(b_step, b * B_STEPS + k)

                if kind == "M":
                    dve.wait_ge(sc_ready, b * 2 * GROUPS + n + 1 + START)
                    nc.vector.tensor_reduce(nm[:, 2 * n:2 * n + 2], sc[n % SC][:, :].rearrange("p (u q) -> p u q", q=NQ),
                                            AX.X, ALU.max, negate=True).then_inc(max_ready, 1)
                elif kind == "R":
                    b2, t, e, k = unit(n)
                    dve.wait_ge(exp_done, b * 4 * GROUPS + 4 * n + 4 + EXP_CREDIT)
                    link(n + 1, nc.vector.reciprocal(rs[:, 4 * n:4 * n + 4], sums[:, 4 * n:4 * n + 4]))
                    if n == 0:
                        dve.wait_ge(v_in, b * 16 + 16)
                    dve.wait_ge(pv_done, b * GROUPS + n - 1 + PV_CREDIT)
                    src = v[:, 2 * b2 + k, t * P:(t + 1) * P].rearrange("p (j e d) -> p e j d", e=2, d=FD)[:, e]
                    nc.vector.tensor_tensor(vsp[:, k, :, FD:2 * FD], src,
                                            bc(rs[:, 4 * n:4 * n + 4].unsqueeze(2), [P, 4, FD]), ALU.mult).then_inc(vs_ready, 1)
                elif step == "F2":
                    dve.wait_ge(nrm_ready, b + 1)
                    base = GROUPS
                    link(base + 1, nc.vector.tensor_scalar(fac[:, 0, :], nrs[:, 0, :], L2_EPS, None, ALU.max))
                    link(base + 2, nc.vector.reciprocal(fac[:, 1, :], fac[:, 0, :]))
                    link(base + 3, nc.vector.tensor_tensor(fac[:, 2, :], nrs[:, 1, :], fac[:, 1, :], ALU.mult))
                    link(base + 4, nc.vector.tensor_scalar(fac[:, 2, :], fac[:, 2, :], L2_EPS, None, ALU.max))
                    link(base + 5, nc.vector.reciprocal(fac[:, 3, :], fac[:, 2, :]))
                    nc.vector.tensor_tensor(fac[:, 4, :], fac[:, 1, :], fac[:, 3, :], ALU.mult).then_inc(fac_ready, 1)
                elif step == "F4":
                    dve.wait_ge(gelu_ready, b + 1)
                    dve.wait_ge(x2_in, b * 16 + 16)
                    nc.vector.scalar_tensor_tensor(zb[:].rearrange("p t o -> p (t o)"), zb[:].rearrange("p t o -> p (t o)"),
                                                   w["tg"][:, 1:2], x2[:].rearrange("p t o -> p (t o)"),
                                                   ALU.mult, ALU.add).then_inc(ob_ready, 1)

            dve.wait_ge(init, 3)
            run(dve, a_part, b_part)


def kernel(**inputs):
    import numpy as np
    import concourse.bacc as bacc
    from concourse.bass_utils import run_bass_kernel_spmd

    def turned(name):
        return np.ascontiguousarray(np.asarray(inputs[name]).T)

    def given(name):
        return np.ascontiguousarray(np.asarray(inputs[name]))

    nc = bacc.Bacc("TRN2", target_bir_lowering=False, num_devices=1)
    arrays = {
        "x": given("x"), "ctx_in": given("ctx_1024"), "g_x": given("g_xattn"), "g_f": given("g_ffn"),
        "ln_g": given("L0_xattn_ln_g"), "ln_b": given("L0_xattn_ln_b"),
        "w_in": given("L0_xattn_w_in"), "w_inT": turned("L0_xattn_w_in"),
        "w1T": turned("L0_xattn_wp_w1"), "b1": given("L0_xattn_wp_b1"),
        "wln_g": given("L0_xattn_wp_ln_g"), "wln_b": given("L0_xattn_wp_ln_b"),
        "w2T": turned("L0_xattn_wp_w2"), "b2": given("L0_xattn_wp_b2"),
        "w_outT": turned("L0_xattn_w_out"), "b_out": given("L0_xattn_b_out"),
        "wq": given("L0_ffn_Wq"), "wk": given("L0_ffn_Wk"), "wv": given("L0_ffn_Wv"),
        "wo": given("L0_ffn_Wo"), "woT": turned("L0_ffn_Wo"), "wff": given("L0_ffn_Wff"),
    }
    aps = {name: nc.dram_tensor(f"in_{name}", a.shape, mybir.dt.from_np(a.dtype), kind="ExternalInput").ap()
           for name, a in arrays.items()}
    out = nc.dram_tensor("out_0", (NB, NQ, DIM), F32, kind="ExternalOutput").ap()
    build(nc, out=out, **aps)
    r = run_bass_kernel_spmd(nc, [{f"in_{name}": a for name, a in arrays.items()}], core_ids=[0])
    return r.results[0]["out_0"]
```

```python
import concourse.bass as bass
from concourse import mybir
from contextlib import ExitStack

F32 = mybir.dt.float32
F16 = mybir.dt.float16
ALU = mybir.AluOpType
ACT = mybir.ActivationFunctionType
AX = mybir.AxisListType

P = 128
NB, NQ, DIM = 32, 256, 256
MK = 77
H, DH = 8, 128
FH, FD = 16, 16
KT = DIM // P
HD = H * DH
ROWS = NB * NQ
NT = ROWS // P
NPAIR = NB // 2
PR = 2 * NQ
PT = PR // P
PM = 2 * MK
HM = H * MK
HT = -(-HM // P)
CROWS = NB * MK
XT, NG = 8, 4
CSTEP = CROWS // NG
CG = -(-CSTEP // P)
START = 2
EPS = 1e-5
L2_EPS = 1e-12
PAD = 127 + MK
PADW = 2 * H * PAD + 127
ALL = slice(None)
WS, KS, FV, MS, VS = 64.0, 64.0, 8.0, 64.0, 16.0

HEAD_PARTS = [(0, 3), (3, 6), (6, 8)]
HM_TILES = [(0, 1), (2, 3), (4,)]
HM_ROWS = [min(P, HM - P * t) for t in range(HT)]


def bc(ap, shape):
    return ap.to_broadcast(shape)


def build(nc, x, ctx_in, g_x, g_f, ln_g, ln_b, w_in, w_inT, w1T, b1, wln_g, wln_b, w2T, b2, w_outT, b_out,
          wq, wk, wv, wo, woT, wff, out):
    kstat = nc.dram_tensor("kstat", (2 * H, CROWS), F32, kind="Internal").ap()
    parts = nc.dram_tensor("parts", (4, DIM, PR), F16, kind="Internal").ap()
    x_rows = x.rearrange("b n d -> (b n) d")
    out_rows = out.rearrange("b n d -> (b n) d")
    c_rows = ctx_in.rearrange("b m d -> (b m) d")

    with ExitStack() as keep:
        def sb(name, shape, dt=F32):
            return keep.enter_context(nc.sbuf_tensor(name, shape, dt))

        def pair(name, shape):
            return {half: sb(name + half, shape, F16) for half in "hl"}

        w = {
            "wT": pair("wT", [P, KT, HD]), "wN": pair("wN", [P, H, DIM]), "woutT": pair("woutT", [P, H, DIM]),
            "wq": pair("wq", [P, KT, DIM]), "wk": pair("wk", [P, KT, DIM]), "wv": pair("wv", [P, KT, DIM]),
            "wof": pair("wof", [P, KT, 2 * DIM]), "ident": sb("ident", [P, P]),
            "gcol": sb("gcol", [P, KT]), "bcol": sb("bcol", [P, KT]), "tb": sb("tb", [P, DIM]),
            "tg": sb("tg", [P, 2]), "cvec": sb("cvec", [P, H]), "wwv": sb("wwv", [P, H]),
            "stats": sb("stats", [P, NT, 2]), "zcT": pair("zcT", [P, KT, CROWS]),
            "mhalf": sb("mhalf", [P, PT * H]), "phalf": sb("phalf", [P, H]), "xin": sb("xin", [P, PT, DIM]),
            "x_ready": keep.enter_context(nc.semaphore("x_ready")),
        }
        with ExitStack() as first:
            setup_phase(nc, first, w, locals())
        with ExitStack() as second:
            main_phase(nc, second, w, x_rows, out_rows, kstat, parts)


def setup_phase(nc, ctx, w, a):
    x_rows, c_rows, kstat = a["x_rows"], a["c_rows"], a["kstat"]

    def sb(name, shape, dt=F32):
        return ctx.enter_context(nc.sbuf_tensor(name, shape, dt))

    def ps(name, shape):
        return ctx.enter_context(nc.psum_tensor(name, shape, F32))

    def sem(name):
        return ctx.enter_context(nc.semaphore(name))

    full = {
        "wT": sb("s_wT", [P, KT, HD]), "wN": sb("s_wN", [P, H, DIM]), "woutT": sb("s_woutT", [P, H, DIM]),
        "wq": sb("s_wq", [P, KT, DIM]), "wk": sb("s_wk", [P, KT, DIM]), "wv": sb("s_wv", [P, KT, DIM]),
        "wo": sb("s_wo", [P, KT, DIM]),
    }
    xin = sb("s_xin", [P, 2, XT, DIM])
    xa = sb("s_xa", [P, 2, XT, DIM + 4])
    xst = sb("s_xst", [P, 2, XT, 6])
    xmv, xtmp = sb("s_xmv", [P, 2, XT, 1]), sb("s_xtmp", [P, 2, XT, 2])
    xrs, xvar, xnm = sb("s_xrs", [P, 2, XT]), sb("s_xvar", [P, 2, XT]), sb("s_xnm", [P, 2, XT])
    g_bc, b_bc = sb("s_gbc", [P, DIM]), sb("s_bbc", [P, DIM])
    cin, cz = sb("s_cin", [P, CG, DIM]), sb("s_cz", [P, CG, DIM])
    cT = {half: sb("s_cT" + half, [P, KT, CSTEP], F16) for half in "hl"}
    cTf = sb("s_cTf", [P, 2, KT, P])
    cst, cmv, ctmp = sb("s_cst", [P, CG, 6]), sb("s_cmv", [P, CG, 1]), sb("s_ctmp", [P, CG, 2])
    cvar, crs, cnm = sb("s_cvar", [P, CG]), sb("s_crs", [P, CG]), sb("s_cnm", [P, CG])
    csums = sb("s_csums", [P, NG * CG, KT])
    fst = sb("s_fst", [P, CG, H, 6])
    ft = sb("s_ft", [P, 6, CG, H])
    kst = sb("s_kst", [P, NG * CG, 2, H])
    kstT = sb("s_kstT", [2 * H, CROWS])
    mhalf = sb("s_mhalf", [P, CG * H])
    zeros = sb("s_zeros", [1, DIM + 1])
    ones = sb("s_ones", [P, P])
    offdiag = sb("s_off", [P, P])
    gates = sb("s_gates", [P, 2])
    woT_sb, wff_sb = sb("s_woT", [P, KT, DIM]), sb("s_wff", [P, KT, DIM])
    w1T_sb, w2T_sb = sb("s_w1T", [P, 2, DH]), sb("s_w2T", [DH, 3])
    rows8 = sb("s_rows8", [H, 3, DH])
    b2row = sb("s_b2", [H, 3])
    gram = sb("s_gram", [P, KT, DIM])
    zs, zg = sb("s_zs", [P, KT]), sb("s_zg", [P, KT])
    sums = sb("s_sums", [P, KT, 2])
    spread = sb("s_spread", [P, 2, KT, P])
    bu, wsum = sb("s_bu", [P, KT, DIM]), sb("s_wsum", [P, H, DIM])
    wmean = sb("s_wmean", [P, KT * H])
    wcT = sb("s_wcT", [P, KT, HD])
    hm = sb("s_hm", [P, KT, HD])
    fc = sb("s_fc", [P, H, DH])
    fcs = sb("s_fcs", [P, H])
    dec = sb("s_dec", [P, H])
    fe = sb("s_fe", [P, 2, H])
    h1, h1s, h1v = sb("s_h1", [H, DH]), sb("s_h1s", [H, 6]), sb("s_h1v", [H, 4])
    h1T = sb("s_h1T", [DH, H])
    lg = sb("s_lg", [H, 8])
    dgw = sb("s_dgw", [H, 3, H])
    mix = sb("s_mix", [P, 3, H])

    gram_ps = [ps(f"s_gram{k}", [P, 512]) for k in range(KT)]
    t_ps = [ps(f"s_tps{k}", [P, 512]) for k in range(2)]
    f_ps = ps("s_fps", [P, 4, 512])

    early, loaded = sem("s_early"), sem("s_loaded")
    x_loaded, c_loaded = [sem("s_xl0"), sem("s_xl1")], sem("s_cl")
    xvar_ready, xr_ready, xnm_ready = sem("s_xvr"), sem("s_xrr"), sem("s_xnr")
    z_ready, grammed, hm_ready = sem("s_zr"), sem("s_grammed"), sem("s_hmr")
    c_var, c_rstd, cnm_ready, cz_ready = sem("s_cvr"), sem("s_crr"), sem("s_cnr"), sem("s_czr")
    ct_turned, ct_full, ct_ready, zc_kept = sem("s_ctt"), sem("s_ctf"), sem("s_ctr"), sem("s_zck")
    f_ready, f_used, ksq_ready, rk_ready = sem("s_fr"), sem("s_fu"), sem("s_ksq"), sem("s_rk")
    kst_ready, kT_ready, kT_stored = sem("s_kstr"), sem("s_kTr"), sem("s_kTs")
    consts, step, turns = sem("s_consts"), sem("s_step"), sem("s_turns")
    pe_step, act_step, pool_step = sem("s_pe"), sem("s_act"), sem("s_pool")
    wT_half, wT_split, w_half, w_gated, wof_half = sem("s_wTh"), sem("s_wTs"), sem("s_wh"), sem("s_wg"), sem("s_wofh")
    LATER = ("wN", "wq", "wk", "wv", "woutT")
    N_EARLY, N_LOADS = 5, 17
    CPOS = [(P * t, 0) for t in range(CG - 1)] + [(CSTEP - P, CG * P - CSTEP)]

    def wait_slot(eng, ready, i, t):
        if t != 1:
            eng.wait_ge(ready, i * CG + max(t - 1, 0) + START)

    with nc.Block() as block:
        @block.sync
        def _(sp):
            def sp_wait(ready, value):
                sp.wait_ge(ready, value)
                sp.sem_inc(turns, 1)

            def load(dst, src, ready=loaded):
                sp.dma_start(dst, src).then_inc(ready, 16)

            def load_x(half, i):
                sp.dma_start(xin[:, half, :, :], x_rows[bass.ds((i * 2 + half) * (XT * P), XT * P), :]
                             .rearrange("(t p) d -> p t d", p=P)).then_inc(x_loaded[half], 16)

            def load_c(i):
                sp.dma_start(cin[:, 0:CG - 1, :], c_rows[bass.ds(i * CSTEP, (CG - 1) * P), :]
                             .rearrange("(t p) d -> p t d", p=P)).then_inc(c_loaded, 16)
                sp.dma_start(cin[:, CG - 1, :], c_rows[bass.ds(i * CSTEP + CPOS[-1][0], P), :]).then_inc(c_loaded, 16)

            def keep_c(i):
                sp_wait(ct_ready, i * CG + CG + START)
                for half in "hl":
                    sp.dma_start(w["zcT"][half][:, :, bass.ds(i * CSTEP, CSTEP)], cT[half][:]).then_inc(zc_kept, 16)

            for waited in (grammed, ct_full, ct_ready, f_used, zc_kept, ct_turned, rk_ready):
                sp.sem_inc(waited, START)
            with nc.allow_non_contiguous_dma(reason="columns of a few values"):
                load_c(0)
                load(full["wT"][:], a["w_inT"].rearrange("(k p) c -> p k c", p=P), early)
                load(w["gcol"][:], a["ln_g"].rearrange("(k p) -> p k", p=P), early)
                load(w["bcol"][:], a["ln_b"].rearrange("(k p) -> p k", p=P), early)
                load(g_bc[:], a["ln_g"].partition_broadcast(P), early)
                load(b_bc[:], a["ln_b"].partition_broadcast(P), early)
                load_x(0, 0)
                load_x(1, 0)
                load(gates[:, 0:1], a["g_x"].partition_broadcast(P))
                load(gates[:, 1:2], a["g_f"].partition_broadcast(P))
                load(full["wN"][:], a["w_in"].rearrange("(h d) k -> d h k", d=DH))
                load(full["woutT"][:], a["w_outT"].rearrange("(h d) o -> d h o", d=DH))
                load(w["tb"][:], a["b_out"].partition_broadcast(P))
                for name in ("wq", "wk", "wv"):
                    load(full[name][:], a[name].rearrange("(k p) c -> p k c", p=P))
                load(full["wo"][:], a["wo"].rearrange("(k p) c -> p k c", p=P))
                load(woT_sb[:], a["woT"].rearrange("(k p) c -> p k c", p=P))
                load(wff_sb[:], a["wff"].rearrange("(k p) c -> p k c", p=P))
                load(w1T_sb[:], a["w1T"].rearrange("(k p) c -> p k c", p=P))
                load(w2T_sb[:], a["w2T"])
                for j, name in enumerate(("b1", "wln_g", "wln_b")):
                    load(rows8[:, j, :], a[name].partition_broadcast(H))
                load(b2row[:], a["b2"].partition_broadcast(H))
                with sp.Fori(0, NG - 1) as i:
                    sp_wait(cz_ready, i + 1)
                    load_c(i + 1)
                    for half in range(2):
                        sp_wait(z_ready, i * 2 + half + 1)
                        load_x(half, i + 1)
                    keep_c(i)
                sp.dma_start(w["xin"][:], x_rows[0:PR, :].rearrange("(t p) d -> p t d", p=P)).then_inc(w["x_ready"], 16)
                keep_c(NG - 1)
                sp.wait_ge(kT_ready, 3)
                sp.dma_start(kstat, kstT[:]).then_inc(kT_stored, 16)
                sp.wait_ge(kT_stored, 16)
                sp.wait_ge(zc_kept, 32 * NG + START)

        @block.gpsimd
        def _(pool):
            nc.gpsimd.memset(w["ident"][:], 0.0).then_inc(pool_step, 1)
            nc.gpsimd.memset(offdiag[:], 1.0).then_inc(pool_step, 1)
            nc.gpsimd.memset(w["mhalf"][:], -0.5).then_inc(consts, 1)
            nc.gpsimd.memset(w["phalf"][:], 0.5).then_inc(consts, 1)
            nc.gpsimd.memset(ones[:], 1.0).then_inc(consts, 1)
            nc.gpsimd.memset(zeros[:], 0.0).then_inc(consts, 1)
            nc.gpsimd.memset(xa[:, :, :, DIM:DIM + 4], 1.0).then_inc(consts, 1)
            nc.gpsimd.memset(mhalf[:], -0.5).then_inc(consts, 1)
            pool.wait_ge(pool_step, 2)
            nc.gpsimd.affine_select(out=w["ident"][:], in_=w["ident"][:], compare_op=ALU.not_equal, fill=1.0,
                                    base=0, pattern=[[-1, P]], channel_multiplier=1).then_inc(consts, 1)
            nc.gpsimd.affine_select(out=offdiag[:], in_=offdiag[:], compare_op=ALU.not_equal, fill=0.0,
                                    base=0, pattern=[[-1, P]], channel_multiplier=1).then_inc(consts, 1)
            pool.wait_ge(consts, 8)
            def c_power(i):
                pool.wait_ge(c_var, i + 1)
                nc.gpsimd.tensor_tensor(crs[:], cvar[:], mhalf[:, 0:CG], ALU.pow).then_inc(c_rstd, 1)

            def k_power(i, part):
                heads = slice(part * H // 2, (part + 1) * H // 2)
                pool.wait_ge(ksq_ready, i + 1)
                nc.gpsimd.tensor_tensor(kst[:, bass.ds(i * CG, CG), 0, heads], ft[:, 0, :, heads],
                                        mhalf[:, 0:CG * H // 2].rearrange("p (t h) -> p t h", h=H // 2),
                                        ALU.pow).then_inc(rk_ready, 1)

            def x_part(i, first=False):
                for half in range(2):
                    pool.wait_ge(xvar_ready, i * 2 + half + 1)
                    nc.gpsimd.tensor_tensor(xrs[:, half, :], xvar[:, half, :], mhalf[:, 0:XT], ALU.pow).then_inc(xr_ready, 1)
                    if half == 0 and not first:
                        k_power(i - 1, 1)

            c_power(0)
            pool.wait_ge(early, 16 * N_EARLY)
            x_part(0, first=True)
            c_power(1)
            k_power(0, 0)
            with pool.Fori(0, NG - 2) as i:
                x_part(i + 1)
                c_power(i + 2)
                k_power(i + 1, 0)
            x_part(NG - 1)
            for part in range(2):
                k_power(NG - 1, part)
            pool.wait_ge(step, DVE_TAIL["h1var"])
            nc.gpsimd.tensor_tensor(h1v[:, 2:3], h1v[:, 1:2], mhalf[0:H, 0:1], ALU.pow).then_inc(pool_step, 1)
            pool.wait_ge(step, DVE_TAIL["dec"])
            nc.gpsimd.tensor_tensor(dec[:], dec[:], w["phalf"][:], ALU.pow).then_inc(pool_step, 1)

        @block.vector
        def _(dve):
            done = [0]

            def link(ins):
                done[0] += 1
                ins.then_inc(step, 1)
                dve.wait_ge(step, done[0])

            def tail_link(name, ins):
                link(ins)
                assert done[0] == DVE_TAIL[name]

            def c_front(i, link):
                dve.wait_ge(c_loaded, i * 32 + 32)
                for t in range(CG):
                    last = nc.vector.bn_stats(cst[:, t, :], cin[:, t, :])
                link(0, last)
                row_moments(nc, link, 0, cst[:], cmv, ctmp)
                nc.vector.tensor_scalar(cvar[:], ctmp[:, :, 1], 1.0 / DIM, EPS, ALU.mult, ALU.add).then_inc(c_var, 1)

            def c_shift(i):
                dve.wait_ge(c_rstd, i + 1)
                nc.vector.scalar_tensor_tensor(cnm[:], cmv[:, :, 0], -1.0, crs[:], ALU.mult, ALU.mult).then_inc(cnm_ready, 1)

            def x_front(i, half, link):
                dve.wait_ge(x_loaded[half], i * 16 + 16)
                for t in range(XT):
                    last = nc.vector.bn_stats(xst[:, half, t, :], xin[:, half, t, :])
                link(0, last)
                row_moments(nc, link, 0, xst[:, half], xmv[:, half], xtmp[:, half])
                nc.vector.tensor_scalar(xvar[:, half, :], xtmp[:, half, :, 1], (1.0 + EPS) / DIM, EPS * EPS,
                                        ALU.mult, ALU.add).then_inc(xvar_ready, 1)
                nc.vector.tensor_copy(w["stats"][:, bass.ds((i * 2 + half) * XT, XT), 0], xmv[:, half, :, 0])

            def x_shift(i, half):
                dve.wait_ge(xr_ready, i * 2 + half + 1)
                nc.vector.scalar_tensor_tensor(xnm[:, half, :], xmv[:, half, :, 0], -1.0, xrs[:, half, :],
                                               ALU.mult, ALU.mult).then_inc(xnm_ready, 1)
                nc.vector.tensor_copy(w["stats"][:, bass.ds((i * 2 + half) * XT, XT), 1], xrs[:, half, :])

            def key_stats(i, t):
                dve.wait_ge(f_ready, i * CG + t + 1)
                for h in range(H):
                    last = nc.vector.bn_stats(fst[:, t, h, :], f_ps[:, 2 * (t % 2) + h // 4, (h % 4) * DH:(h % 4 + 1) * DH])
                last.then_inc(f_used, 1)

            def tiles(i, link, following):
                def left(t):
                    at, seen = CPOS[t]
                    dve.wait_ge(ct_full, i * CG + t + 1 + START)
                    if t == 0:
                        dve.wait_ge(zc_kept, i * 32 + START)
                    nc.vector.tensor_tensor(cT["l"][:, :, at + seen:at + P], cTf[:, t % 2, :, seen:P],
                                            cT["h"][:, :, at + seen:at + P], ALU.subtract).then_inc(ct_ready, 1)

                x_front(i, 0, link)
                left(0)
                left(1)
                x_front(i, 1, link)
                x_shift(i, 0)
                x_shift(i, 1)
                for t in range(2, CG):
                    left(t)
                    key_stats(i, t - 2)
                key_stats(i, CG - 2)
                if following:
                    c_front(i + 1, link)
                key_stats(i, CG - 1)
                if following:
                    c_shift(i + 1)
                dve.wait_ge(f_used, i * CG + CG + START)
                dve.wait_ge(rk_ready, i * 2 + START)
                moments(nc, link, 0, fst[:], ft, WS)
                dve.sem_inc(ksq_ready, 1)
                link(0, ratio_num(nc, ft))
                link(0, ratio_den(nc, ft))
                link(0, nc.vector.reciprocal(ft[:, 3, :, :], ft[:, 3, :, :]))
                nc.vector.tensor_tensor(kst[:, bass.ds(i * CG, CG), 1, :], ft[:, 2, :, :], ft[:, 3, :, :],
                                        ALU.mult).then_inc(kst_ready, 1)

            def straight(_, ins):
                link(ins)

            dve.wait_ge(consts, 8)
            c_front(0, straight)
            c_shift(0)
            dve.wait_ge(wT_half, 1)
            nc.vector.scalar_tensor_tensor(w["wT"]["l"][:], full["wT"][:], WS, w["wT"]["h"][:],
                                           ALU.mult, ALU.subtract).then_inc(wT_split, 1)
            before = done[0]
            with dve.Fori(0, NG - 1) as i:
                count = [0]

                def in_loop(_, ins):
                    count[0] += 1
                    ins.then_inc(step, 1)
                    dve.wait_ge(step, i * STEP_LINKS + before + count[0])

                tiles(i, in_loop, True)
                assert count[0] == STEP_LINKS
            done[0] = before + (NG - 1) * STEP_LINKS
            tiles(NG - 1, straight, False)
            link(nc.vector.tensor_reduce(wmean[:], full["wT"][:].rearrange("p k (h d) -> p (k h) d", d=DH), AX.X, ALU.add))
            link(nc.vector.tensor_scalar(wmean[:], wmean[:], -1.0 / DH, None, ALU.mult))
            link(nc.vector.tensor_tensor(wcT[:].rearrange("p k (h d) -> p (k h) d", d=DH),
                                         full["wT"][:].rearrange("p k (h d) -> p (k h) d", d=DH),
                                         bc(wmean[:].unsqueeze(2), [P, KT * H, DH]), ALU.add))
            assert done[0] == DVE_LOOPS
            dve.wait_ge(ct_full, NG * CG + START)
            nc.vector.tensor_reduce(sums[:, :, 1], csums[:].rearrange("p n k -> p k n"), AX.X, ALU.add)
            dve.wait_ge(act_step, 1)
            nc.vector.tensor_scalar(full["woutT"][:], full["woutT"][:], w["tg"][:, 0:1], None, ALU.mult).then_inc(w_gated, 1)
            nc.vector.tensor_scalar(w["tb"][:], w["tb"][:], w["tg"][:, 0:1], None, ALU.mult)

            def split_rest(n):
                name = LATER[n]
                dve.wait_ge(w_half, n + 1)
                nc.vector.scalar_tensor_tensor(w[name]["l"][:], full[name][:], WS, w[name]["h"][:], ALU.mult, ALU.subtract)

            dve.wait_ge(pe_step, 1)
            nc.vector.tensor_copy(zs[:, 0:1], gram_ps[0][:, DIM:DIM + 1])
            link(nc.vector.tensor_copy(zs[:, 1:2], gram_ps[1][:, DIM:DIM + 1]))
            link(nc.vector.tensor_tensor(zg[:], zs[:], w["gcol"][:], ALU.mult))
            link(nc.vector.scalar_tensor_tensor(sums[:, :, 0], w["bcol"][:], float(ROWS), zg[:], ALU.mult, ALU.add))
            for j in range(2):
                for k in range(KT):
                    last = nc.vector.tensor_scalar(spread[:, j, k, :], ones[:], sums[:, k, j:j + 1], None, ALU.mult)
            tail_link("spread", last)
            upper = [slice(k * P, DIM) for k in range(KT)]
            for k, cols in enumerate(upper):
                last = nc.vector.tensor_tensor(gram[:, k, cols], gram_ps[k][:, cols], g_bc[:, cols], ALU.mult)
            link(last)
            for k, cols in enumerate(upper):
                last = nc.vector.scalar_tensor_tensor(gram[:, k, cols], b_bc[:, cols], zs[:, k:k + 1], gram[:, k, cols],
                                                      ALU.mult, ALU.add)
            link(last)
            dve.wait_ge(pe_step, 3)
            for k, cols in enumerate(upper):
                last = nc.vector.tensor_scalar(bu[:, k, cols], t_ps[0][:, cols], w["bcol"][:, k:k + 1], None, ALU.mult)
            link(last)
            for k, cols in enumerate(upper):
                last = nc.vector.scalar_tensor_tensor(gram[:, k, cols], gram[:, k, cols], w["gcol"][:, k:k + 1],
                                                      bu[:, k, cols], ALU.mult, ALU.add)
            tail_link("gram", last)
            dve.wait_ge(pe_step, 4)
            tail_link("lower", nc.vector.tensor_copy(gram[:, 1, 0:P], t_ps[1][:, 0:P]))
            dve.wait_ge(wof_half, 2)
            tail_link("wof", nc.vector.scalar_tensor_tensor(
                w["wof"]["l"][:, :, DIM:2 * DIM], f_ps[:, 3, :].rearrange("p (k c) -> p k c", c=DIM), WS,
                w["wof"]["h"][:, :, DIM:2 * DIM], ALU.mult, ALU.subtract))
            dve.wait_ge(loaded, 16 * N_LOADS)
            for j in range(2):
                link(nc.vector.tensor_tensor(wsum[:], full["wN"][:], bc(t_ps[0][:, j * DIM:(j + 1) * DIM].unsqueeze(1),
                                                                        [P, H, DIM]), ALU.mult))
                link(nc.vector.tensor_reduce(fe[:, j, :], wsum[:], AX.X, ALU.add))
            nc.vector.tensor_scalar(fe[:, 0, :], fe[:, 0, :], 1.0 / ROWS, None, ALU.mult)
            tail_link("fe", nc.vector.tensor_scalar(fe[:, 1, :], fe[:, 1, :], 1.0 / CROWS, None, ALU.mult))
            split_rest(0)
            dve.wait_ge(pe_step, 8)
            link(nc.vector.tensor_tensor(h1[:], t_ps[1][0:H, 0:DH], rows8[:, 0, :], ALU.add))
            link(nc.vector.bn_stats(h1s[:], h1[:]))
            link(nc.vector.bn_aggr(h1v[:, 0:2], h1s[:]))
            tail_link("h1var", nc.vector.tensor_scalar(h1v[:, 1:2], h1v[:, 1:2], EPS, None, ALU.add))
            dve.wait_ge(pool_step, 3)
            link(nc.vector.tensor_scalar(h1[:], h1[:], h1v[:, 0:1], h1v[:, 2:3], ALU.subtract, ALU.mult))
            link(nc.vector.tensor_tensor(h1[:], h1[:], rows8[:, 1, :], ALU.mult))
            link(nc.vector.tensor_tensor(h1[:], h1[:], rows8[:, 2, :], ALU.add))
            tail_link("h1", nc.vector.tensor_scalar(h1[:], h1[:], 0.0, None, ALU.max))

            def correlation(a):
                heads = slice(a * 4, a * 4 + 4)
                link(nc.vector.tensor_tensor(fc[:, heads, :], gram_ps[a][:, :].rearrange("p (h d) -> p h d", d=DH),
                                             bc(offdiag[:].unsqueeze(1), [P, 4, DH]), ALU.mult))
                link(nc.vector.tensor_tensor(fc[:, heads, :], fc[:, heads, :], fc[:, heads, :], ALU.mult))
                tail_link(f"fcsum{a}", nc.vector.tensor_reduce(fcs[:, heads], fc[:, heads, :], AX.X, ALU.add))

            dve.wait_ge(pe_step, 9)
            correlation(0)
            dve.wait_ge(pe_step, 10)
            tail_link("h1T", nc.vector.tensor_copy(h1T[:], t_ps[0][:, 0:H]))
            split_rest(1)
            dve.wait_ge(pe_step, 11)
            correlation(1)
            dve.wait_ge(pe_step, 12)
            link(nc.vector.tensor_tensor(lg[:, 0:3], t_ps[1][0:H, 0:3], b2row[:], ALU.add))
            tail_link("lmax", nc.vector.tensor_reduce(lg[:, 3:4], lg[:, 0:3], AX.X, ALU.max, negate=True))
            dve.wait_ge(pe_step, 14)
            tail_link("dec", nc.vector.tensor_copy(dec[:], t_ps[0][:, DIM:DIM + H]))
            split_rest(2)
            dve.wait_ge(act_step, 2)
            link(nc.vector.reciprocal(lg[:, 4:5], lg[:, 4:5]))
            link(nc.vector.tensor_scalar(lg[:, 5:8], lg[:, 5:8], lg[:, 4:5], None, ALU.mult))
            for j in range(3):
                last = nc.vector.tensor_scalar(dgw[:, j, :], w["ident"][0:H, 0:H], lg[:, 5 + j:6 + j], None, ALU.mult)
            tail_link("dgw", last)
            split_rest(3)
            split_rest(4)
            dve.wait_ge(wof_half, 1)
            nc.vector.scalar_tensor_tensor(w["wof"]["l"][:, :, 0:DIM], full["wo"][:], WS, w["wof"]["h"][:, :, 0:DIM],
                                           ALU.mult, ALU.subtract)
            dve.wait_ge(pe_step, 16)
            link(nc.vector.tensor_copy(mix[:].rearrange("p a h -> p (a h)"), t_ps[0][:, 0:3 * H]))
            dve.wait_ge(act_step, 3)
            link(nc.vector.tensor_tensor(dec[:], dec[:], mix[:, 1, :], ALU.mult))
            nc.vector.tensor_tensor(w["cvec"][:], dec[:], mix[:, 0, :], ALU.add)
            link(nc.vector.tensor_copy(w["wwv"][:], mix[:, 2, :]))

        @block.scalar
        def _(act):
            act.wait_ge(early, 16 * N_EARLY)
            nc.scalar.activation(w["wT"]["h"][:], full["wT"][:], ACT.Copy, scale=WS).then_inc(wT_half, 1)

            def c_norm(i):
                act.wait_ge(cnm_ready, i + 1)
                for t in range(CG):
                    last = nc.scalar.activation(cz[:, t, :], cin[:, t, :], ACT.Identity, scale=crs[:, t:t + 1],
                                                bias=cnm[:, t:t + 1])
                last.then_inc(cz_ready, 1)

            def tiles(i):
                def turned(t):
                    at, seen = CPOS[t]
                    act.wait_ge(ct_turned, i * CG + t + 1 + START)
                    if t == 0:
                        act.wait_ge(zc_kept, i * 32 + START)
                    for k in range(KT):
                        nc.scalar.activation(cT["h"][:, k, at + seen:at + P], t_ps[t % 2][:, k * P + seen:(k + 1) * P],
                                             ACT.Identity, scale=w["gcol"][:, k:k + 1], bias=w["bcol"][:, k:k + 1])
                    wait_slot(act, ct_ready, i, t)
                    for k in range(KT):
                        last = nc.scalar.activation(cTf[:, t % 2, k, seen:P], t_ps[t % 2][:, k * P + seen:(k + 1) * P],
                                                    ACT.Identity, scale=w["gcol"][:, k:k + 1], bias=w["bcol"][:, k:k + 1],
                                                    accum_out=csums[:, bass.ds(i * CG + t, 1), k])
                    last.then_inc(ct_full, 1)

                for t in range(3):
                    turned(t)
                for half in range(2):
                    act.wait_ge(xnm_ready, i * 2 + half + 1)
                    act.wait_ge(grammed, i * 2 + half - 1 + START)
                    for t in range(XT):
                        last = nc.scalar.activation(xa[:, half, t, 0:DIM], xin[:, half, t, :], ACT.Identity,
                                                    scale=xrs[:, half, t:t + 1], bias=xnm[:, half, t:t + 1])
                    last.then_inc(z_ready, 1)
                    if half == 0:
                        turned(3)
                        turned(4)

            c_norm(0)
            with act.Fori(0, NG - 1) as i:
                tiles(i)
                c_norm(i + 1)
            tiles(NG - 1)
            act.wait_ge(loaded, 16 * N_LOADS)
            nc.scalar.activation(w["tg"][:], gates[:], ACT.Tanh).then_inc(act_step, 1)
            for name in LATER:
                if name == "woutT":
                    act.wait_ge(w_gated, 1)
                nc.scalar.activation(w[name]["h"][:], full[name][:], ACT.Copy, scale=WS).then_inc(w_half, 1)
            nc.scalar.activation(w["wof"]["h"][:, :, 0:DIM], full["wo"][:], ACT.Copy, scale=WS).then_inc(wof_half, 1)
            act.wait_ge(pe_step, 2)
            nc.scalar.activation(w["wof"]["h"][:, :, DIM:2 * DIM], f_ps[:, 3, :].rearrange("p (k c) -> p k c", c=DIM),
                                 ACT.Copy, scale=WS).then_inc(wof_half, 1)
            for k in range(KT):
                act.wait_ge(pe_step, 5 + k)
                nc.scalar.activation(hm[:, k, :].rearrange("p (c n) -> p c n", n=512), f_ps[:, 2 * k:2 * k + 2, :],
                                     ACT.Copy).then_inc(hm_ready, 1)
            rows = kstT[:].rearrange("h (i n) -> h i n", n=CSTEP)
            for n in range(NG // 2):
                act.wait_ge(pe_step, (7, 13)[n])
                steps = slice(2 * n, 2 * n + 2)
                nc.scalar.activation(rows[:, steps, 0:512], f_ps[0:2 * H, steps, :], ACT.Copy).then_inc(kT_ready, 1)
            act.wait_ge(step, DVE_TAIL["lmax"])
            nc.scalar.activation(lg[:, 5:8], lg[:, 0:3], ACT.Exp, bias=lg[:, 3:4],
                                 accum_out=lg[:, 4:5]).then_inc(act_step, 1)
            act.wait_ge(pe_step, 15)
            at, seen = CPOS[-1]
            nc.scalar.activation(rows[:, :, at + seen:at + P],
                                 gram_ps[1][0:2 * H, :].rearrange("h (i n) -> h i n", n=P)[:, :, seen:P],
                                 ACT.Copy).then_inc(kT_ready, 1)
            act.wait_ge(pool_step, 4)
            nc.scalar.activation(dec[:], dec[:], ACT.Exp, scale=-5.0 / (ROWS * DH * DH)).then_inc(act_step, 1)

        @block.tensor
        def _(pe):
            pe.wait_ge(consts, 8)
            GRAM = [(slice(0, DIM + 1), DIM + 1), (slice(P, DIM + 1), DIM + 1 - P)]
            for k, (cols, n) in enumerate(GRAM):
                nc.tensor.matmul(gram_ps[k][:, cols], zeros[:, 0:P], zeros[:, 0:n], start=True, stop=False)

            def turn(i, t):
                if t == 0:
                    pe.wait_ge(cz_ready, i + 1)
                wait_slot(pe, ct_full, i, t)
                for k in range(KT):
                    last = nc.tensor.transpose(t_ps[t % 2][:, k * P:(k + 1) * P], cz[:, t, k * P:(k + 1) * P], w["ident"][:])
                last.then_inc(ct_turned, 1)

            def project(i, t):
                at = CPOS[t][0]
                pe.wait_ge(ct_ready, i * CG + t + 1 + START)
                wait_slot(pe, f_used, i, t)
                for c in range(2):
                    for k in range(KT):
                        last = products(nc, f_ps[:, 2 * (t % 2) + c, :], cT, (ALL, k, slice(at, at + P)),
                                        w["wT"], (ALL, k, slice(c * 512, (c + 1) * 512)), k == 0, k == KT - 1)
                last.then_inc(f_ready, 1)

            def tiles(i, following):
                for t in range(CG):
                    if t + 2 < CG:
                        turn(i, t + 2)
                    project(i, t)
                for half in range(2):
                    pe.wait_ge(z_ready, i * 2 + half + 1)
                    for t in range(XT):
                        if following and half == 1 and t == XT // 2:
                            turn(i + 1, 0)
                            turn(i + 1, 1)
                        for k, (cols, n) in enumerate(GRAM):
                            last = nc.tensor.matmul(gram_ps[k][:, cols], xa[:, half, t, k * P:(k + 1) * P],
                                                    xa[:, half, t, cols], start=False, stop=False)
                    last.then_inc(grammed, 1)

            turn(0, 0)
            turn(0, 1)
            pe.wait_ge(wT_split, 1)
            with pe.Fori(0, NG - 1) as i:
                tiles(i, True)
            tiles(NG - 1, False)
            for k, (cols, n) in enumerate(GRAM):
                last = nc.tensor.matmul(gram_ps[k][:, cols], zeros[:, 0:P], zeros[:, 0:n], start=False, stop=True)
            last.then_inc(pe_step, 1)
            pe.wait_ge(loaded, 16 * N_LOADS)
            pe.wait_ge(f_used, NG * CG + START)
            for m in range(KT):
                for k in range(KT):
                    last = nc.tensor.matmul(f_ps[:, 3, m * DIM:(m + 1) * DIM], woT_sb[:, k, m * P:(m + 1) * P],
                                            wff_sb[:, k, :], start=(k == 0), stop=(k == KT - 1))
            last.then_inc(pe_step, 1)
            pe.wait_ge(step, DVE_TAIL["spread"])
            for j in range(2):
                for k in range(KT):
                    last = nc.tensor.matmul(t_ps[0][:, j * DIM + k * P:j * DIM + (k + 1) * P], spread[:, j, k, :],
                                            w["ident"][:], start=True, stop=True)
            last.then_inc(pe_step, 1)
            pe.wait_ge(step, DVE_TAIL["gram"])
            nc.tensor.transpose(t_ps[1][:, 0:P], gram[:, 0, P:DIM], w["ident"][:]).then_inc(pe_step, 1)
            for m in range(KT):
                if m == 1:
                    pe.wait_ge(step, DVE_TAIL["wof"])
                for k in range(KT):
                    if m == 0 and k == 1:
                        pe.wait_ge(step, DVE_TAIL["lower"])
                    for c in range(2):
                        last = nc.tensor.matmul(f_ps[:, 2 * m + c, :], gram[:, k, m * P:(m + 1) * P],
                                                wcT[:, k, c * 512:(c + 1) * 512], start=(k == 0), stop=(k == KT - 1))
                last.then_inc(pe_step, 1)

            def turn_stats(dst, i, t):
                return nc.tensor.transpose(dst, kst[:, i * CG + t, :, :].rearrange("p a h -> p (a h)"), w["ident"][:])

            def turn_keys(n):
                pe.wait_ge(hm_ready, n + 1)
                for i in (2 * n, 2 * n + 1):
                    for t in range(CG - 1):
                        last = turn_stats(f_ps[0:2 * H, i, t * P:(t + 1) * P], i, t)
                last.then_inc(pe_step, 1)

            def correlate(a):
                for h in range(4 * a, 4 * a + 4):
                    for k in range(KT):
                        last = nc.tensor.matmul(gram_ps[a][:, (h % 4) * DH:(h % 4 + 1) * DH],
                                                wcT[:, k, h * DH:(h + 1) * DH], hm[:, k, h * DH:(h + 1) * DH],
                                                start=(k == 0), stop=(k == KT - 1))
                last.then_inc(pe_step, 1)

            pe.wait_ge(kst_ready, NG)
            pe.wait_ge(rk_ready, 2 * NG + START)
            turn_keys(0)
            pe.wait_ge(step, DVE_TAIL["fe"])
            for k in range(2):
                last = nc.tensor.matmul(t_ps[1][0:H, 0:DH], fe[:, k, :], w1T_sb[:, k, :], start=(k == 0), stop=(k == 1))
            last.then_inc(pe_step, 1)
            pe.wait_ge(hm_ready, KT)
            correlate(0)
            pe.wait_ge(step, DVE_TAIL["h1"])
            nc.tensor.transpose(t_ps[0][:, 0:H], h1[:], w["ident"][0:H, 0:H]).then_inc(pe_step, 1)
            correlate(1)
            pe.wait_ge(step, DVE_TAIL["h1T"])
            nc.tensor.matmul(t_ps[1][0:H, 0:3], h1T[:], w2T_sb[:], start=True, stop=True).then_inc(pe_step, 1)
            turn_keys(1)
            pe.wait_ge(step, DVE_TAIL["fcsum1"])
            nc.tensor.matmul(t_ps[0][:, DIM:DIM + H], ones[:], fcs[:], start=True, stop=True).then_inc(pe_step, 1)
            for i in range(NG):
                last = turn_stats(gram_ps[1][0:2 * H, i * P:(i + 1) * P], i, CG - 1)
            last.then_inc(pe_step, 1)
            pe.wait_ge(step, DVE_TAIL["dgw"])
            nc.tensor.matmul(t_ps[0][:, 0:3 * H], ones[0:H, :], dgw[:].rearrange("p a h -> p (a h)"),
                             start=True, stop=True).then_inc(pe_step, 1)


STEP_LINKS = 4 + 8 + 8
DVE_LOOPS = 4 + 3 + NG * STEP_LINKS - 4
_TAIL = ["zs", "zg", "sums", "spread", "gramg", "gramb", "bu", "gram", "lower", "wof", "wx", "xmean", "wc", "cmean", "fe",
         "h1add", "h1bn", "h1aggr", "h1var", "h1norm", "h1g", "h1b", "h1", "fcmask0", "fcsq0", "fcsum0", "h1T",
         "fcmask1", "fcsq1", "fcsum1", "ladd", "lmax", "dec", "lrec", "lscale", "dgw"]
DVE_TAIL = {name: DVE_LOOPS + 1 + n for n, name in enumerate(_TAIL)}


def products(nc, out, a, at, b, bt, first=True, last=True):
    nc.tensor.matmul(out, a["h"][at], b["h"][bt], start=first, stop=False)
    nc.tensor.matmul(out, a["h"][at], b["l"][bt], start=False, stop=False)
    return nc.tensor.matmul(out, a["l"][at], b["h"][bt], start=False, stop=last)


def moments(nc, link, k0, st, ft, scale=1.0):
    half = DH // 2
    me, qe, mo, qo = (st[:, :, :, j] for j in (1, 2, 4, 5))
    nc.vector.tensor_tensor(ft[:, 0, :, :], me, mo, ALU.add)
    nc.vector.tensor_tensor(ft[:, 1, :, :], me, mo, ALU.subtract)
    link(k0, nc.vector.tensor_tensor(ft[:, 2, :, :], qe, qo, ALU.add))
    nc.vector.tensor_tensor(ft[:, 3, :, :], ft[:, 1, :, :], ft[:, 1, :, :], ALU.mult)
    link(k0 + 1, nc.vector.tensor_tensor(ft[:, 4, :, :], ft[:, 0, :, :], ft[:, 0, :, :], ALU.mult))
    link(k0 + 2, nc.vector.scalar_tensor_tensor(ft[:, 2, :, :], ft[:, 3, :, :], half / 2.0, ft[:, 2, :, :],
                                                ALU.mult, ALU.add))
    nc.vector.tensor_scalar(ft[:, 1, :, :], ft[:, 2, :, :], 1.0 / ((DH - 1) * scale * scale), None, ALU.mult)
    link(k0 + 3, nc.vector.scalar_tensor_tensor(ft[:, 0, :, :], ft[:, 4, :, :], DH / 4.0, ft[:, 2, :, :],
                                                ALU.mult, ALU.add))
    link(k0 + 4, nc.vector.tensor_copy(ft[:, 5, :, :], ft[:, 1, :, :]))


def row_moments(nc, link, k0, st, mv, tmp):
    me, qe, mo, qo = (st[:, :, j] for j in (1, 2, 4, 5))
    nc.vector.tensor_tensor(mv[:, :, 0], me, mo, ALU.add)
    nc.vector.tensor_tensor(tmp[:, :, 0], me, mo, ALU.subtract)
    link(k0, nc.vector.tensor_tensor(tmp[:, :, 1], qe, qo, ALU.add))
    nc.vector.tensor_scalar(mv[:, :, 0], mv[:, :, 0], 0.5, None, ALU.mult)
    link(k0 + 1, nc.vector.tensor_tensor(tmp[:, :, 0], tmp[:, :, 0], tmp[:, :, 0], ALU.mult))
    link(k0 + 2, nc.vector.scalar_tensor_tensor(tmp[:, :, 1], tmp[:, :, 0], DIM / 4.0, tmp[:, :, 1], ALU.mult, ALU.add))


def ratio_num(nc, ft):
    return nc.vector.tensor_scalar(ft[:, 2, :, :], ft[:, 1, :, :], 1.0, 2.0, ALU.min, ALU.mult)


def ratio_den(nc, ft):
    return nc.vector.tensor_scalar(ft[:, 3, :, :], ft[:, 1, :, :], 1.0, None, ALU.add)


WORK = 3
GROUPS = 2 * FH * KT // 4
PG = 3
SC = 3
PV_CREDIT, OT_CREDIT = GROUPS, 2
EXP_CREDIT = 4 * GROUPS
A_STEPS, B_STEPS = 13, GROUPS + 5

ORDER = """
qs1 G0 G1 S0 G2 G0.h M0 G1.h G0.l ldr S1 G2.h G1.l qpow G2.l S2 G3 G4 M1 X0 G3.h G4.h S3 G3.l V0 M2 G4.l X1 X2 S4 M3
V0.h R0 G5 V1 G5.h M4 P0 S5 X3 X4 V1.h G5.l V0.l R1 M5 S6 qs2 d0 S7 d1 V1.l d0.o d2 M6 d1.o X5 M7 d2.o P1 S8 R2 d3 X6
M8 V2 xb S9 X7 d3.o V2.h X8 M9 S10 V3 R3 X9 S11 x0 M10 V2.l V3.h P2 M11 X10 S12 x1 V4 X11 V3.l S13 M12 m0 V4.h R4 m1
ldx m0.h S14 P3 m1.h M13 X12 P4 V4.l m2 m2.h m0.l R5 d4 X13 m1.l S15 M14 m2.l d4.o d5 E0 S16 P5 M15 d5.o M16 d6 X14
S17 V5 R6 X15 d7 d6.o S18 X16 S19 P6 M17 d7.o M18 V5.h x2 x3 R7 V5.l X17 y0 m3 M19 z R8 y0.o S20 m4 X18 S21 X19 m3.h
L0 S22 ldk m3.l M20 m4.h m5 P7 m5.h m4.l E1 fk0 P8 X20 R9 m5.l M21 S23 fk0.h L1 fk0.l y1 X21 M22 R10 X22 fk0.k S24 zT0
M23 O0 y1.o S25 kh0 M24 P9 zT0.h X23 fk1 ln1 lpow zT0.f O0. P10 fk1.h M25 X24 R11 O1 X25 fk1.l P11 ln2 S26 S27 zz0 kl0
fk1.k R12 S28 zz1 O1. zz0.h M26 zz1.h zz0.l zz1.l M27 X26 P12 fk2 fk2.h zT1 zT1.h X27 fk2.l fk2.k S29 pq0 pq0.h zT1.f
M28 zT0.l M29 pq1 X28 R13 S30 pq0.l pk0 S31 M30 pq1.h pq1.l zT1.l E2 pk0.h X29 pk1 M31 pk0.l pk1.h P13 X30 q0 pk1.l q1
X31 R14 P14 L2 parts R15 q0.o P15 E3 q2 L3 q1.o O2 O2. kh1 q2.o O3 O3. back q3 q4 F1 q3.o kh2 q4.o q5 F2 kl1 F3 q5.o
q6 q6.o F4 out q7 kl2 pv0 pv0.v q7.o res pv1 pv1.v
""".split()
CHUNKS = [s for s in ORDER if any(t.startswith(s + ".") for t in ORDER)]
A_INDEX = {name: k for k, name in enumerate(CHUNKS)}
WORK_USES = [len(range(s, len(CHUNKS), WORK)) for s in range(WORK)]


def lead(step):
    if step[0] in "SMXRPELOF" or step == "out":
        return 2
    return 0 if step.split(".")[0].rstrip("0123456789") in ("z", "zT", "fk", "kh", "kl", "q", "ldx", "ldk") else 1


HALVES = [[s[:-2] for s in ORDER if s.endswith(".h") and s[:2] != "zT" and lead(s) == n] for n in range(2)]


def last_use(n, slots, count):
    return n - slots if n >= slots else max(m for m in range(count) if m % slots == n % slots) - count


def unit(group):
    return group // 8, group % 8 // 4, group % 4 // 2, group % 2


def window(t, h, b2):
    return PAD * (2 * h + b2) + 127 + P * t - MK * h


def tile_heads(t):
    return [h for h in range(H) if MK * h < P * (t + 1) and MK * (h + 1) > P * t]


def main_phase(nc, ctx, w, x_rows, out_rows, kstat, parts):
    def sb(name, shape, dt=F32):
        return ctx.enter_context(nc.sbuf_tensor(name, shape, dt))

    def ps(name, shape):
        return ctx.enter_context(nc.psum_tensor(name, shape, F32))

    def sem(name):
        return ctx.enter_context(nc.semaphore(name))

    def pair(name, shape):
        return {half: sb(name + half, shape, F16) for half in "hl"}

    xin, xb, zz = w["xin"], sb("xb", [P, PT, DIM]), sb("zz", [P, PT, DIM])
    z, xTf = sb("z", [P, PT, DIM]), sb("xTf", [P, KT, PR])
    krows = sb("krows", [P, H, PM])
    fvp, kT, G, Vp = pair("fvp", [P, PADW]), pair("kT", [P, H, PM]), pair("G", [P, KT, H * PM]), pair("Vp", [P, 2, HT, DIM])
    xT, mT, zzT, oT = pair("xT", [P, KT, PR]), pair("mT", [P, HT, 2 * P]), pair("zzT", [P, KT, PR]), pair("oT", [P, 2, PR])
    khat = sb("khat", [P, H, PM])
    mixed, tmp = sb("mixed", [P, 2, HM]), sb("tmp", [P, HM])
    st4, qst, qft = sb("st4", [P, PT, 2]), sb("qst", [P, PT, H, 6]), sb("qft", [P, 6, PT, H])
    rq, sq, wqr = sb("rq", [P, PT, H]), sb("sq", [P, PT, H]), sb("wqr", [P, PT, H])
    x2S, l2s, l2m = sb("x2S", [P, PT, DIM]), sb("l2s", [P, PT, 6]), sb("l2m", [P, PT, 2])
    l2t = sb("l2t", [P, PT, 2])
    l2v, l2r = sb("l2v", [P, PT]), sb("l2r", [P, PT])
    qk = {a: pair(a, [P, 2, PR]) for a in "qk"}
    v = sb("v", [P, PT, DIM])
    stack = {a: sb(a + "stack", [P, FH // 2, PR], F16) for a in "qk"}
    x2 = sb("x2", [P, PT, DIM])
    prob, vsp = sb("prob", [P, PG * 4, NQ]), sb("vsp", [P, KT, 4, 3 * FD])
    nm, sums, rs = sb("nm", [P, 4 * GROUPS]), sb("sums", [P, 4 * GROUPS]), sb("rs", [P, 4 * GROUPS])
    zb, junk = sb("zb", [P, PT, DIM]), sb("junk", [P, 2, DIM], mybir.dt.bfloat16)
    nrm, nrs, fac = sb("nrm", [P, 2, PT]), sb("nrs", [P, 2, PT]), sb("fac", [P, 5, PT])

    work = [ps(f"work{s}", [P, 512]) for s in range(WORK)]
    sc = [ps(f"score{s}", [P, 512]) for s in range(SC)]
    pvb = [ps(f"attended{s}", [P, 512]) for s in range(2)]

    filled, drained = [sem(f"filled{s}") for s in range(WORK)], [sem(f"drained{s}") for s in range(WORK)]
    init, rk_in, kr_in, x_ready = sem("init"), sem("rk_in"), sem("kr_in"), w["x_ready"]
    z_ready, xb_ready, kT_ready = sem("z_ready"), sem("xb_ready"), sem("kT_ready")
    qsq_ready, rq_ready, wqr_ready, mixed_ready = sem("qsq"), sem("rq_ready"), sem("wqr_ready"), sem("mixed_ready")
    v2_ready, r2_ready, zz_ready = sem("v2_ready"), sem("r2_ready"), sem("zz_ready")
    hi_ready = [sem("hi_first"), sem("hi_ready")]
    parts_stored, stack_in, x2_in = sem("parts_stored"), sem("stack_in"), sem("x2_in")
    sc_ready, max_ready, exp_done = sem("sc_ready"), sem("max_ready"), sem("exp_done")
    vs_ready, pv_done, ot_done = sem("vs_ready"), sem("pv_done"), sem("ot_done")
    nrm_ready, fac_ready = sem("nrm_ready"), sem("fac_ready")
    gelu_ready, ob_ready, stored = sem("gelu_ready"), sem("ob_ready"), sem("stored")
    a_step, b_step, tmp_ready, turns = sem("a_step"), sem("b_step"), sem("tmp_ready"), sem("turns")
    xT_ready, kT_half = sem("xT_ready"), sem("kT_half")
    ot_half, fv_ready, st_ready = sem("ot_half"), sem("fv_ready"), sem("st_ready")

    def bank(name):
        return work[A_INDEX[name] % WORK]

    def used_by(name, turn):
        k = A_INDEX[name]
        return turn * WORK_USES[k % WORK] + k // WORK

    def uses(name, pair):
        return used_by(name, pair + lead(name))

    def latest(names):
        last = {}
        for name in sorted(names, key=A_INDEX.get):
            last[A_INDEX[name] % WORK] = name
        return last.items()

    def wait_filled(eng, pair, *names):
        for s, name in latest(names):
            eng.wait_ge(filled[s], uses(name, pair) + 1)

    def wait_drained(eng, pair, *names):
        for s, name in latest(names):
            eng.wait_ge(drained[s], uses(name, pair) + 1)

    def wait_free(eng, name, pair):
        eng.wait_ge(drained[A_INDEX[name] % WORK], uses(name, pair))

    def fill(ins, name):
        ins.then_inc(filled[A_INDEX[name] % WORK], 1)

    def drain(ins, name):
        ins.then_inc(drained[A_INDEX[name] % WORK], 1)

    def key_rows(ap):
        return ap.rearrange("p h (b m) -> p h b m", m=MK)

    def emptied(e, half):
        kind, c, bk = e[:-1], int(e[-1]), bank(e)
        if kind == "fk":
            lo_h, hi_h = HEAD_PARTS[c]
            rows = fvp[half][:, 0:2 * H * PAD].rearrange("p (n c) -> p n c", c=PAD)
            return (rows[:, 2 * lo_h:2 * hi_h, 127:PAD],
                    bk[:, 0:(hi_h - lo_h) * PM].rearrange("p (n m) -> p n m", m=MK), FV / WS)
        if kind == "G":
            lo_h, hi_h = HEAD_PARTS[c % 3]
            return G[half][:, c // 3, lo_h * PM:hi_h * PM], bk[:, 0:(hi_h - lo_h) * PM], 1.0 / WS
        if kind == "V":
            tiles = HM_TILES[c % 3]
            return (Vp[half][:, c // 3, tiles[0]:tiles[-1] + 1, :],
                    bk[:, 0:len(tiles) * DIM].rearrange("p (t o) -> p t o", o=DIM), 1.0 / WS)
        if kind == "m":
            tiles = HM_TILES[c % 3]
            r = HM_ROWS[tiles[0]]
            return (mT[half][0:r, tiles[0]:tiles[-1] + 1, :],
                    bk[0:r, 0:len(tiles) * 2 * P].rearrange("p (t n) -> p t n", n=2 * P), MS)
        if kind == "zz":
            return zzT[half][:, c, :], bk[:, :], 1.0
        return qk[kind[1]][half][:, c, :], bk[:, :], (1.0 / 16 if kind == "pq" else 1.0) / WS

    def run(eng, a_part, b_part, passed=None):
        def part_of(s, pair):
            (b_part if lead(s) == 2 else a_part)(s, pair)

        def short_turn(t):
            for s in ORDER:
                if 0 <= t - lead(s) < NPAIR:
                    part_of(s, t - lead(s))
                elif passed and s in A_INDEX:
                    passed(s, t)

        short_turn(0)
        short_turn(1)
        with eng.Fori(0, NPAIR - 2) as i:
            for s in ORDER:
                part_of(s, i + 2 - lead(s))
        short_turn(NPAIR)
        short_turn(NPAIR + 1)

    with nc.Block() as block:
        @block.sync
        def _(sp):
            for waited in (stack_in, ob_ready, vs_ready, sc_ready, stored):
                sp.sem_inc(waited, START)
            sp.sem_inc(exp_done, EXP_CREDIT)
            sp.sem_inc(pv_done, PV_CREDIT)
            sp.sem_inc(ot_done, OT_CREDIT)

            def sp_wait(ready, value):
                sp.wait_ge(ready, value)
                sp.sem_inc(turns, 1)

            def sp_wait_drained(pair, *names):
                for s, name in latest(names):
                    sp_wait(drained[s], uses(name, pair) + 1)

            def a_part(step, a):
                if step == "ldx":
                    if isinstance(a, int) and a == 0:
                        return
                    sp_wait(z_ready, a)
                    sp_wait(xb_ready, a)
                    sp.dma_start(xin[:], x_rows[bass.ds(a * PR, PR), :].rearrange("(t p) d -> p t d", p=P)).then_inc(x_ready, 16)
                elif step == "ldk":
                    sp_wait(mixed_ready, a * PT)
                    sp.dma_start(krows[:], kstat[0:H, bass.ds(a * PM, PM)].partition_broadcast(P)).then_inc(rk_in, 16)
                elif step == "ldr":
                    sp_wait_drained(a, "fk0", "fk1", "fk2")
                    sp.dma_start(krows[:], kstat[H:2 * H, bass.ds(a * PM, PM)].partition_broadcast(P)).then_inc(kr_in, 16)
                elif step == "parts":
                    sp_wait_drained(a, "pq0", "pq1", "pk0", "pk1")
                    sp_wait(stack_in, a * 256 + START)
                    for n, t in enumerate((qk["q"]["h"], qk["q"]["l"], qk["k"]["h"], qk["k"]["l"])):
                        sp.dma_start(parts[n].rearrange("(t p) n -> p t n", p=P), t[:]).then_inc(parts_stored, 16)
                elif step == "back":
                    sp_wait(parts_stored, a * 64 + 64)
                    sp_wait(sc_ready, a * 2 * GROUPS + START)
                    for c in range(4):
                        for e in range(2):
                            for name, n in (("k", 2 + c // 2), ("q", c % 2)):
                                src = parts[n].rearrange("(q e d) n -> e d q n", e=2, d=FD)[e]
                                sp.dma_start(stack[name][64 * e + FD * c:64 * e + FD * (c + 1), :, :],
                                             src).then_inc(stack_in, 16)
                elif step == "res":
                    sp_wait_drained(a, "y0", "y1")
                    sp_wait(ob_ready, a + START)
                    sp.dma_start(x2[:], x2S[:]).then_inc(x2_in, 16)

            def b_part(step, b):
                if step == "out":
                    sp_wait(ob_ready, b + 1 + START)
                    sp.dma_start(out_rows[bass.ds(b * PR, PR), :].rearrange("(t p) d -> p t d", p=P),
                                 zb[:]).then_inc(stored, 16)

            run(sp, a_part, b_part)
            sp.wait_ge(stored, 16 * NPAIR + START)

        @block.tensor
        def _(pe):
            ident = w["ident"]

            def a_part(e, a):
                if e not in A_INDEX:
                    return
                kind, c = e[:-1], int(e[-1])
                bk = bank(e)
                wait_free(pe, e, a)
                if kind in ("zT", "zz"):
                    src = z if kind == "zT" else zz
                    pe.wait_ge(z_ready if kind == "zT" else zz_ready, a + 1)
                    for t in range(PT):
                        last = nc.tensor.transpose(bk[:, t * P:(t + 1) * P], src[:, t, c * P:(c + 1) * P], ident[:])
                elif kind == "fk":
                    lo_h, hi_h = HEAD_PARTS[c]
                    for h in range(lo_h, hi_h):
                        for k in range(KT):
                            last = products(nc, bk[:, (h - lo_h) * PM:(h - lo_h + 1) * PM],
                                            w["wT"], (ALL, k, slice(h * DH, (h + 1) * DH)),
                                            w["zcT"], (ALL, k, bass.ds(a * PM, PM)), k == 0, k == KT - 1)
                elif kind == "q":
                    if c == 0:
                        pe.wait_ge(xT_ready, a * KT + KT)
                    t, half = c // 2, c % 2
                    for k in range(KT):
                        last = products(nc, bk[:, :], xT, (ALL, k, slice(t * P, (t + 1) * P)),
                                        w["wT"], (ALL, k, slice(half * 512, (half + 1) * 512)), k == 0, k == KT - 1)
                elif kind == "G":
                    k, (lo_h, hi_h) = c // 3, HEAD_PARTS[c % 3]
                    pe.wait_ge(kT_ready, a * 3 + c % 3 + 1)
                    for h in range(lo_h, hi_h):
                        last = products(nc, bk[:, (h - lo_h) * PM:(h - lo_h + 1) * PM],
                                        w["wN"], (ALL, h, slice(k * P, (k + 1) * P)), kT, (ALL, h))
                elif kind == "V":
                    b2, tiles = c // 3, HM_TILES[c % 3]
                    if c == 0:
                        pe.wait_ge(fv_ready, a * 3 + 3)
                    for n, t in enumerate(tiles):
                        heads = tile_heads(t)
                        for h in heads:
                            last = products(nc, bk[:, n * DIM:(n + 1) * DIM],
                                            fvp, (ALL, slice(window(t, h, b2), window(t, h, b2) + P)),
                                            w["woutT"], (ALL, h), h == heads[0], h == heads[-1])
                elif kind == "d":
                    t, half = c // 2, c % 2
                    rows = {part: G[part][:].rearrange("p k (h b m) -> p k h b m", b=2, m=MK) for part in "hl"}
                    if c == 0:
                        wait_drained(pe, a, *(f"G{g}" for g in range(6)))
                    for k in range(KT):
                        last = products(nc, bk[:, 0:HM // 2], xT, (ALL, k, slice(t * P, (t + 1) * P)),
                                        rows, (ALL, k, slice(4 * half, 4 * half + 4), t // 2), k == 0, k == KT - 1)
                elif kind == "m":
                    b2, tiles = c // 3, HM_TILES[c % 3]
                    pe.wait_ge(mixed_ready, a * PT + 2 * b2 + 2)
                    for n, t in enumerate(tiles):
                        for r in range(2):
                            last = nc.tensor.transpose(bk[0:HM_ROWS[t], (2 * n + r) * P:(2 * n + r + 1) * P],
                                                       mixed[:, r, t * P:t * P + HM_ROWS[t]], ident[:])
                elif kind == "y":
                    wait_drained(pe, a, *(f"{kind}{n}" for kind in "mV" for n in range(3 * c, 3 * c + 3)))
                    for r in range(2):
                        for t in range(HT):
                            last = products(nc, bk[:, r * DIM:(r + 1) * DIM],
                                            mT, (slice(0, HM_ROWS[t]), t, slice(r * P, (r + 1) * P)),
                                            Vp, (slice(0, HM_ROWS[t]), c, t), t == 0, t == HT - 1)
                elif kind in ("pq", "pk"):
                    if e == "pq0":
                        wait_drained(pe, a, "zz0", "zz1")
                    for k in range(KT):
                        last = products(nc, bk[:, :], w["w" + kind[1]], (ALL, k, slice(c * P, (c + 1) * P)), zzT, (ALL, k),
                                        k == 0, k == KT - 1)
                elif kind == "pv":
                    for r in range(2):
                        for k in range(KT):
                            last = products(nc, bk[:, r * DIM:(r + 1) * DIM],
                                            zzT, (ALL, k, slice((2 * c + r) * P, (2 * c + r + 1) * P)),
                                            w["wv"], (ALL, k), k == 0, k == KT - 1)
                fill(last, e)

            def b_part(step, b):
                if step == "out":
                    return
                kind, n = step[0], int(step[1:].rstrip("."))
                if step.endswith("."):
                    return
                if kind == "S":
                    b2, t, e, k = unit(n // 2)
                    if n == 0:
                        pe.wait_ge(stack_in, b * 256 + 256 + START)
                    pe.wait_ge(exp_done, b * 4 * GROUPS + 2 * last_use(n, SC, 2 * GROUPS) + 2 + EXP_CREDIT)
                    for jj in range(2):
                        j = 4 * t + 2 * (n % 2) + jj
                        last = nc.tensor.matmul(sc[n % SC][:, jj * NQ:(jj + 1) * NQ],
                                                stack["k"][64 * e:64 * e + 64, j, b2 * NQ + k * P:b2 * NQ + (k + 1) * P],
                                                stack["q"][64 * e:64 * e + 64, j, b2 * NQ:(b2 + 1) * NQ],
                                                start=True, stop=True)
                    last.then_inc(sc_ready, 1)
                elif kind == "P":
                    b2, t, e, k = unit(n)
                    pe.wait_ge(vs_ready, b * GROUPS + n + 1 + START)
                    if n % 4 == 0:
                        pe.wait_ge(ot_done, b * 4 + n // 4 + 1)
                    lo_c = FD * (1 - e)
                    for j in range(4):
                        last = nc.tensor.matmul(pvb[t][32 * j:32 * j + 32, 0:NQ], vsp[:, k, j, lo_c:lo_c + 2 * FD],
                                                prob[:, (n % PG) * 4 + j, :], start=(n % 4 == 0), stop=(n % 4 == 3))
                    last.then_inc(pv_done, 1)
                elif kind == "O":
                    wait_free(pe, step, b)
                    pe.wait_ge(ot_done, b * 4 + 2 * (n // 2) + 2 + OT_CREDIT)
                    for k in range(2):
                        last = products(nc, bank(step)[:, :], oT, (ALL, k, slice(n * P, (n + 1) * P)), w["wof"], (ALL, k),
                                        k == 0, k == 1)
                    fill(last, step)

            def passed(step, turn):
                pe.wait_ge(drained[A_INDEX[step] % WORK], used_by(step, turn))
                pe.sem_inc(filled[A_INDEX[step] % WORK], 1)
                pe.sem_inc(drained[A_INDEX[step] % WORK], 1)

            run(pe, a_part, b_part, passed)

        @block.scalar
        def _(act):
            act.wait_ge(init, 3)

            def a_part(e, a):
                e, _, part = e.partition(".")
                if e in ("kh0", "kh1", "kh2"):
                    lo_h, hi_h = HEAD_PARTS[int(e[-1])]
                    wait_drained(act, a, "fk" + e[-1])
                    nc.scalar.activation(kT["h"][:, lo_h:hi_h, :], khat[:, lo_h:hi_h, :], ACT.Copy).then_inc(kT_half, 1)
                elif e[:-1] == "zT" and part in ("h", "f"):
                    c, bk = int(e[-1]), bank(e)
                    if part == "h":
                        wait_filled(act, a, e)
                    ins = nc.scalar.activation((xT["h"] if part == "h" else xTf)[:, c, :], bk[:, :], ACT.Identity,
                                               scale=w["gcol"][:, c:c + 1], bias=w["bcol"][:, c:c + 1])
                    if part == "f":
                        drain(ins, e)
                elif part == "h":
                    if e == "m3":
                        wait_filled(act, a, "m3", "y0")
                    else:
                        wait_filled(act, a, e)
                    if e[:-1] in ("pq", "pk"):
                        act.wait_ge(parts_stored, a * 64)
                    dst, src, scale = emptied(e, "h")
                    nc.scalar.activation(dst, src, ACT.Copy, scale=scale).then_inc(hi_ready[lead(e)], 1)
                elif e[:-1] == "pv" and part == "v":
                    c = int(e[-1])
                    wait_filled(act, a, e)
                    act.wait_ge(vs_ready, a * GROUPS + START)
                    drain(nc.scalar.activation(v[:, 2 * c:2 * c + 2, :], bank(e)[:, :].rearrange("p (t o) -> p t o", o=DIM),
                                               ACT.Copy, scale=VS / WS), e)

            def b_part(step, b):
                if step == "out":
                    return
                kind, n = step[0], int(step[1:].rstrip("."))
                if kind == "X":
                    g = n // 2
                    act.wait_ge(max_ready, b * 2 * GROUPS + n + 1)
                    if n % 2 == 0:
                        act.wait_ge(pv_done, b * GROUPS + last_use(g, PG, GROUPS) + 1 + PV_CREDIT)
                    for jj in range(2):
                        u = 2 * n + jj
                        nc.scalar.activation(prob[:, (g % PG) * 4 + u % 4, :], sc[n % SC][:, jj * NQ:(jj + 1) * NQ], ACT.Exp,
                                             bias=nm[:, u:u + 1], accum_out=sums[:, u:u + 1]).then_inc(exp_done, 1)
                elif kind == "E":
                    act.wait_ge(pv_done, b * GROUPS + 4 * n + 4 + PV_CREDIT)
                    wait_filled(act, b - 1, f"O{n // 2 * 2 + 1}")
                    nc.scalar.activation(oT["h"][:, n % 2, (n // 2) * NQ:(n // 2 + 1) * NQ], pvb[n % 2][:, 0:NQ],
                                         ACT.Copy).then_inc(ot_half, 1)
                elif kind == "O" and step.endswith("."):
                    bk = bank(step[:-1])
                    wait_filled(act, b, step[:-1])
                    if n == 0:
                        act.wait_ge(stored, b * 16 + START)
                    else:
                        wait_drained(act, b, f"O{n - 1}")
                    for j in range(2):
                        nc.scalar.activation(junk[:, j, :], bk[:, j * DIM:(j + 1) * DIM], ACT.Square,
                                             scale=1.0 / (VS * WS), accum_out=nrm[:, j, n:n + 1])
                    drain(nc.scalar.activation(zb[:, n, :], bk[:, DIM:2 * DIM], ACT.Copy, scale=1.0 / (VS * WS)), step[:-1])
                elif step == "F3":
                    act.wait_ge(fac_ready, b + 1)
                    for t in range(PT):
                        last = nc.scalar.activation(zb[:, t, :], zb[:, t, :], ACT.Gelu, scale=fac[:, 4, t:t + 1])
                    last.then_inc(gelu_ready, 1)

            run(act, a_part, b_part)

        @block.gpsimd
        def _(pool):
            for half in "hl":
                nc.gpsimd.memset(fvp[half][:], 0.0).then_inc(init, 1)
            nc.gpsimd.memset(vsp[:], 0.0).then_inc(init, 1)

            def a_part(e, a):
                if e == "xb":
                    pool.wait_ge(x_ready, a * 16 + 16)
                    pool.wait_ge(v2_ready, a)
                    nc.gpsimd.tensor_tensor(xb[:], xin[:], bc(w["tb"][:].unsqueeze(1), [P, PT, DIM]),
                                            ALU.add).then_inc(xb_ready, 1)
                elif e == "qpow":
                    pool.wait_ge(qsq_ready, a + 1)
                    nc.gpsimd.tensor_tensor(rq[:], qft[:, 0, :, :], w["mhalf"][:].rearrange("p (t h) -> p t h", h=H),
                                            ALU.pow).then_inc(rq_ready, 1)
                elif e[:-1] == "kl":
                    n = int(e[-1])
                    lo_h, hi_h = HEAD_PARTS[n]
                    pool.wait_ge(kT_half, a * 3 + n + 1)
                    nc.gpsimd.tensor_tensor(kT["l"][:, lo_h:hi_h, :], khat[:, lo_h:hi_h, :], kT["h"][:, lo_h:hi_h, :],
                                            ALU.subtract).then_inc(kT_ready, 1)
                elif e[0] == "x":
                    t = int(e[1])
                    pool.wait_ge(kr_in, a * 16 + 16)
                    pool.wait_ge(wqr_ready, a + 1)
                    pool.wait_ge(mixed_ready, a * PT + t)
                    nc.gpsimd.tensor_tensor(tmp[:].rearrange("p (h m) -> p h m", m=MK),
                                            krows[:, :, (t // 2) * MK:(t // 2 + 1) * MK],
                                            bc(wqr[:, t, :].unsqueeze(2), [P, H, MK]), ALU.mult).then_inc(tmp_ready, 1)
                    pool.wait_ge(tmp_ready, a * PT + t + 1)
                    wait_drained(pool, a, f"d{2 * t}", f"d{2 * t + 1}")
                    nc.gpsimd.tensor_tensor(mixed[:, t % 2, :], mixed[:, t % 2, :], tmp[:], ALU.add).then_inc(mixed_ready, 1)
                elif e == "lpow":
                    pool.wait_ge(v2_ready, a + 1)
                    nc.gpsimd.tensor_tensor(l2r[:], l2v[:], w["mhalf"][:, 0:PT], ALU.pow).then_inc(r2_ready, 1)

            def b_part(step, b):
                if step == "F1":
                    wait_drained(pool, b, *(f"O{n}" for n in range(PT)))
                    nc.gpsimd.tensor_tensor(nrs[:].rearrange("p j t -> p (j t)"), nrm[:].rearrange("p j t -> p (j t)"),
                                            w["phalf"][:, 0:2 * PT], ALU.pow).then_inc(nrm_ready, 1)

            run(pool, a_part, b_part)

        @block.vector
        def _(dve):

            def a_part(e, a):
                def link(k, ins):
                    ins.then_inc(a_step, 1)
                    dve.wait_ge(a_step, a * A_STEPS + k)

                full, e = e, e.split(".")[0]
                kind, c = e[:-1], e[-1]
                part = full[len(e) + 1:]
                if e in A_INDEX and part in ("", "h", "f"):
                    return
                if e == "z":
                    dve.wait_ge(x_ready, a * 16 + 16)
                    nc.vector.tensor_copy(st4[:], w["stats"][:, bass.ds(a * PT, PT), :]).then_inc(st_ready, 1)
                    dve.wait_ge(st_ready, a + 1)
                    for t in range(PT):
                        last = nc.vector.tensor_scalar(z[:, t, :], xin[:, t, :], st4[:, t, 0:1], st4[:, t, 1:2],
                                                       ALU.subtract, ALU.mult)
                    last.then_inc(z_ready, 1)
                elif part == "l" and kind != "zT":
                    done = HALVES[lead(e)]
                    dve.wait_ge(hi_ready[lead(e)], a * len(done) + done.index(e) + 1)
                    dst, src, scale = emptied(e, "l")
                    ins = nc.vector.scalar_tensor_tensor(dst, src, scale, emptied(e, "h")[0], ALU.mult, ALU.subtract)
                    if kind == "fk":
                        ins.then_inc(fv_ready, 1)
                    else:
                        drain(ins, e)
                elif part == "k":
                    lo_h, hi_h = HEAD_PARTS[int(c)]
                    dve.wait_ge(rk_in, a * 16 + 16)
                    ins = nc.vector.scalar_tensor_tensor(
                        khat[:, lo_h:hi_h, :], bank(e)[:, 0:(hi_h - lo_h) * PM].rearrange("p (h n) -> p h n", n=PM), KS,
                        krows[:, lo_h:hi_h, :], ALU.mult, ALU.mult)
                    drain(ins, e)
                elif kind == "zT" and part == "l":
                    wait_drained(dve, a, e)
                    nc.vector.tensor_tensor(xT["l"][:, int(c), :], xTf[:, int(c), :], xT["h"][:, int(c), :],
                                            ALU.subtract).then_inc(xT_ready, 1)
                elif kind == "q":
                    t, half = int(c) // 2, int(c) % 2
                    wait_filled(dve, a, e)
                    for h in range(4):
                        last = nc.vector.bn_stats(qst[:, t, 4 * half + h, :], bank(e)[:, h * DH:(h + 1) * DH])
                    drain(last, e)
                elif e == "qs1":
                    wait_drained(dve, a, *(f"q{n}" for n in range(2 * PT)))
                    dve.wait_ge(mixed_ready, a * PT)
                    moments(nc, link, 1, qst[:], qft, WS)
                    dve.sem_inc(qsq_ready, 1)
                    ratio_num(nc, qft)
                    link(6, ratio_den(nc, qft))
                    link(7, nc.vector.reciprocal(qft[:, 3, :, :], qft[:, 3, :, :]))
                    link(8, nc.vector.tensor_tensor(qft[:, 2, :, :], qft[:, 2, :, :], qft[:, 3, :, :], ALU.mult))
                    nc.vector.tensor_tensor(wqr[:], qft[:, 2, :, :], bc(w["wwv"][:].unsqueeze(1), [P, PT, H]),
                                            ALU.mult).then_inc(wqr_ready, 1)
                elif e == "qs2":
                    dve.wait_ge(rq_ready, a + 1)
                    link(9, nc.vector.tensor_tensor(sq[:], rq[:], bc(w["cvec"][:].unsqueeze(1), [P, PT, H]), ALU.mult))
                elif kind == "d":
                    t, half = int(c) // 2, int(c) % 2
                    if t >= 2:
                        wait_filled(dve, a, e, "m0", "m1", "m2")
                    else:
                        wait_filled(dve, a, e)
                    drain(nc.vector.tensor_tensor(
                        mixed[:, t % 2, half * (HM // 2):(half + 1) * (HM // 2)].rearrange("p (h m) -> p h m", m=MK),
                        bank(e)[:, 0:HM // 2].rearrange("p (h m) -> p h m", m=MK),
                        bc(sq[:, t, 4 * half:4 * half + 4].unsqueeze(2), [P, 4, MK]), ALU.mult), e)
                elif kind == "y":
                    c = int(c)
                    wait_filled(dve, a, e)
                    dve.wait_ge(xb_ready, a + 1)
                    dve.wait_ge(x2_in, a * 16)
                    drain(nc.vector.scalar_tensor_tensor(
                        x2S[:, 2 * c:2 * c + 2, :], bank(e)[:, :].rearrange("p (t o) -> p t o", o=DIM), 1.0 / (FV * MS),
                        xb[:, 2 * c:2 * c + 2, :], ALU.mult, ALU.add), e)
                elif e == "ln1":
                    wait_drained(dve, a, "y0", "y1")
                    for t in range(PT):
                        last = nc.vector.bn_stats(l2s[:, t, :], x2S[:, t, :])
                    link(10, last)
                    row_moments(nc, link, 11, l2s, l2m, l2t)
                    nc.vector.tensor_scalar(l2v[:], l2t[:, :, 1], 1.0 / DIM, EPS, ALU.mult, ALU.add).then_inc(v2_ready, 1)
                elif e == "ln2":
                    dve.wait_ge(r2_ready, a + 1)
                    for t in range(PT):
                        last = nc.vector.tensor_scalar(zz[:, t, :], x2S[:, t, :], l2m[:, t, 0:1], l2r[:, t:t + 1],
                                                       ALU.subtract, ALU.mult)
                    last.then_inc(zz_ready, 1)

            def b_part(step, b):
                if step == "out":
                    return
                kind, n = step[0], int(step[1:].rstrip("."))

                def link(k, ins):
                    ins.then_inc(b_step, 1)
                    dve.wait_ge(b_step, b * B_STEPS + k)

                if kind == "L":
                    dve.wait_ge(ot_half, b * 4 + n + 1)
                    at = (ALL, n % 2, slice((n // 2) * NQ, (n // 2 + 1) * NQ))
                    nc.vector.tensor_tensor(oT["l"][at], pvb[n % 2][:, 0:NQ], oT["h"][at], ALU.subtract).then_inc(ot_done, 1)
                elif kind == "M":
                    dve.wait_ge(sc_ready, b * 2 * GROUPS + n + 1 + START)
                    nc.vector.tensor_reduce(nm[:, 2 * n:2 * n + 2], sc[n % SC][:, :].rearrange("p (u q) -> p u q", q=NQ),
                                            AX.X, ALU.max, negate=True).then_inc(max_ready, 1)
                elif kind == "R":
                    b2, t, e, k = unit(n)
                    if n == 0:
                        dve.wait_ge(init, 3)
                    dve.wait_ge(exp_done, b * 4 * GROUPS + 4 * n + 4 + EXP_CREDIT)
                    link(n + 1, nc.vector.reciprocal(rs[:, 4 * n:4 * n + 4], sums[:, 4 * n:4 * n + 4]))
                    if n == 0:
                        wait_drained(dve, b, "pv0", "pv1")
                    dve.wait_ge(pv_done, b * GROUPS + n - 1 + PV_CREDIT)
                    src = v[:, 2 * b2 + k, t * P:(t + 1) * P].rearrange("p (j e d) -> p e j d", e=2, d=FD)[:, e]
                    nc.vector.tensor_tensor(vsp[:, k, :, FD:2 * FD], src,
                                            bc(rs[:, 4 * n:4 * n + 4].unsqueeze(2), [P, 4, FD]), ALU.mult).then_inc(vs_ready, 1)
                elif step == "F2":
                    dve.wait_ge(nrm_ready, b + 1)
                    base = GROUPS
                    link(base + 1, nc.vector.tensor_scalar(fac[:, 0, :], nrs[:, 0, :], L2_EPS, None, ALU.max))
                    link(base + 2, nc.vector.reciprocal(fac[:, 1, :], fac[:, 0, :]))
                    link(base + 3, nc.vector.tensor_tensor(fac[:, 2, :], nrs[:, 1, :], fac[:, 1, :], ALU.mult))
                    link(base + 4, nc.vector.tensor_scalar(fac[:, 2, :], fac[:, 2, :], L2_EPS, None, ALU.max))
                    link(base + 5, nc.vector.reciprocal(fac[:, 3, :], fac[:, 2, :]))
                    nc.vector.tensor_tensor(fac[:, 4, :], fac[:, 1, :], fac[:, 3, :], ALU.mult).then_inc(fac_ready, 1)
                elif step == "F4":
                    dve.wait_ge(gelu_ready, b + 1)
                    dve.wait_ge(x2_in, b * 16 + 16)
                    nc.vector.scalar_tensor_tensor(zb[:].rearrange("p t o -> p (t o)"), zb[:].rearrange("p t o -> p (t o)"),
                                                   w["tg"][:, 1:2], x2[:].rearrange("p t o -> p (t o)"),
                                                   ALU.mult, ALU.add).then_inc(ob_ready, 1)

            run(dve, a_part, b_part)


def kernel(**inputs):
    import numpy as np
    import concourse.bacc as bacc
    from concourse.bass_utils import run_bass_kernel_spmd

    def turned(name):
        return np.ascontiguousarray(np.asarray(inputs[name]).T)

    def given(name):
        return np.ascontiguousarray(np.asarray(inputs[name]))

    nc = bacc.Bacc("TRN2", target_bir_lowering=False, num_devices=1)
    arrays = {
        "x": given("x"), "ctx_in": given("ctx_1024"), "g_x": given("g_xattn"), "g_f": given("g_ffn"),
        "ln_g": given("L0_xattn_ln_g"), "ln_b": given("L0_xattn_ln_b"),
        "w_in": given("L0_xattn_w_in"), "w_inT": turned("L0_xattn_w_in"),
        "w1T": turned("L0_xattn_wp_w1"), "b1": given("L0_xattn_wp_b1"),
        "wln_g": given("L0_xattn_wp_ln_g"), "wln_b": given("L0_xattn_wp_ln_b"),
        "w2T": turned("L0_xattn_wp_w2"), "b2": given("L0_xattn_wp_b2"),
        "w_outT": turned("L0_xattn_w_out"), "b_out": given("L0_xattn_b_out"),
        "wq": given("L0_ffn_Wq"), "wk": given("L0_ffn_Wk"), "wv": given("L0_ffn_Wv"),
        "wo": given("L0_ffn_Wo"), "woT": turned("L0_ffn_Wo"), "wff": given("L0_ffn_Wff"),
    }
    aps = {name: nc.dram_tensor(f"in_{name}", a.shape, mybir.dt.from_np(a.dtype), kind="ExternalInput").ap()
           for name, a in arrays.items()}
    out = nc.dram_tensor("out_0", (NB, NQ, DIM), F32, kind="ExternalOutput").ap()
    build(nc, out=out, **aps)
    r = run_bass_kernel_spmd(nc, [{f"in_{name}": a for name, a in arrays.items()}], core_ids=[0])
    return r.results[0]["out_0"]
```
